# Optimizing a Trainium2 kernel written in Bass

```python
import numpy as np
import jax
import jax.numpy as jnp

def _softmax(x, axis=-1):
    return jax.nn.softmax(x, axis=axis)

def _gelu(x):
    return jax.nn.gelu(x, approximate=True)

def _silu(x):
    return jax.nn.silu(x)

def _sigmoid(x):
    return jax.nn.sigmoid(x)

def _layernorm(x, axis=-1, eps=1e-05):
    m = jnp.mean(x, axis=axis, keepdims=True)
    v = jnp.var(x, axis=axis, keepdims=True)
    return (x - m) / jnp.sqrt(v + eps)

def _scatter_add(tgt, idx, src, axis=0):
    return tgt.at[idx].add(src)

def _segment_sum(src, seg, n):
    return jax.ops.segment_sum(src, seg, n)
kernel_name = 'mk_seq_postln_d2_jaxref_r4_bc5e17'

def setup_inputs(seed: int=0):
    np.random.seed(seed)
    _w = jnp.asarray

    def _L0_attn_setup():
        import jax, jax.numpy as jnp
        import numpy as np
        BLOCK_H = 32
        BLOCK_W = 32
        N_FEAT = 1024
        K_FEAT = 1024
        key = jax.random.key(seed)
        k1, k2, k3 = jax.random.split(key, 3)
        data = jax.random.normal(k1, (4, 256, K_FEAT), dtype=jnp.float32)
        weight = jax.random.normal(k2, (N_FEAT, K_FEAT), dtype=jnp.float32) * 0.02
        nb, kb = (N_FEAT // BLOCK_H, K_FEAT // BLOCK_W)
        block_pattern = jax.random.randint(k3, (nb, kb), 0, 2, dtype=jnp.int32)
        mask = jnp.repeat(jnp.repeat(block_pattern, BLOCK_H, axis=0), BLOCK_W, axis=1)
        return {'data': data, 'weight': weight, 'mask': mask}
    _L0_attn_in = _L0_attn_setup()

    def _L0_ffn_setup():
        import jax, jax.numpy as jnp
        import numpy as np
        NF4 = jnp.array([-1.0, -0.6961928009986877, -0.5250730514526367, -0.39491748809814453, -0.28444138169288635, -0.18477343022823334, -0.09105003625154495, 0.0, 0.07958029955625534, 0.16093020141124725, 0.24611230194568634, 0.33791524171829224, 0.44070982933044434, 0.5626170039176941, 0.7229568362236023, 1.0], dtype=jnp.float32)
        BLOCK = 64

        def dequant_nf4(codes, scales):
            out_dim, in_dim = codes.shape
            vals = NF4[codes].reshape(out_dim, in_dim // BLOCK, BLOCK)
            return (vals * scales[:, :, None]).reshape(out_dim, in_dim)
        key = jax.random.key(seed)
        ks = jax.random.split(key, 7)
        H, I = (1024, 2752)
        B, S = (4, 512)
        return {'x': jax.random.normal(ks[0], (B, S, H), dtype=jnp.float32), 'gate_codes': jax.random.randint(ks[1], (I, H), 0, 16, dtype=jnp.int32), 'gate_scales': jax.random.uniform(ks[2], (I, H // BLOCK), dtype=jnp.float32) * 0.02, 'up_codes': jax.random.randint(ks[3], (I, H), 0, 16, dtype=jnp.int32), 'up_scales': jax.random.uniform(ks[4], (I, H // BLOCK), dtype=jnp.float32) * 0.02, 'down_codes': jax.random.randint(ks[5], (H, I), 0, 16, dtype=jnp.int32), 'down_scales': jax.random.uniform(ks[6], (H, I // BLOCK), dtype=jnp.float32) * 0.02}
    _L0_ffn_in = _L0_ffn_setup()

    def _L1_attn_setup():
        import jax, jax.numpy as jnp
        import numpy as np
        B, S, D = (2, 512, 1024)
        H = 32
        HD = D // H
        THETA = 10000.0

        def _rope_cos_sin(seq_len, head_dim, theta=THETA):
            inv = 1.0 / theta ** (np.arange(0, head_dim, 2)[:head_dim // 2].astype(np.float32) / head_dim)
            t = np.arange(seq_len)
            f = np.outer(t, inv).astype(np.float32)
            return (jnp.asarray(np.cos(f)), jnp.asarray(np.sin(f)))

        def _apply_rotary(x, cos, sin):
            xr = x.astype(jnp.float32).reshape(*x.shape[:-1], HD // 2, 2)
            x0, x1 = (xr[..., 0], xr[..., 1])
            c = cos[None, :, None, :]
            s = sin[None, :, None, :]
            o0 = x0 * c - x1 * s
            o1 = x0 * s + x1 * c
            return jnp.stack((o0, o1), axis=-1).reshape(*x.shape[:-1], HD)
        key = jax.random.key(seed)
        ks = jax.random.split(key, 5)
        std = 0.02
        return {'x': jax.random.normal(ks[0], (B, S, D), dtype=jnp.float32), 'wq': jax.random.normal(ks[1], (D, D), dtype=jnp.float32) * std, 'wk': jax.random.normal(ks[2], (D, D), dtype=jnp.float32) * std, 'wv': jax.random.normal(ks[3], (D, D), dtype=jnp.float32) * std, 'wo': jax.random.normal(ks[4], (D, D), dtype=jnp.float32) * std}
    _L1_attn_in = _L1_attn_setup()

    def _L1_ffn_setup():
        import jax, jax.numpy as jnp
        import numpy as np
        import math
        E, DK, R = (8, 32, 16)
        SCALING = 16.0 / 16.0
        key = jax.random.key(seed)
        ks = jax.random.split(key, 7)
        Bt, S, Din, Dout = (4, 512, 1024, 1024)
        x = jax.random.normal(ks[0], (Bt, S, Din), jnp.float32)
        W = jax.random.normal(ks[1], (Dout, Din), jnp.float32) * 0.02
        b = jnp.zeros((Dout,), jnp.float32)
        Wq = jax.random.normal(ks[2], (E * DK, Din), jnp.float32) * 0.02
        Wk = jax.random.normal(ks[3], (E * DK, Din), jnp.float32) * 0.02
        A = jax.random.normal(ks[4], (E, R, Din), jnp.float32) * 0.02
        Bm = jax.random.normal(ks[5], (E, Dout, R), jnp.float32) * 0.02
        return {'x': x, 'W': W, 'b': b, 'Wq': Wq, 'Wk': Wk, 'A': A, 'Bm': Bm}
    _L1_ffn_in = _L1_ffn_setup()
    _d = {'L0_attn_data': _L0_attn_in['data'], 'L0_attn_weight': _L0_attn_in['weight'], 'L0_attn_mask': _L0_attn_in['mask'], 'L0_ffn_gate_codes': _L0_ffn_in['gate_codes'], 'L0_ffn_gate_scales': _L0_ffn_in['gate_scales'], 'L0_ffn_up_codes': _L0_ffn_in['up_codes'], 'L0_ffn_up_scales': _L0_ffn_in['up_scales'], 'L0_ffn_down_codes': _L0_ffn_in['down_codes'], 'L0_ffn_down_scales': _L0_ffn_in['down_scales'], 'L1_attn_wq': _L1_attn_in['wq'], 'L1_attn_wk': _L1_attn_in['wk'], 'L1_attn_wv': _L1_attn_in['wv'], 'L1_attn_wo': _L1_attn_in['wo'], 'L1_ffn_W': _L1_ffn_in['W'], 'L1_ffn_b': _L1_ffn_in['b'], 'L1_ffn_Wq': _L1_ffn_in['Wq'], 'L1_ffn_Wk': _L1_ffn_in['Wk'], 'L1_ffn_A': _L1_ffn_in['A'], 'L1_ffn_Bm': _L1_ffn_in['Bm']}
    _x0 = _d['L0_attn_data']
    _d['L0_attn_data'] = jax.random.normal(jax.random.fold_in(jax.random.key(seed), 1), (4, 512, 1024), dtype=_x0.dtype)
    del _x0
    return _d

def reference(L0_attn_data, L0_attn_weight, L0_attn_mask, L0_ffn_gate_codes, L0_ffn_gate_scales, L0_ffn_up_codes, L0_ffn_up_scales, L0_ffn_down_codes, L0_ffn_down_scales, L1_attn_wq, L1_attn_wk, L1_attn_wv, L1_attn_wo, L1_ffn_W, L1_ffn_b, L1_ffn_Wq, L1_ffn_Wk, L1_ffn_A, L1_ffn_Bm):

    def _L0_attn_ref(data, weight, mask):
        import jax, jax.numpy as jnp
        import numpy as np
        BLOCK_H = 32
        BLOCK_W = 32
        N_FEAT = 1024
        K_FEAT = 1024
        N, K = weight.shape
        nb, kb = (N // BLOCK_H, K // BLOCK_W)
        block_mask = mask.reshape(nb, BLOCK_H, kb, BLOCK_W).astype(jnp.float32).sum(axis=(1, 3)) > 0
        elem_mask = jnp.repeat(jnp.repeat(block_mask, BLOCK_H, axis=0), BLOCK_W, axis=1)
        w_masked = weight * elem_mask.astype(weight.dtype)
        out = jnp.einsum('bsk,nk->bsn', data, w_masked)
        return out

    def _L0_ffn_ref(x, gate_codes, gate_scales, up_codes, up_scales, down_codes, down_scales):
        import jax, jax.numpy as jnp
        import numpy as np
        NF4 = jnp.array([-1.0, -0.6961928009986877, -0.5250730514526367, -0.39491748809814453, -0.28444138169288635, -0.18477343022823334, -0.09105003625154495, 0.0, 0.07958029955625534, 0.16093020141124725, 0.24611230194568634, 0.33791524171829224, 0.44070982933044434, 0.5626170039176941, 0.7229568362236023, 1.0], dtype=jnp.float32)
        BLOCK = 64

        def dequant_nf4(codes, scales):
            out_dim, in_dim = codes.shape
            vals = NF4[codes].reshape(out_dim, in_dim // BLOCK, BLOCK)
            return (vals * scales[:, :, None]).reshape(out_dim, in_dim)
        Wg = dequant_nf4(gate_codes, gate_scales)
        Wu = dequant_nf4(up_codes, up_scales)
        Wd = dequant_nf4(down_codes, down_scales)
        gate = jnp.einsum('bsh,ih->bsi', x, Wg)
        up = jnp.einsum('bsh,ih->bsi', x, Wu)
        inter = jax.nn.silu(gate) * up
        return jnp.einsum('bsi,hi->bsh', inter, Wd)

    def _L1_attn_ref(x, wq, wk, wv, wo):
        import jax, jax.numpy as jnp
        import numpy as np
        B, S, D = (2, 512, 1024)
        H = 32
        HD = D // H
        THETA = 10000.0

        def _rope_cos_sin(seq_len, head_dim, theta=THETA):
            inv = 1.0 / theta ** (np.arange(0, head_dim, 2)[:head_dim // 2].astype(np.float32) / head_dim)
            t = np.arange(seq_len)
            f = np.outer(t, inv).astype(np.float32)
            return (jnp.asarray(np.cos(f)), jnp.asarray(np.sin(f)))

        def _apply_rotary(x, cos, sin):
            xr = x.astype(jnp.float32).reshape(*x.shape[:-1], HD // 2, 2)
            x0, x1 = (xr[..., 0], xr[..., 1])
            c = cos[None, :, None, :]
            s = sin[None, :, None, :]
            o0 = x0 * c - x1 * s
            o1 = x0 * s + x1 * c
            return jnp.stack((o0, o1), axis=-1).reshape(*x.shape[:-1], HD)
        b, s, d = x.shape
        q = (x @ wq).reshape(b, s, H, HD)
        k = (x @ wk).reshape(b, s, H, HD)
        v = (x @ wv).reshape(b, s, H, HD)
        cos, sin = _rope_cos_sin(s, HD)
        q = _apply_rotary(q, cos, sin)
        k = _apply_rotary(k, cos, sin)
        scale = 1.0 / jnp.sqrt(jnp.float32(HD))
        scores = jnp.einsum('bqhd,bkhd->bhqk', q, k) * scale
        causal = jnp.tril(jnp.ones((s, s), dtype=bool))
        scores = jnp.where(causal[None, None], scores, jnp.finfo(scores.dtype).min)
        probs = jax.nn.softmax(scores, axis=-1)
        out = jnp.einsum('bhqk,bkhd->bqhd', probs, v).reshape(b, s, d)
        return out @ wo

    def _L1_ffn_ref(x, W, b, Wq, Wk, A, Bm):
        import jax, jax.numpy as jnp
        import numpy as np
        import math
        E, DK, R = (8, 32, 16)
        SCALING = 16.0 / 16.0
        Bt, S, Din = x.shape
        result = jnp.einsum('bsi,oi->bso', x, W) + b
        q = jnp.einsum('bsi,ni->bsn', x, Wq).reshape(Bt, S, E, DK)
        k = jnp.einsum('bsi,ni->bsn', x, Wk).reshape(Bt, S, E, DK)
        scores = jnp.einsum('bsed,bsed->bse', q, k) / math.sqrt(DK)
        w = jax.nn.softmax(scores, axis=-1)
        h = jnp.einsum('bsi,eri->bser', x, A)
        combined = jnp.einsum('bse,bser,eor->bso', w, h, Bm) * SCALING
        return result + combined
    x = L0_attn_data
    x = _layernorm(x + _L0_attn_ref(x, L0_attn_weight, L0_attn_mask), axis=-1)
    x = _layernorm(x + _L0_ffn_ref(x, L0_ffn_gate_codes, L0_ffn_gate_scales, L0_ffn_up_codes, L0_ffn_up_scales, L0_ffn_down_codes, L0_ffn_down_scales), axis=-1)
    x = _layernorm(x + _L1_attn_ref(x, L1_attn_wq, L1_attn_wk, L1_attn_wv, L1_attn_wo), axis=-1)
    x = _layernorm(x + _L1_ffn_ref(x, L1_ffn_W, L1_ffn_b, L1_ffn_Wq, L1_ffn_Wk, L1_ffn_A, L1_ffn_Bm), axis=-1)
    return x

_drawn_inputs = setup_inputs


def setup_inputs(seed=0):
    import zlib

    import numpy as np

    out = dict(_drawn_inputs(seed))
    spreads = {'L1_ffn_b': (0.0, 0.1)}
    factors = {'L0_ffn_gate_scales': 8.0,
     'L0_ffn_up_scales': 8.0,
     'L0_ffn_down_scales': 8.0,
     'L1_attn_wq': 3.696,
     'L1_attn_wk': 3.571,
     'L1_ffn_Wq': 8.0,
     'L1_ffn_Wk': 8.0,
     'L1_ffn_A': 4.134,
     'L1_ffn_Bm': 4.132}
    for name, (base, spread) in spreads.items():
        noise = np.random.default_rng([zlib.crc32(name.encode()), seed]).standard_normal(out[name].shape)
        drawn = base * np.exp(spread * noise) if base else spread * noise
        out[name] = jnp.asarray(drawn.astype(out[name].dtype))
    for name, factor in factors.items():
        out[name] = (out[name] * factor).astype(out[name].dtype)
    return out
```

```python
import numpy as np
import concourse.bass as bass
from concourse import mybir
from contextlib import ExitStack

F32 = mybir.dt.float32
F32R = mybir.dt.float32r
I32 = mybir.dt.int32
BF16 = mybir.dt.bfloat16
ALU = mybir.AluOpType
ACT = mybir.ActivationFunctionType
AX = mybir.AxisListType

P = 128
T, D = 2048, 1024
BATCH, SEQ = 4, 512
TILES = T // P
KT = D // P
BANK = 512
BLK = 32
I_FFN = 2752
CH = -(-I_FFN // P)
NF4_BLOCK = 64
HEADS, HD = 32, 32
GROUPS = 8
QK_GROUPS = 4
EXPERTS, DK, RANK = 8, 32, 16
EPS = 1e-5
SLOTS = 2
MASKED = -1e30

HI, LO = 0, 1
PASSES = ((LO, HI), (HI, LO), (HI, HI))


def one(ap):
    return ap.rearrange("a p n -> p (a n)")


class LayerNorm:

    STEPS = 15

    def __init__(self, nc, ctx, tag, sum_ready, base=SLOTS, slots=2, in_place=False):
        sb = lambda name, shape, dt=F32: ctx.enter_context(nc.sbuf_tensor(f"{tag}_{name}", shape, dt))
        sem = lambda name: ctx.enter_context(nc.semaphore(f"{tag}_{name}"))
        self.nc = nc
        self.x = None if in_place else sb("x", [P, slots, D])
        self.stats = sb("stats", [P, slots, 2, 6])
        self.mv = sb("mv", [P, slots, 2])
        self.small = sb("small", [P, slots, 8])
        self.sum_ready, self.base = sum_ready, base
        self.steps = sem("steps")
        self.stats_seen = sem("stats_seen")
        self.x_ready = sem("x_ready")

    def vector(self, dve, n, s, r):
        v, sm, mv, steps, at = self.nc.vector, self.small[:, s, :], self.mv[:, s, :], self.steps, n * self.STEPS
        dve.wait_ge(self.sum_ready, n + self.base + 1)
        v.bn_stats(self.stats[:, s, 0, :], r[:, 0:BANK])
        v.bn_stats(self.stats[:, s, 1, :], r[:, BANK:D]).then_inc(steps, 1)
        dve.wait_ge(steps, at + 1)
        dve.sem_inc(self.stats_seen, 1)
        v.bn_aggr(mv, self.stats[:, s, :, :].rearrange("p a b -> p (a b)")).then_inc(steps, 1)
        dve.wait_ge(steps, at + 2)
        ve, half, y, t = sm[:, 0:1], sm[:, 1:2], sm[:, 2:3], sm[:, 3:4]
        v.tensor_scalar(ve, mv[:, 1:2], EPS, None, ALU.add).then_inc(steps, 1)
        dve.wait_ge(steps, at + 3)
        v.tensor_scalar(half.bitcast(I32), ve.bitcast(I32), 1, None, ALU.logical_shift_right).then_inc(steps, 1)
        dve.wait_ge(steps, at + 4)
        v.tensor_scalar(y.bitcast(I32), half.bitcast(I32), -1.0, float(0x5F3759DF), ALU.mult, ALU.add).then_inc(steps, 1)
        for k in range(3):
            done = at + 3 * k + 5
            dve.wait_ge(steps, done)
            v.scalar_tensor_tensor(t, ve, -0.5, y, ALU.mult, ALU.mult).then_inc(steps, 1)
            dve.wait_ge(steps, done + 1)
            v.tensor_tensor(t, t, y, ALU.mult).then_inc(steps, 1)
            dve.wait_ge(steps, done + 2)
            v.scalar_tensor_tensor(y, t, 1.5, y, ALU.add, ALU.mult).then_inc(steps, 1)
        dve.wait_ge(steps, at + 14)
        v.scalar_tensor_tensor(sm[:, 4:5], mv[:, 0:1], -1.0, y, ALU.mult, ALU.mult).then_inc(steps, 1)

    def scalar(self, act, n, s, r, x_free=None, free_at=0):
        a, sm = self.nc.scalar, self.small[:, s, :]
        act.wait_ge(self.steps, (n + 1) * self.STEPS)
        if x_free is not None:
            act.wait_ge(x_free, free_at)
        a.activation(r if self.x is None else self.x[:, s, :], r, ACT.Identity, bias=sm[:, 4:5], scale=sm[:, 2:3]).then_inc(self.x_ready, 1)


def linear_ln(nc, tag, acts, weight, resid, out, mask=None):
    with ExitStack() as ctx:
        sb = lambda name, shape, dt=F32: ctx.enter_context(nc.sbuf_tensor(f"{tag}_{name}", shape, dt))
        sem = lambda name: ctx.enter_context(nc.semaphore(f"{tag}_{name}"))
        w = sb("w", [P, 2, KT, D], F32R)
        w_raw = sb("w_raw", [P, 2, D])
        a_raw = sb("a_raw", [P, 2, KT * P])
        a = sb("a", [P, 2, 2, KT * P], F32R)
        r = sb("r", [P, 2, D])
        ps = ctx.enter_context(nc.psum_tensor(f"{tag}_ps", [P, 2, D], F32))
        w_loaded = [sem(f"w_loaded{s}") for s in range(2)]
        w_hi, w_lo = sem("w_hi"), sem("w_lo")
        if mask is not None:
            w_masked = sem("w_masked")
            m_raw = sb("m_raw", [P, 2, D], I32)
            m_sum = sb("m_sum", [P, 2, BLK])
            m_one = sb("m_one", [P, 2, BLK])
            same = sb("same", [P, P])
            pm = ctx.enter_context(nc.psum_tensor(f"{tag}_pm", [P, 2, BANK], F32))
            m_loaded = [sem(f"m_loaded{s}") for s in range(2)]
            same_ready, sums_ready, blocks_ready, ones_ready = (
                sem(x) for x in ("same_ready", "sums_ready", "blocks_ready", "ones_ready"))
        a_loaded = [sem(f"a_loaded{s}") for s in range(2)]
        r_loaded = [sem(f"r_loaded{s}") for s in range(2)]
        a_hi, a_lo = sem("a_hi"), sem("a_lo")
        y_ready = sem("y_ready")
        sum_ready = sem("sum_ready")
        stored = [sem(f"stored{s}") for s in range(2)]
        ln = LayerNorm(nc, ctx, f"{tag}_ln", sum_ready)

        acts_tile = lambda n: acts[bass.ds(n, 1)].rearrange("a p u i -> (a p) u i")
        a_view = lambda s: a_raw[:, s, :].rearrange("p (u i) -> p u i", u=acts.shape[2])

        with nc.Block() as block:
            @block.sync
            def _(sp):
                sp.sem_inc(stored[0], 16)
                sp.sem_inc(stored[1], 16)
                for s in range(2):
                    sp.dma_start(a_view(s), acts_tile(s)).then_inc(a_loaded[s], 16)
                    sp.dma_start(r[:, s, :], resid[s]).then_inc(r_loaded[s], 16)
                    sp.dma_start(w_raw[:, s, :], weight[s]).then_inc(w_loaded[s], 16)
                    if mask is not None:
                        sp.dma_start(m_raw[:, s, :], mask[s]).then_inc(m_loaded[s], 16)
                with sp.Fori(1, KT // 2) as j:
                    for s in range(2):
                        sp.wait_ge(w_lo, j * 2 + s - 1)
                        sp.dma_start(w_raw[:, s, :], one(weight[bass.ds(j * 2 + s, 1)])).then_inc(w_loaded[s], 16)
                        if mask is not None:
                            sp.dma_start(m_raw[:, s, :], one(mask[bass.ds(j * 2 + s, 1)])).then_inc(m_loaded[s], 16)
                with sp.Fori(1, TILES // 2) as j:
                    for s in range(2):
                        sp.wait_ge(a_lo, j * 2 + s - 1)
                        sp.dma_start(a_view(s), acts_tile(j * 2 + s)).then_inc(a_loaded[s], 16)
                        sp.wait_ge(ln.x_ready, j * 2 + s - 1)
                        sp.dma_start(one(out[bass.ds(j * 2 + s - 2, 1)]), ln.x[:, s, :]).then_inc(stored[s], 16)
                        sp.dma_start(r[:, s, :], one(resid[bass.ds(j * 2 + s, 1)])).then_inc(r_loaded[s], 16)
                for s in range(2):
                    sp.wait_ge(ln.x_ready, TILES - 1 + s)
                    sp.dma_start(out[TILES - 2 + s], ln.x[:, s, :]).then_inc(stored[s], 16)
                for s in range(2):
                    sp.wait_ge(stored[s], 16 * (TILES // 2 + 1))

            @block.scalar
            def _(act):
                with act.Fori(0, KT // 2) as j:
                    for s in range(2):
                        if mask is None:
                            act.wait_ge(w_loaded[s], j * 16 + 16)
                        else:
                            act.wait_ge(w_masked, j * 2 + s + 1)
                        nc.scalar.copy(w[:, HI, bass.ds(j * 2 + s, 1), :].rearrange("p a n -> p (a n)"),
                                       w_raw[:, s, :]).then_inc(w_hi, 1)

                def split_hi(n, s, loads):
                    act.wait_ge(a_loaded[s], loads * 16)
                    act.wait_ge(y_ready, n + 1)
                    nc.scalar.copy(a[:, s, HI, :], a_raw[:, s, :]).then_inc(a_hi, 1)

                split_hi(0, 0, 1)
                with act.Fori(0, TILES // 2 - 1) as j:
                    split_hi(j * 2 + 1, 1, j + 1)
                    ln.scalar(act, j * 2, 0, r[:, 0, :], stored[0], j * 16 + 16)
                    split_hi(j * 2 + 2, 0, j + 2)
                    ln.scalar(act, j * 2 + 1, 1, r[:, 1, :], stored[1], j * 16 + 16)
                split_hi(TILES - 1, 1, TILES // 2)
                for s in range(2):
                    ln.scalar(act, TILES - 2 + s, s, r[:, s, :], stored[s], TILES // 2 * 16)

            @block.vector
            def _(dve):
                if mask is not None:
                    nc.vector.memset(same[:], 0.0).then_inc(same_ready, 1)
                    dve.wait_ge(same_ready, 1)
                    for b in range(P // BLK):
                        nc.vector.memset(same[b * BLK:(b + 1) * BLK, b * BLK:(b + 1) * BLK], 1.0).then_inc(same_ready, 1)
                with dve.Fori(0, KT // 2) as j:
                    for s in range(2):
                        dve.wait_ge(w_loaded[s], j * 16 + 16)
                        if mask is not None:
                            dve.wait_ge(m_loaded[s], j * 16 + 16)
                            nc.vector.reduce_sum(m_sum[:, s, :], m_raw[:, s, :].rearrange("p (b c) -> p b c", c=BLK),
                                                 AX.X).then_inc(sums_ready, 1)
                            dve.wait_ge(blocks_ready, j * 2 + s + 1)
                            nc.vector.tensor_scalar(m_one[:, s, :], pm[:, s, 0:BLK], 0.0, None, ALU.is_gt).then_inc(ones_ready, 1)
                            dve.wait_ge(ones_ready, j * 2 + s + 1)
                            w3 = w_raw[:, s, :].rearrange("p (b c) -> p b c", c=BLK)
                            nc.vector.tensor_tensor(w3, w3, m_one[:, s, :].unsqueeze(2).to_broadcast([P, BLK, BLK]),
                                                    ALU.mult).then_inc(w_masked, 1)
                        dve.wait_ge(w_hi, j * 2 + s + 1)
                        nc.vector.tensor_tensor(w[:, LO, bass.ds(j * 2 + s, 1), :].rearrange("p a n -> p (a n)"),
                                                w_raw[:, s, :],
                                                w[:, HI, bass.ds(j * 2 + s, 1), :].rearrange("p a n -> p (a n)").bitcast(F32),
                                                ALU.subtract).then_inc(w_lo, 1)

                def split_lo(n, s):
                    dve.wait_ge(a_hi, n + 1)
                    nc.vector.tensor_tensor(a[:, s, LO, :], a_raw[:, s, :], a[:, s, HI, :].bitcast(F32),
                                            ALU.subtract).then_inc(a_lo, 1)

                def finish(n, s, loads):
                    dve.wait_ge(r_loaded[s], loads * 16)
                    dve.wait_ge(y_ready, n + SLOTS + 1)
                    nc.vector.tensor_tensor(r[:, s, :], ps[:, s, :], r[:, s, :], ALU.add).then_inc(sum_ready, 1)
                    ln.vector(dve, n, s, r[:, s, :])

                dve.sem_inc(sum_ready, SLOTS)
                split_lo(0, 0)
                with dve.Fori(0, TILES // 2 - 1) as j:
                    split_lo(j * 2 + 1, 1)
                    finish(j * 2, 0, j + 1)
                    split_lo(j * 2 + 2, 0)
                    finish(j * 2 + 1, 1, j + 1)
                split_lo(TILES - 1, 1)
                for s in range(2):
                    finish(TILES - 2 + s, s, TILES // 2)

            @block.tensor
            def _(pe):
                if mask is not None:
                    pe.wait_ge(same_ready, 1 + P // BLK)
                    with pe.Fori(0, KT // 2) as j:
                        for s in range(2):
                            pe.wait_ge(sums_ready, j * 2 + s + 1)
                            nc.tensor.matmul(pm[:, s, 0:BLK], same[:], m_sum[:, s, :], start=True, stop=True).then_inc(blocks_ready, 1)
                pe.sem_inc(y_ready, SLOTS)
                pe.wait_ge(w_lo, KT)
                with pe.Fori(0, TILES // 2) as j:
                    for s in range(2):
                        n = j * 2 + s
                        pe.wait_ge(a_lo, n + 1)
                        pe.wait_ge(sum_ready, n + 1)
                        for h in range(2):
                            for kt in range(KT):
                                for wa, wb in PASSES:
                                    mm = nc.tensor.matmul(ps[:, s, h * BANK:(h + 1) * BANK], a[:, s, wa, kt * P:(kt + 1) * P],
                                                          w[:, wb, kt, h * BANK:(h + 1) * BANK],
                                                          start=(kt == 0 and (wa, wb) == PASSES[0]),
                                                          stop=(kt == KT - 1 and (wa, wb) == PASSES[-1]))
                        mm.then_inc(y_ready, 1)


NF4 = np.array([-1.0, -0.6961928009986877, -0.5250730514526367, -0.39491748809814453, -0.28444138169288635,
                -0.18477343022833334, -0.09105003625154495, 0.0, 0.07958029955625534, 0.16093020141124725,
                0.24611230194568634, 0.33791524171829224, 0.44070982933044434, 0.5626170039176941,
                0.7229568362236023, 1.0], np.float32)
NF4_ZERO = 7


def nf4_lines():
    def line(code, sign, values):
        x0 = code - NF4_ZERO
        slope = np.float64(values[1]) - np.float64(values[0])
        best = None
        for i in range(-64, 65):
            scale = np.float32(slope + i * np.float64(np.spacing(np.float32(slope))))
            for k in range(-8, 9):
                shift = np.float32(np.float64(values[0]) - np.float64(scale) * x0)
                shift = np.float32(shift + k * np.float64(np.spacing(shift)))
                got = [np.float32(np.float64(scale) * (x0 + n) + np.float64(shift)) for n in range(2)]
                miss = sum(abs(np.float64(g) - np.float64(v)) for g, v in zip(got, values))
                if best is None or miss < best[0]:
                    best = (miss, float(scale), float(shift))
        return best[1:]
    above = [line(c, 1, NF4[c:c + 2]) for c in (14, 12, 10, 8)]
    below = [line(c, -1, -NF4[c:c + 2]) for c in (0, 2, 4)]
    below.append(line(6, -1, [-NF4[6], np.float32(-1e-3)]))
    x = np.arange(16) - NF4_ZERO
    value = lambda lines: np.max([[np.float32(np.float64(np.float32(a)) * v + np.float64(np.float32(b))) for v in x]
                                  for a, b in lines] + [np.zeros(16)], axis=0)
    assert np.array_equal(np.float32(value(above)) - np.float32(value(below)), NF4)
    return above, below


def transpose_tokens(nc, tag, x, xT, ident):
    with ExitStack() as ctx:
        sb = lambda name, shape, dt=F32: ctx.enter_context(nc.sbuf_tensor(f"{tag}_{name}", shape, dt))
        sem = lambda name: ctx.enter_context(nc.semaphore(f"{tag}_{name}"))
        xn = sb("xn", [P, 2, D])
        ps = ctx.enter_context(nc.psum_tensor(f"{tag}_ps", [P, 2, D], F32))
        x_loaded = [sem(f"x_loaded{s}") for s in range(2)]
        turned, hi_ready, lo_ready = sem("turned"), sem("hi_ready"), sem("lo_ready")
        part = lambda comp, n: xT[:, comp, :, bass.ds(n * P, P)]
        with nc.Block() as block:
            @block.sync
            def _(sp):
                for s in range(2):
                    sp.dma_start(xn[:, s, :], x[s]).then_inc(x_loaded[s], 16)
                with sp.Fori(1, TILES // 2) as j:
                    for s in range(2):
                        sp.wait_ge(turned, j * 2 + s - 1)
                        sp.dma_start(xn[:, s, :], one(x[bass.ds(j * 2 + s, 1)])).then_inc(x_loaded[s], 16)

            @block.tensor
            def _(pe):
                with pe.Fori(0, TILES // 2) as j:
                    for s in range(2):
                        pe.wait_ge(x_loaded[s], j * 16 + 16)
                        pe.wait_ge(lo_ready, j * 2 + s + 1)
                        for kt in range(KT):
                            mm = nc.tensor.transpose(ps[:, s, kt * P:(kt + 1) * P], xn[:, s, kt * P:(kt + 1) * P], ident[:])
                        mm.then_inc(turned, 1)

            @block.scalar
            def _(act):
                with act.Fori(0, TILES // 2) as j:
                    for s in range(2):
                        act.wait_ge(turned, j * 2 + s + 1)
                        nc.scalar.copy(part(HI, j * 2 + s), ps[:, s, :].rearrange("p (k t) -> p k t", k=KT)).then_inc(hi_ready, 1)

            @block.vector
            def _(dve):
                dve.sem_inc(lo_ready, SLOTS)
                with dve.Fori(0, TILES // 2) as j:
                    for s in range(2):
                        dve.wait_ge(hi_ready, j * 2 + s + 1)
                        nc.vector.tensor_tensor(part(LO, j * 2 + s), ps[:, s, :].rearrange("p (k t) -> p k t", k=KT),
                                                part(HI, j * 2 + s).bitcast(F32), ALU.subtract).then_inc(lo_ready, 1)


GATE, UP, DOWN = range(3)


def ffn_up(nc, xT, codes, scales, down_w, inter):
    with ExitStack() as ctx:
        sb = lambda name, shape, dt=F32: ctx.enter_context(nc.sbuf_tensor(f"up_{name}", shape, dt))
        sem = lambda name: ctx.enter_context(nc.semaphore(f"up_{name}"))
        code = sb("code", [P, 2, D], I32)
        scale = sb("scale", [P, 2, D])
        line = sb("line", [P, 3, D])
        above, below = sb("above", [P, D]), sb("below", [P, D])
        w = sb("w", [P, 2, 2, 2, D], F32R)
        act_g = sb("act_g", [P, 2, BANK])
        prod = sb("prod", [P, 2, BANK])
        ps = ctx.enter_context(nc.psum_tensor("up_ps", [P, 2, BATCH, BANK], F32))
        code_loaded = [sem(f"code_loaded{s}") for s in range(2)]
        scale_loaded = [sem(f"scale_loaded{s}") for s in range(2)]
        centered = sem("centered")
        line_ready = sem("line_ready")
        folded = sem("folded")
        w_hi, w_lo = sem("w_hi"), sem("w_lo")
        down_stored = sem("down_stored")
        gate_ready, up_ready = sem("gate_ready"), sem("up_ready")
        silu_ready, prod_ready = sem("silu_ready"), sem("prod_ready")
        prod_stored = [sem(f"prod_stored{s}") for s in range(2)]
        W_FREE = 2 * BATCH
        PS_FREE = BATCH
        hi_lines, lo_lines = nf4_lines()
        LINES = hi_lines + lo_lines
        shifts = sb("shifts", [P, len(LINES)])
        shifts_set = sem("shifts_set")
        places = [above[:], line[:, 0, :], line[:, 1, :], line[:, 2, :],
                  below[:], line[:, 0, :], line[:, 1, :], line[:, 2, :]]

        def load_code(sp, c, m, slot):
            sp.dma_start(code[:, slot, :], one(codes[m][bass.ds(c, 1)])).then_inc(code_loaded[slot], 16)

        def load_scale(sp, c, m, slot):
            for h in range(2):
                dst = scale[64 * h:64 * h + 64, slot, :]
                if m == DOWN:
                    src = scales[m][bass.ds(c, 1), h, :].to_broadcast([64, D])
                    sp.dma_start(dst, src).then_inc(scale_loaded[slot], 16)
                else:
                    src = scales[m][bass.ds(c, 1), h].to_broadcast([64, KT, P])
                    sp.dma_start(dst.rearrange("p (k i) -> p k i", k=KT), src).then_inc(scale_loaded[slot], 16)

        def uses(k, slot):
            return (k - slot) // 2 + 1 if isinstance(k, int) else None

        with nc.Block() as block:
            @block.sync
            def _(sp):
                def after_unit(c, m, slot, k, c2, m2, load=True):
                    if load:
                        sp.wait_ge(line_ready, k * 8 + 8)
                        load_code(sp, c2, m2, slot)
                    if m == DOWN:
                        sp.wait_ge(folded, k * 8 + 8)
                        sp.dma_start(one(down_w[bass.ds(c, 1)]), scale[:, slot, :]).then_inc(down_stored, 16)
                        sp.wait_ge(down_stored, c * 16 + 16)
                    else:
                        sp.wait_ge(w_lo, c * 2 + m + 1)
                    if load:
                        load_scale(sp, c2, m2, slot)

                def store(c, tb):
                    sp.wait_ge(prod_ready, c * BATCH + tb + 1 + PS_FREE)
                    sp.dma_start(inter[bass.ds(c, 1), tb].rearrange("a p n -> p (a n)"),
                                 prod[:, tb % 2, :]).then_inc(prod_stored[tb % 2], 16)

                def nxt(c, m):
                    return (c + (m + 2) // 3, (m + 2) % 3)

                for m in (GATE, UP):
                    load_code(sp, 0, m, m % 2)
                    load_scale(sp, 0, m, m % 2)
                for m in range(3):
                    after_unit(0, m, m % 2, m, *nxt(0, m))

                def chunk(c, odd, units, loads=3):
                    for tb in range(BATCH):
                        if tb < 3 and units:
                            k = (c + 1) * 3 + tb
                            after_unit(c + 1, tb, (odd + 1 + tb) % 2, k, *nxt(c + 1, tb), load=tb < loads)
                        store(c, tb)
                with sp.Fori(0, CH // 2 - 1) as j:
                    chunk(j * 2, 0, True)
                    chunk(j * 2 + 1, 1, True)
                chunk(CH - 2, 0, True, loads=1)
                chunk(CH - 1, 1, False)
                for s in range(2):
                    sp.wait_ge(prod_stored[s], 16 * (CH * 2 + 1))

            @block.scalar
            def _(act):
                def unit(k, slot):
                    act.wait_ge(centered, k + 1)
                    for i, (a, b) in enumerate(LINES):
                        if i == 0 and not (isinstance(k, int) and k == 0):
                            act.wait_ge(folded, k * 8)
                        if i >= 5:
                            act.wait_ge(folded, k * 8 + i - 4)
                        x = code[:, slot, :].bitcast(F32)
                        func = ACT.Relu if i in (0, 4) else ACT.Identity
                        nc.scalar.activation(places[i], x, func, bias=shifts[:, i:i + 1], scale=a).then_inc(line_ready, 1)

                def silu(c, tb):
                    act.wait_ge(gate_ready, c * BATCH + tb + 1)
                    act.wait_ge(prod_ready, c * BATCH + tb - 1 + PS_FREE)
                    nc.scalar.activation(act_g[:, tb % 2, :], ps[:, GATE, tb, :], ACT.Silu).then_inc(silu_ready, 1)

                def chunk(c, odd, units):
                    for tb in range(BATCH):
                        if tb < 3 and units:
                            unit((c + 1) * 3 + tb, (odd + 1 + tb) % 2)
                        silu(c, tb)
                act.wait_ge(shifts_set, len(LINES))
                for k in range(3):
                    unit(k, k % 2)
                with act.Fori(0, CH // 2 - 1) as j:
                    chunk(j * 2, 0, True)
                    chunk(j * 2 + 1, 1, True)
                chunk(CH - 2, 0, True)
                chunk(CH - 1, 1, False)

            @block.vector
            def _(dve):
                v = nc.vector
                for i, (a, b) in enumerate(LINES):
                    v.memset(shifts[:, i:i + 1], b).then_inc(shifts_set, 1)
                dve.sem_inc(prod_ready, PS_FREE)
                for s in range(2):
                    dve.sem_inc(prod_stored[s], 16)

                def center(k, slot, loads):
                    dve.wait_ge(code_loaded[slot], loads * 16)
                    v.tensor_scalar(code[:, slot, :].bitcast(F32), code[:, slot, :], float(NF4_ZERO), None,
                                    ALU.subtract).then_inc(centered, 1)

                def fold(k, slot, loads):
                    for m in range(1, 7):
                        i = m if m < 4 else m + 1
                        into = above if m < 4 else below
                        dve.wait_ge(line_ready, k * 8 + i + 1)
                        if m > 1:
                            dve.wait_ge(folded, k * 8 + m - 1)
                        v.tensor_tensor(into[:], into[:], places[i], ALU.max).then_inc(folded, 1)
                    dve.wait_ge(folded, k * 8 + 6)
                    v.tensor_tensor(above[:], above[:], below[:], ALU.subtract).then_inc(folded, 1)
                    dve.wait_ge(folded, k * 8 + 7)
                    dve.wait_ge(scale_loaded[slot], loads * 32)
                    v.tensor_tensor(scale[:, slot, :], above[:], scale[:, slot, :], ALU.mult).then_inc(folded, 1)

                def split(c, m, slot, odd, k):
                    dve.wait_ge(folded, k * 8 + 8)
                    dve.wait_ge(up_ready, c * BATCH + W_FREE - BATCH)
                    v.tensor_copy(w[:, odd, m, HI, :], scale[:, slot, :]).then_inc(w_hi, 1)
                    dve.wait_ge(w_hi, c * 2 + m + 1)
                    v.tensor_tensor(w[:, odd, m, LO, :], scale[:, slot, :], w[:, odd, m, HI, :].bitcast(F32),
                                    ALU.subtract).then_inc(w_lo, 1)

                def unit(c, m, odd, slot, k, loads, next_loads, more=True):
                    fold(k, slot, loads)
                    if more:
                        center(k + 1, 1 - slot, next_loads)
                    if m != DOWN:
                        split(c, m, slot, odd, k)

                def product(c, tb, stores):
                    s = tb % 2
                    dve.wait_ge(silu_ready, c * BATCH + tb + 1)
                    dve.wait_ge(up_ready, c * BATCH + tb + 1 + W_FREE)
                    dve.wait_ge(prod_stored[s], stores * 16)
                    v.tensor_tensor(prod[:, s, :], act_g[:, s, :], ps[:, UP, tb, :], ALU.mult).then_inc(prod_ready, 1)

                center(0, 0, 1)
                for k in range(3):
                    unit(0, k, 0, k % 2, k, k // 2 + 1, (k + 1) // 2 + 1)

                def chunk(c, odd, units, half):
                    for tb in range(BATCH):
                        if tb < 3 and units:
                            rest = 3 * odd + 3 + tb
                            unit(c + 1, tb, 1 - odd, rest % 2, half * 6 + rest, half * 3 + rest // 2 + 1,
                                 half * 3 + (rest + 1) // 2 + 1,
                                 more=not (isinstance(c, int) and c == CH - 2 and tb == 2))
                        product(c, tb, half * 4 + 2 * odd + tb // 2 + 1)
                with dve.Fori(0, CH // 2 - 1) as j:
                    chunk(j * 2, 0, True, j)
                    chunk(j * 2 + 1, 1, True, j)
                chunk(CH - 2, 0, True, CH // 2 - 1)
                chunk(CH - 1, 1, False, CH // 2 - 1)

            @block.tensor
            def _(pe):
                pe.sem_inc(up_ready, W_FREE)

                def chunk(c, odd):
                    pe.wait_ge(w_lo, c * 2 + 2)
                    for tb in range(BATCH):
                        pe.wait_ge(prod_ready, c * BATCH + tb + 1)
                        for m, ready in ((GATE, gate_ready), (UP, up_ready)):
                            for kt in range(KT):
                                for wa, wb in PASSES:
                                    mm = nc.tensor.matmul(ps[:, m, tb, :], w[:, odd, m, wa, kt * P:(kt + 1) * P],
                                                          xT[:, wb, kt, tb * BANK:(tb + 1) * BANK],
                                                          start=(kt == 0 and (wa, wb) == PASSES[0]),
                                                          stop=(kt == KT - 1 and (wa, wb) == PASSES[-1]))
                            mm.then_inc(ready, 1)
                with pe.Fori(0, CH // 2) as j:
                    chunk(j * 2, 0)
                    chunk(j * 2 + 1, 1)


def ffn_down(nc, inter, weight, resid, out):
    with ExitStack() as ctx:
        sb = lambda name, shape, dt=F32: ctx.enter_context(nc.sbuf_tensor(f"down_{name}", shape, dt))
        sem = lambda name: ctx.enter_context(nc.semaphore(f"down_{name}"))
        w = sb("w", [P, 2, CH, D], F32R)
        w_raw = sb("w_raw", [P, D])
        a_raw = sb("a_raw", [P, 2, BANK])
        a = sb("a", [P, 2, 2, BANK], F32R)
        r = sb("r", [P, 4, D])
        ps = ctx.enter_context(nc.psum_tensor("down_ps", [P, 4, D], F32))
        w_loaded = sem("w_loaded")
        w_hi, w_lo = sem("w_hi"), sem("w_lo")
        a_loaded = [sem(f"a_loaded{s}") for s in range(2)]
        a_hi, a_lo = sem("a_hi"), sem("a_lo")
        r_loaded = [sem(f"r_loaded{t}") for t in range(4)]
        used = sem("used")
        y_ready = sem("y_ready")
        sum_ready = sem("sum_ready")
        stored = [sem(f"stored{t}") for t in range(4)]
        ln = LayerNorm(nc, ctx, "down_ln", sum_ready, base=4, slots=4, in_place=True)
        HEAD = 12
        NORM_AT, STORE_AT, RESID_AT = 2, 3, 8

        def over_k(eng, step, first):
            for k in range(HEAD):
                step(k, k % 2, k // 2, first)
            with eng.Fori(HEAD // 2, CH // 2) as j:
                for s in range(2):
                    step(j * 2 + s, s, j, first)

        with nc.Block() as block:
            @block.sync
            def _(sp):
                def block_of(tb, first):
                    def step(k, s, pair, first):
                        if first:
                            if not (isinstance(k, int) and k == 0):
                                sp.wait_ge(w_lo, k)
                            sp.dma_start(w_raw[:], one(weight[bass.ds(k, 1)])).then_inc(w_loaded, 16)
                        if not (first and isinstance(k, int) and k < 2):
                            sp.wait_ge(a_lo, tb * CH + k - 1)
                        sp.dma_start(a_raw[:, s, :], inter[bass.ds(k, 1), bass.ds(tb, 1)].rearrange("a b p n -> p (a b n)")
                                     ).then_inc(a_loaded[s], 16)
                        if isinstance(k, int) and not first and STORE_AT <= k < STORE_AT + 4:
                            store(tb - 1, k - STORE_AT)
                        if isinstance(k, int) and RESID_AT <= k < RESID_AT + 4:
                            t = k - RESID_AT
                            if not first:
                                sp.wait_ge(stored[t], tb * 16)
                            sp.dma_start(r[:, t, :], one(resid[bass.ds(tb * 4 + t, 1)])).then_inc(r_loaded[t], 16)
                    over_k(sp, step, first)

                def store(tb, t):
                    sp.wait_ge(ln.x_ready, tb * 4 + t + 1)
                    sp.dma_start(one(out[bass.ds(tb * 4 + t, 1)]), r[:, t, :]).then_inc(stored[t], 16)

                block_of(0, True)
                with sp.Fori(1, BATCH) as tb:
                    block_of(tb, False)
                for t in range(4):
                    store(BATCH - 1, t)
                for t in range(4):
                    sp.wait_ge(stored[t], BATCH * 16)

            @block.scalar
            def _(act):
                def block_of(tb, first):
                    def step(k, s, pair, first):
                        if first:
                            act.wait_ge(w_loaded, k * 16 + 16)
                            nc.scalar.copy(w[:, HI, bass.ds(k, 1), :].rearrange("p a n -> p (a n)"), w_raw[:]).then_inc(w_hi, 1)
                        act.wait_ge(a_loaded[s], (tb * (CH // 2) + pair) * 16 + 16)
                        act.wait_ge(used, tb * CH + k + 1)
                        nc.scalar.copy(a[:, s, HI, :], a_raw[:, s, :]).then_inc(a_hi, 1)
                        if isinstance(k, int) and not first and NORM_AT <= k < NORM_AT + 4:
                            ln.scalar(act, tb * 4 - 4 + k - NORM_AT, k - NORM_AT, r[:, k - NORM_AT, :])
                    over_k(act, step, first)
                block_of(0, True)
                with act.Fori(1, BATCH) as tb:
                    block_of(tb, False)
                for t in range(4):
                    ln.scalar(act, (BATCH - 1) * 4 + t, t, r[:, t, :])

            @block.vector
            def _(dve):
                def add(n, t, loads):
                    dve.wait_ge(r_loaded[t], loads * 16)
                    dve.wait_ge(y_ready, n + 1)
                    nc.vector.tensor_tensor(r[:, t, :], ps[:, t, :], r[:, t, :], ALU.add).then_inc(sum_ready, 1)

                def block_of(tb, first):
                    def step(k, s, pair, first):
                        if first:
                            dve.wait_ge(w_hi, k + 1)
                            lo = w[:, LO, bass.ds(k, 1), :].rearrange("p a n -> p (a n)")
                            hi = w[:, HI, bass.ds(k, 1), :].rearrange("p a n -> p (a n)").bitcast(F32)
                            nc.vector.tensor_tensor(lo, w_raw[:], hi, ALU.subtract).then_inc(w_lo, 1)
                        dve.wait_ge(a_hi, tb * CH + k + 1)
                        nc.vector.tensor_tensor(a[:, s, LO, :], a_raw[:, s, :], a[:, s, HI, :].bitcast(F32),
                                                ALU.subtract).then_inc(a_lo, 1)
                        if isinstance(k, int) and not first:
                            if k == 0:
                                for t in range(4):
                                    add(tb * 4 - 4 + t, t, tb)
                            if NORM_AT <= k + 1 < NORM_AT + 4:
                                ln.vector(dve, tb * 4 - 4 + k + 1 - NORM_AT, k + 1 - NORM_AT, r[:, k + 1 - NORM_AT, :])
                    over_k(dve, step, first)
                dve.sem_inc(sum_ready, 4)
                block_of(0, True)
                with dve.Fori(1, BATCH) as tb:
                    block_of(tb, False)
                for t in range(4):
                    add((BATCH - 1) * 4 + t, t, BATCH)
                for t in range(4):
                    ln.vector(dve, (BATCH - 1) * 4 + t, t, r[:, t, :])

            @block.tensor
            def _(pe):
                pe.sem_inc(used, SLOTS)

                def products(tb, k, s, start, last, first):
                    pe.wait_ge(a_lo, tb * CH + k + 1)
                    if first:
                        pe.wait_ge(w_lo, k + 1)
                    for t in range(4):
                        if start:
                            pe.wait_ge(sum_ready, tb * 4 + t + 1)
                        for h in range(2):
                            for wa, wb in PASSES:
                                rhs = w[:, wb, bass.ds(k, 1), h * BANK:(h + 1) * BANK].rearrange("p a n -> p (a n)")
                                mm = nc.tensor.matmul(ps[:, t, h * BANK:(h + 1) * BANK], a[:, s, wa, t * P:(t + 1) * P], rhs,
                                                      start=(start and (wa, wb) == PASSES[0]),
                                                      stop=(last and (wa, wb) == PASSES[-1]))
                        if last and t < 3:
                            mm.then_inc(y_ready, 1)
                    if last:
                        mm.then_inc(y_ready, 1)
                        pe.wait_ge(y_ready, tb * 4 + 4)
                        pe.sem_inc(used, 1)
                    else:
                        mm.then_inc(used, 1)

                def block_of(tb, first):
                    products(tb, 0, 0, True, False, first)
                    products(tb, 1, 1, False, False, first)
                    with pe.Fori(1, CH // 2 - 1) as j:
                        products(tb, j * 2, 0, False, False, first)
                        products(tb, j * 2 + 1, 1, False, False, first)
                    products(tb, CH - 2, 0, False, False, first)
                    products(tb, CH - 1, 1, False, True, first)
                block_of(0, True)
                with pe.Fori(1, BATCH) as tb:
                    block_of(tb, False)


def project_qk(nc, xT, weight, tables, out):
    UNITS = 2 * QK_GROUPS
    with ExitStack() as ctx:
        sb = lambda name, shape, dt=F32: ctx.enter_context(nc.sbuf_tensor(f"qk_{name}", shape, dt))
        sem = lambda name: ctx.enter_context(nc.semaphore(f"qk_{name}"))
        w_raw = sb("w_raw", [P, KT * 2 * P])
        w = sb("w", [P, 2, 2, KT, 2, P], F32R)
        table = sb("table", [P, 2, 2, SEQ])
        t = sb("t", [P, 4, SEQ])
        o = sb("o", [P, 2, 2, 2, SEQ], F32R)
        ps = ctx.enter_context(nc.psum_tensor("qk_ps", [P, 2, 2, BANK], F32))
        table_loaded = sem("table_loaded")
        w_loaded, w_hi, w_lo = sem("w_loaded"), sem("w_hi"), sem("w_lo")
        y_ready = sem("y_ready")
        turned = sem("turned")
        out_hi, out_lo = sem("out_hi"), sem("out_lo")
        stored = [sem(f"stored{s}") for s in range(2)]
        W_FREE = 2 * BATCH
        PS_FREE = 2 * 6
        T_FREE = 2

        with nc.Block() as block:
            @block.sync
            def _(sp):
                sp.dma_start(w_raw[:], weight[0]).then_inc(w_loaded, 16)
                sp.dma_start(table[:], tables.rearrange("m i p n -> p m i n")).then_inc(table_loaded, 16)

                def unit(u, last=False):
                    if not last:
                        sp.wait_ge(w_lo, u + 1)
                        sp.dma_start(w_raw[:], one(weight[bass.ds(u + 1, 1)])).then_inc(w_loaded, 16)
                    for b in range(BATCH):
                        n, s = u * BATCH + b, b % 2
                        sp.wait_ge(out_lo, n * 2 + 2 + T_FREE)
                        for comp in range(2):
                            for ab in range(2):
                                sp.dma_start(out[bass.ds(u, 1), b, :, comp, ab].rearrange("a h j n -> (a h) j n"),
                                             o[:, s, comp, ab, :].bitcast(F32)).then_inc(stored[s], 16)
                with sp.Fori(0, UNITS - 1) as u:
                    unit(u)
                unit(UNITS - 1, last=True)
                for s in range(2):
                    sp.wait_ge(stored[s], (UNITS * BATCH // 2 + 1) * 64)

            @block.scalar
            def _(act):
                def split_hi(u, s):
                    act.wait_ge(w_loaded, u * 16 + 16)
                    act.wait_ge(y_ready, u * BATCH + BATCH)
                    nc.scalar.copy(w[:, s, HI].rearrange("p k a i -> p (k a i)"), w_raw[:]).then_inc(w_hi, 1)

                def outputs(u, b, stores):
                    n, s = u * BATCH + b, b % 2
                    for ab in range(2):
                        act.wait_ge(turned, n * 6 + 3 + 3 * ab + PS_FREE)
                        if ab == 0:
                            act.wait_ge(stored[s], stores * 64)
                        nc.scalar.copy(o[:, s, HI, ab, :], t[:, 2 * ab, :]).then_inc(out_hi, 1)

                def unit(u, s, more=True):
                    for b in range(BATCH):
                        outputs(u, b, u * 2 + b // 2 + 1)
                        if b == 0 and more:
                            split_hi(u + 1, 1 - s)

                split_hi(0, 0)
                with act.Fori(0, UNITS // 2 - 1) as j:
                    unit(j * 2, 0)
                    unit(j * 2 + 1, 1)
                unit(UNITS - 2, 0)
                unit(UNITS - 1, 1, more=False)

            @block.vector
            def _(dve):
                v = nc.vector

                def split_lo(u, s):
                    dve.wait_ge(w_hi, u + 1)
                    v.tensor_tensor(w[:, s, LO].rearrange("p k a i -> p (k a i)"), w_raw[:],
                                    w[:, s, HI].rearrange("p k a i -> p (k a i)").bitcast(F32),
                                    ALU.subtract).then_inc(w_lo, 1)

                def rotate(u, b, m):
                    n, s = u * BATCH + b, b % 2
                    dve.wait_ge(y_ready, n + 1 + W_FREE)
                    for ab in range(2):
                        dve.wait_ge(out_lo, n * 2 + ab - 1 + T_FREE)
                        v.tensor_tensor(t[:, 2 * ab, :], ps[:, s, 0, :], table[:, m, ab, :], ALU.mult).then_inc(turned, 1)
                        v.tensor_tensor(t[:, 2 * ab + 1, :], ps[:, s, 1, :], table[:, m, 1 - ab, :], ALU.mult).then_inc(turned, 1)
                        dve.wait_ge(turned, n * 6 + 3 * ab + 2 + PS_FREE)
                        v.tensor_tensor(t[:, 2 * ab, :], t[:, 2 * ab, :], t[:, 2 * ab + 1, :],
                                        ALU.add if ab else ALU.subtract).then_inc(turned, 1)
                    for ab in range(2):
                        dve.wait_ge(out_hi, n * 2 + ab + 1)
                        v.tensor_tensor(o[:, s, LO, ab, :], t[:, 2 * ab, :], o[:, s, HI, ab, :].bitcast(F32),
                                        ALU.subtract).then_inc(out_lo, 1)

                for s in range(2):
                    dve.sem_inc(stored[s], 64)
                dve.sem_inc(turned, PS_FREE)
                dve.sem_inc(out_lo, T_FREE)
                dve.wait_ge(table_loaded, 16)
                def unit(u, s, m, more=True):
                    for b in range(BATCH):
                        rotate(u, b, m)
                        if b == 0 and more:
                            split_lo(u + 1, 1 - s)

                split_lo(0, 0)
                with dve.Fori(0, QK_GROUPS // 2) as j:
                    unit(j * 2, 0, 0)
                    unit(j * 2 + 1, 1, 0)
                with dve.Fori(QK_GROUPS // 2, UNITS // 2 - 1) as j:
                    unit(j * 2, 0, 1)
                    unit(j * 2 + 1, 1, 1)
                unit(UNITS - 2, 0, 1)
                unit(UNITS - 1, 1, 1, more=False)

            @block.tensor
            def _(pe):
                pe.sem_inc(y_ready, W_FREE)
                with pe.Fori(0, UNITS // 2) as j:
                    for slot in range(2):
                        u = j * 2 + slot
                        pe.wait_ge(w_lo, u + 1)
                        for b in range(BATCH):
                            n, s = u * BATCH + b, b % 2
                            pe.wait_ge(turned, n * 6 + 6)
                            for ab in range(2):
                                for kt in range(KT):
                                    for wa, wb in PASSES:
                                        mm = nc.tensor.matmul(ps[:, s, ab, :], w[:, slot, wa, kt, ab, :],
                                                              xT[:, wb, kt, b * BANK:(b + 1) * BANK],
                                                              start=(kt == 0 and (wa, wb) == PASSES[0]),
                                                              stop=(kt == KT - 1 and (wa, wb) == PASSES[-1]))
                            mm.then_inc(y_ready, 1)


def project_v(nc, xT, weight, out):
    with ExitStack() as ctx:
        sb = lambda name, shape, dt=F32: ctx.enter_context(nc.sbuf_tensor(f"v_{name}", shape, dt))
        sem = lambda name: ctx.enter_context(nc.semaphore(f"v_{name}"))
        w_raw = sb("w_raw", [P, KT, BANK])
        w = sb("w", [P, 2, 2, KT, BANK], F32R)
        o = sb("o", [P, 2, BANK])
        ps = ctx.enter_context(nc.psum_tensor("v_ps", [P, 4, BANK], F32))
        w_loaded, w_hi, w_lo = sem("w_loaded"), sem("w_hi"), sem("w_lo")
        y_ready = sem("y_ready")
        taken = sem("taken")
        stored = [sem(f"stored{s}") for s in range(2)]
        PS_FREE = 4
        with nc.Block() as block:
            @block.sync
            def _(sp):
                for half in range(2):
                    for kt in range(KT):
                        if half:
                            sp.wait_ge(w_lo, kt + 1)
                        sp.dma_start(w_raw[:, kt, :], weight[half][:, kt * BANK:(kt + 1) * BANK]).then_inc(w_loaded, 16)
                        sp.wait_ge(w_loaded, (half * KT + kt + 1) * 16)
                with sp.Fori(0, 2) as half:
                    for n in range(TILES):
                        sp.wait_ge(taken, half * TILES + n + 1 + PS_FREE)
                        sp.dma_start(out[bass.ds(half * 2, 2), n // 4, n % 4].rearrange("u p c -> p u c"),
                                     o[:, n % 2, :].rearrange("p (u c) -> p u c", u=2)).then_inc(stored[n % 2], 16)
                for s in range(2):
                    sp.wait_ge(stored[s], (TILES + 1) * 16)

            @block.scalar
            def _(act):
                def split_hi(half, kt):
                    act.wait_ge(w_loaded, (half * KT + kt + 1) * 16)
                    nc.scalar.copy(w[:, half, HI, kt, :], w_raw[:, kt, :]).then_inc(w_hi, 1)

                for half in range(2):
                    for kt in range(KT):
                        split_hi(half, kt)
                with act.Fori(0, 2) as half:
                    for n in range(TILES):
                        act.wait_ge(y_ready, half * TILES + n + 1)
                        act.wait_ge(stored[n % 2], (half * (TILES // 2) + n // 2 + 1) * 16)
                        nc.scalar.copy(o[:, n % 2, :], ps[:, n % 4, :]).then_inc(taken, 1)

            @block.vector
            def _(dve):
                dve.sem_inc(taken, PS_FREE)
                for s in range(2):
                    dve.sem_inc(stored[s], 16)
                for half in range(2):
                    for kt in range(KT):
                        dve.wait_ge(w_hi, half * KT + kt + 1)
                        nc.vector.tensor_tensor(w[:, half, LO, kt, :], w_raw[:, kt, :], w[:, half, HI, kt, :].bitcast(F32),
                                                ALU.subtract).then_inc(w_lo, 1)

            @block.tensor
            def _(pe):
                with pe.Fori(0, 2) as half:
                    pe.wait_ge(w_lo, half * KT + KT)
                    for n in range(TILES):
                        pe.wait_ge(taken, half * TILES + n + 1)
                        for kt in range(KT):
                            for wa, wb in PASSES:
                                rhs = w[:, bass.ds(half, 1), wb, kt, :].rearrange("p a n -> p (a n)")
                                mm = nc.tensor.matmul(ps[:, n % 4, :], xT[:, wa, kt, n * P:(n + 1) * P], rhs,
                                                      start=(kt == 0 and (wa, wb) == PASSES[0]),
                                                      stop=(kt == KT - 1 and (wa, wb) == PASSES[-1]))
                        mm.then_inc(y_ready, 1)


def attention(nc, ident, ident_b, above_b, qk, v, out):
    NS, HU = 16, 8
    N_HEADS = NS * HU
    QT = SEQ // P
    CAUSAL = P * (QT * (QT + 1) // 2)
    WIDE = 2 * P
    S_AT = (2 * BANK + WIDE, 2 * BANK, BANK, 0)
    S_BANKS = ((3,), (2,), (1, 0))
    N_AT = (0, 128, 384, 768)
    T_AT = (0, BANK, 2 * BANK, BANK + 3 * P)
    T_PARTS = ((0,), (1, 3, 2))
    with ExitStack() as ctx:
        sb = lambda name, shape, dt=F32: ctx.enter_context(nc.sbuf_tensor(f"at_{name}", shape, dt))
        sem = lambda name: ctx.enter_context(nc.semaphore(f"at_{name}"))
        qk_sb = sb("qk", [P, 2, 2, 2, SEQ], F32R)
        vc = sb("vc", [P, QT, 2 * P])
        vp = sb("vp", [P, 2, QT * 4 * P])
        prob = sb("prob", [P, 4, CAUSAL])
        pt = sb("pt", [P, 2, CAUSAL])
        ot = sb("ot", [P, 2, SEQ])
        top = sb("top", [P, 2, 4])
        total = sb("total", [P, 2, 4])
        inv = sb("inv", [P, 2, 4])
        ps_s = ctx.enter_context(nc.psum_tensor("at_s", [P, 3 * BANK], F32))
        ps_t = ctx.enter_context(nc.psum_tensor("at_t", [P, 3 * BANK], F32))
        ps_o = ctx.enter_context(nc.psum_tensor("at_o", [P, 2, BANK], F32))
        qk_loaded = [sem(f"qk_loaded{s}") for s in range(2)]
        v_loaded = sem("v_loaded")
        s_ready = sem("s_ready")
        top_ready = sem("top_ready")
        exp_ready = sem("exp_ready")
        inv_ready = sem("inv_ready")
        prob_act, prob_dve = sem("prob_act"), sem("prob_dve")
        turned = sem("turned")
        pt_act, pt_dve = sem("pt_act"), sem("pt_dve")
        zeros_set, vp_seen = sem("zeros_set"), sem("vp_seen")
        vp_ready = sem("vp_ready")
        head_done = sem("head_done")
        o_out = sem("o_out")
        stored = [sem(f"stored{s}") for s in range(2)]
        S_BASE, EXP_BASE, PT_BASE, DONE_BASE, O_BASE = 12, 3, 3, 8, 2

        def spread(slot):
            t = vp[:, slot, :]
            return bass.AP(t.tensor, t.offset, [list(t.ap[0]), [4 * P, QT], [P + HD, 4], [1, HD]])

        with nc.Block() as block:
            @block.sync
            def _(sp):
                def load_pair(n, p, s):
                    sp.wait_ge(s_ready, (n * 8 + 2 * p - 2) * 3 + S_BASE)
                    for m in range(2):
                        src = qk[m, bass.ds(n, 1), 2 * p:2 * p + 2].rearrange("a h c r t -> (a c) r h t")
                        for rows in range(4):
                            comp = rows % 2 if m == 0 else rows // 2
                            sp.dma_start(qk_sb[rows * HD:(rows + 1) * HD, s, m].bitcast(F32), src[comp]).then_inc(qk_loaded[s], 16)

                def load_v(n):
                    sp.dma_start(vc[:], v[bass.ds(n, 1)].rearrange("a k p c -> (a p) k c")).then_inc(v_loaded, 16)

                def store(n, gg):
                    sp.wait_ge(o_out, n * 2 + gg + 1 + O_BASE)
                    dst = out[bass.ds(n * QT, QT), :, gg * P:(gg + 1) * P].rearrange("t p i -> p t i")
                    sp.dma_start(dst, ot[:, gg, :].rearrange("p (t i) -> p t i", t=QT)).then_inc(stored[gg], 16)

                def eight(n, first=False, last=False):
                    load_pair(n, 2, 0)
                    load_pair(n, 3, 1)
                    if not first:
                        store(n - 1, 1)
                    if not last:
                        sp.wait_ge(vp_ready, n * 2 + 2)
                        load_v(n + 1)
                        load_pair(n + 1, 0, 0)
                        load_pair(n + 1, 1, 1)
                    store(n, 0)

                load_pair(0, 0, 0)
                load_pair(0, 1, 1)
                load_v(0)
                eight(0, first=True)
                with sp.Fori(1, NS - 1) as n:
                    eight(n)
                eight(NS - 1, last=True)
                store(NS - 1, 1)
                for s in range(2):
                    sp.wait_ge(stored[s], (NS + 1) * 16)

            @block.gpsimd
            def _(pool):
                g = nc.gpsimd
                g.memset(vp[:], 0.0).then_inc(zeros_set, 1)
                pool.wait_ge(zeros_set, 1)

                def spread_v(n, gg):
                    if gg == 0:
                        pool.wait_ge(v_loaded, n * 16 + 16)
                    pool.wait_ge(head_done, n * 8 + gg * 4 - 4 + DONE_BASE)
                    pool.sem_inc(vp_seen, 1)
                    g.tensor_copy(spread(gg), vc[:, :, gg * P:(gg + 1) * P].rearrange(
                        "p k (j d) -> p k j d", j=4)).then_inc(vp_ready, 1)

                with pool.Fori(0, NS) as n:
                    for gg in range(2):
                        spread_v(n, gg)

            @block.scalar
            def _(act):
                a = nc.scalar

                def exponentials(n, hh):
                    s, i = hh % 2, n * 8 + hh
                    for bank, tiles in enumerate(S_BANKS):
                        act.wait_ge(top_ready, i * 3 + bank + 1)
                        for q in tiles:
                            e = a.activation(prob[:, hh % 4, N_AT[q]:N_AT[q] + (q + 1) * P], ps_s[:, S_AT[q]:S_AT[q] + (q + 1) * P],
                                             ACT.Exp, bias=top[:, s, q:q + 1], accum_out=total[:, s, q:q + 1])
                        e.then_inc(exp_ready, 1)

                def normalize(i, hh):
                    act.wait_ge(inv_ready, i + 1)
                    x = prob[:, hh % 4, N_AT[3]:CAUSAL]
                    a.activation(x, x, ACT.Copy, scale=inv[:, hh % 2, 3:4]).then_inc(prob_act, 1)

                def take_part(i, hh):
                    act.wait_ge(head_done, i - 1 + DONE_BASE)
                    act.wait_ge(turned, i * 2 + 1)
                    a.copy(pt[:, hh % 2, 0:BANK], ps_t[:, 0:BANK]).then_inc(pt_act, 1)

                def step(n, hh, first=False):
                    i = n * 8 + hh
                    if not first or hh >= 2:
                        take_part(i - 2, (hh - 2) % HU)
                    exponentials(n, hh)
                    if not first or hh >= 1:
                        normalize(i - 1, (hh - 1) % HU)
                for hh in range(HU):
                    step(0, hh, first=True)
                with act.Fori(1, NS) as n:
                    for hh in range(HU):
                        step(n, hh)
                take_part(N_HEADS - 2, 6)
                normalize(N_HEADS - 1, 7)
                take_part(N_HEADS - 1, 7)

            @block.vector
            def _(dve):
                v_ = nc.vector
                for s, start in ((s_ready, S_BASE), (exp_ready, EXP_BASE), (pt_act, PT_BASE), (pt_dve, PT_BASE),
                                 (head_done, DONE_BASE), (o_out, O_BASE), (stored[0], 16), (stored[1], 16)):
                    dve.sem_inc(s, start)

                def maxima(n, hh):
                    s, i = hh % 2, n * 8 + hh
                    for bank, tiles in enumerate(S_BANKS):
                        dve.wait_ge(s_ready, i * 3 + bank + 1 + S_BASE)
                        for q in tiles:
                            m = v_.reduce_max(top[:, s, q:q + 1], ps_s[:, S_AT[q]:S_AT[q] + (q + 1) * P], AX.X, negate=True)
                        m.then_inc(top_ready, 1)

                def normalize(i, hh):
                    dve.wait_ge(exp_ready, i * 3 + 3 + EXP_BASE)
                    v_.reciprocal(inv[:, hh % 2, :], total[:, hh % 2, :]).then_inc(inv_ready, 1)
                    dve.wait_ge(inv_ready, i + 1)
                    for q in range(3):
                        x = prob[:, hh % 4, N_AT[q]:N_AT[q] + (q + 1) * P]
                        m = v_.tensor_scalar(x, x, inv[:, hh % 2, q:q + 1], None, ALU.mult)
                    m.then_inc(prob_dve, 1)

                def take_part(i, hh):
                    dve.wait_ge(head_done, i - 1 + DONE_BASE)
                    dve.wait_ge(turned, i * 2 + 2)
                    v_.tensor_copy(pt[:, hh % 2, BANK:CAUSAL], ps_t[:, BANK:CAUSAL]).then_inc(pt_dve, 1)

                def take_out(n, gg):
                    dve.wait_ge(head_done, n * 8 + gg * 4 + 4 + DONE_BASE)
                    dve.wait_ge(stored[gg], n * 16 + 16)
                    v_.tensor_copy(ot[:, gg, :], ps_o[:, gg, :]).then_inc(o_out, 1)

                def step(n, hh, first=False):
                    i = n * 8 + hh
                    maxima(n, hh)
                    if not first or hh >= 1:
                        normalize(i - 1, (hh - 1) % HU)
                    if not first or hh >= 2:
                        take_part(i - 2, (hh - 2) % HU)
                    if hh == 3 and not first:
                        take_out(n - 1, 1)
                    if hh == 7:
                        take_out(n, 0)
                for hh in range(HU):
                    step(0, hh, first=True)
                with dve.Fori(1, NS) as n:
                    for hh in range(HU):
                        step(n, hh)
                normalize(N_HEADS - 1, 7)
                take_part(N_HEADS - 2, 6)
                take_part(N_HEADS - 1, 7)
                take_out(NS - 1, 1)

            @block.tensor
            def _(pe):
                def scores(n, hh):
                    i, slot = n * 8 + hh, (hh // 2) % 2
                    if hh % 2 == 0:
                        pe.wait_ge(qk_loaded[slot], (n * 2 + hh // 4 + 1) * 128)
                    for bank, tiles in enumerate(S_BANKS):
                        pe.wait_ge(exp_ready, (i - 1) * 3 + bank + 1 + EXP_BASE)
                        for q in tiles:
                            keys = (q + 1) * P
                            nc.tensor.matmul(ps_s[:, S_AT[q]:S_AT[q] + max(keys, WIDE)], qk_sb[:, slot, 0, hh % 2, q * P:keys],
                                             qk_sb[:, slot, 1, hh % 2, 0:max(keys, WIDE)], start=True, stop=True)
                            m = nc.tensor.matmul(ps_s[:, S_AT[q] + q * P:S_AT[q] + keys], ident_b[:], above_b[:], start=False,
                                                 stop=True, skip_group_check=True)
                        m.then_inc(s_ready, 1)

                def transposes(i, hh):
                    pe.wait_ge(prob_act, i + 1)
                    pe.wait_ge(prob_dve, i + 1)
                    for part, (tiles, taken) in enumerate(zip(T_PARTS, (pt_act, pt_dve))):
                        pe.wait_ge(taken, i + PT_BASE)
                        for k in tiles:
                            for q in range(k, QT):
                                at = T_AT[k] + (q - k) * P
                                m = nc.tensor.transpose(ps_t[:, at:at + P],
                                                        prob[:, hh % 4, N_AT[q] + k * P:N_AT[q] + (k + 1) * P], ident[:])
                        m.then_inc(turned, 1)

                def outputs(n, hh):
                    i, j, gg = n * 8 + hh, hh % 4, hh // 4
                    if j == 0:
                        pe.wait_ge(zeros_set, 1)
                        pe.wait_ge(vp_ready, n * 2 + gg + 1)
                        pe.wait_ge(o_out, n * 2 + gg - 1 + O_BASE)
                    pe.wait_ge(pt_act, i + 1 + PT_BASE)
                    pe.wait_ge(pt_dve, i + 1 + PT_BASE)
                    for k in range(QT):
                        m = nc.tensor.matmul(ps_o[:, gg, k * P:SEQ], vp[:, gg, (k * 4 + j) * P:(k * 4 + j + 1) * P],
                                             pt[:, hh % 2, T_AT[k]:T_AT[k] + (QT - k) * P],
                                             start=(j == 0 and k == 0), stop=(j == 3 and k == 3), skip_group_check=True)
                    m.then_inc(head_done, 1)

                def step(n, hh, first=False):
                    i = n * 8 + hh
                    scores(n, hh)
                    if not first or hh >= 2:
                        transposes(i - 2, (hh - 2) % HU)
                    if not first or hh >= 3:
                        outputs(n if hh >= 3 else n - 1, (hh - 3) % HU)
                for hh in range(HU):
                    step(0, hh, first=True)
                with pe.Fori(1, NS) as n:
                    for hh in range(HU):
                        step(n, hh)
                transposes(N_HEADS - 2, 6)
                outputs(NS - 1, 5)
                transposes(N_HEADS - 1, 7)
                outputs(NS - 1, 6)
                outputs(NS - 1, 7)


def make_constants(nc, ident, above, ident_b, above_b):
    with nc.semaphore("const_filled") as filled, nc.semaphore("const_shaped") as shaped, \
            nc.semaphore("const_ready") as ready, nc.Block() as block:
        @block.gpsimd
        def _(pool):
            nc.gpsimd.memset(ident[:], 0.0).then_inc(filled, 1)
            nc.gpsimd.memset(above[:], 0.0).then_inc(filled, 1)
            pool.wait_ge(filled, 2)
            nc.gpsimd.affine_select(out=ident[:], in_=ident[:], compare_op=ALU.not_equal, fill=1.0, base=0,
                                    pattern=[[-1, P]], channel_multiplier=1).then_inc(shaped, 1)
            nc.gpsimd.affine_select(out=above[:], in_=above[:], compare_op=ALU.is_ge, fill=MASKED, base=0,
                                    pattern=[[-1, P]], channel_multiplier=1).then_inc(shaped, 1)

        @block.vector
        def _(dve):
            dve.wait_ge(shaped, 2)
            nc.vector.tensor_copy(ident_b[:], ident[:]).then_inc(ready, 1)
            nc.vector.tensor_copy(above_b[:], above[:]).then_inc(ready, 1)

        @block.tensor
        def _(pe):
            pe.wait_ge(ready, 2)


def ffn_lora(nc, x, weight, bias, lora_b, ident, out):
    N_W, N_Q, N_H = D, EXPERTS * DK, EXPERTS * RANK
    Q_AT, H_AT, K_AT = N_W, N_W + N_Q, N_W + N_Q + N_H
    N_ALL = N_W + 2 * N_Q + N_H
    SCALE = float(1.0 / np.sqrt(np.float64(DK)))
    with ExitStack() as ctx:
        sb = lambda name, shape, dt=F32: ctx.enter_context(nc.sbuf_tensor(f"lora_{name}", shape, dt))
        sem = lambda name: ctx.enter_context(nc.semaphore(f"lora_{name}"))
        w = sb("w", [P, 2, KT, N_ALL], F32R)
        b = sb("b", [P, 2, D], F32R)
        w_raw = sb("w_raw", [P, 2, N_ALL])
        bias_sb = sb("bias", [P, D])
        xn = sb("xn", [P, 2, D])
        xT = sb("xT", [P, 2, 2, KT * P], F32R)
        r = sb("r", [P, 2, D])
        prod = sb("prod", [P, N_Q])
        score = sb("score", [P, EXPERTS])
        small = sb("small", [P, 4])
        expert = sb("expert", [P, EXPERTS])
        h = sb("h", [P, N_H])
        hT = sb("hT", [P, 2, P], F32R)
        ps_y = ctx.enter_context(nc.psum_tensor("lora_ps_y", [P, 2, D], F32))
        ps_qh = ctx.enter_context(nc.psum_tensor("lora_ps_qh", [P, BANK], F32))
        ps_k = ctx.enter_context(nc.psum_tensor("lora_ps_k", [P, BANK], F32))
        ps_x = ctx.enter_context(nc.psum_tensor("lora_ps_x", [P, D], F32))
        ps_h = ps_k[:, N_Q:N_Q + P]
        w_loaded = [sem(f"w_loaded{s}") for s in range(2)]
        w_hi, w_lo = sem("w_hi"), sem("w_lo")
        bias_loaded = sem("bias_loaded")
        x_loaded = [sem(f"x_loaded{s}") for s in range(2)]
        x_turned, x_hi, x_lo = sem("x_turned"), sem("x_hi"), sem("x_lo")
        r_ready, r_seen = sem("r_ready"), sem("r_seen")
        qhk_ready = sem("qhk_ready")
        chain = sem("chain")
        exp_ready = sem("exp_ready")
        weigh = sem("weigh")
        h_turned, h_hi, h_lo = sem("h_turned"), sem("h_hi"), sem("h_lo")
        y_ready, sum_ready = sem("y_ready"), sem("sum_ready")
        stored = [sem(f"stored{s}") for s in range(2)]
        ln = LayerNorm(nc, ctx, "lora_ln", sum_ready, in_place=True)
        X_BASE = 2

        with nc.Block() as block:
            @block.sync
            def _(sp):
                def load_x(n, s):
                    sp.dma_start(xn[:, s, :], one(x[bass.ds(n, 1)])).then_inc(x_loaded[s], 16)
                for s in range(2):
                    load_x(s, s)
                    sp.dma_start(w_raw[:, s, :], weight[s]).then_inc(w_loaded[s], 16)
                sp.dma_start(bias_sb[:], bias.to_broadcast([P, D])).then_inc(bias_loaded, 16)
                for kt in range(2, KT + 1):
                    sp.wait_ge(w_lo, kt - 1)
                    if kt < KT:
                        sp.dma_start(w_raw[:, kt % 2, :], weight[kt]).then_inc(w_loaded[kt % 2], 16)
                    else:
                        sp.dma_start(w_raw[:, kt % 2, 0:D], lora_b).then_inc(w_loaded[kt % 2], 16)

                def tile(n, s, store=True):
                    sp.wait_ge(x_turned, n - 1)
                    sp.wait_ge(r_ready, n - 1)
                    load_x(n, s)
                    sp.wait_ge(ln.x_ready, n - 1 + X_BASE)
                    sp.dma_start(one(out[bass.ds(n - 2, 1)]), r[:, s, :]).then_inc(stored[s], 16)
                with sp.Fori(1, TILES // 2) as j:
                    for s in range(2):
                        tile(j * 2 + s, s)
                for s in range(2):
                    sp.wait_ge(ln.x_ready, TILES - 1 + s + X_BASE)
                    sp.dma_start(out[TILES - 2 + s], r[:, s, :]).then_inc(stored[s], 16)
                for s in range(2):
                    sp.wait_ge(stored[s], 16 * (TILES // 2 + 1))

            @block.gpsimd
            def _(pool):
                for s in range(2):
                    pool.sem_inc(stored[s], 16)
                pool.wait_ge(bias_loaded, 16)
                with pool.Fori(0, TILES // 2) as j:
                    for s in range(2):
                        pool.wait_ge(x_loaded[s], j * 16 + 16)
                        pool.wait_ge(stored[s], j * 16 + 16)
                        pool.sem_inc(r_seen, 1)
                        nc.gpsimd.tensor_tensor(r[:, s, :], xn[:, s, :], bias_sb[:], ALU.add).then_inc(r_ready, 1)

            @block.scalar
            def _(act):
                a = nc.scalar
                act.sem_inc(ln.x_ready, X_BASE)
                for kt in range(KT + 1):
                    act.wait_ge(w_loaded[kt % 2], (kt // 2 + 1) * 16)
                    if kt < KT:
                        a.copy(w[:, HI, kt, :], w_raw[:, kt % 2, :]).then_inc(w_hi, 1)
                    else:
                        a.copy(b[:, HI, :], w_raw[:, kt % 2, 0:D]).then_inc(w_hi, 1)

                def split_x(n, s):
                    act.wait_ge(x_turned, n + 1)
                    a.copy(xT[:, s, HI, :], ps_x[:]).then_inc(x_hi, 1)

                def tile(n, s, more=True):
                    if more:
                        split_x(n + 1, 1 - s)
                    act.wait_ge(chain, n * 4 + 4)
                    a.activation(expert[:], score[:], ACT.Exp, bias=small[:, 1:2], scale=SCALE,
                                 accum_out=small[:, 2:3]).then_inc(exp_ready, 1)
                    act.wait_ge(h_turned, n + 1)
                    a.copy(hT[:, HI, :], ps_h).then_inc(h_hi, 1)
                    ln.scalar(act, n, s, r[:, s, :])
                split_x(0, 0)
                with act.Fori(0, TILES // 2 - 1) as j:
                    for s in range(2):
                        tile(j * 2 + s, s)
                tile(TILES - 2, 0)
                tile(TILES - 1, 1, more=False)

            @block.vector
            def _(dve):
                v = nc.vector
                dve.sem_inc(sum_ready, SLOTS)
                for kt in range(KT + 1):
                    dve.wait_ge(w_hi, kt + 1)
                    if kt < KT:
                        v.tensor_tensor(w[:, LO, kt, :], w_raw[:, kt % 2, :], w[:, HI, kt, :].bitcast(F32),
                                        ALU.subtract).then_inc(w_lo, 1)
                    else:
                        v.tensor_tensor(b[:, LO, :], w_raw[:, kt % 2, 0:D], b[:, HI, :].bitcast(F32),
                                        ALU.subtract).then_inc(w_lo, 1)

                def split_x(n, s):
                    dve.wait_ge(x_hi, n + 1)
                    v.tensor_tensor(xT[:, s, LO, :], ps_x[:], xT[:, s, HI, :].bitcast(F32), ALU.subtract).then_inc(x_lo, 1)

                def tile(n, s, more=True):
                    dve.wait_ge(qhk_ready, n + 1)
                    v.tensor_copy(prod[:], ps_k[:, 0:N_Q]).then_inc(chain, 1)
                    dve.wait_ge(chain, n * 4 + 1)
                    v.tensor_tensor(prod[:], ps_qh[:, 0:N_Q], prod[:], ALU.mult).then_inc(chain, 1)
                    dve.wait_ge(chain, n * 4 + 2)
                    v.reduce_sum(score[:], prod[:].rearrange("p (e d) -> p e d", e=EXPERTS), AX.X).then_inc(chain, 1)
                    dve.wait_ge(chain, n * 4 + 3)
                    v.reduce_max(small[:, 0:1], score[:], AX.X, negate=True).then_inc(weigh, 1)
                    dve.wait_ge(weigh, n * 4 + 1)
                    v.tensor_scalar(small[:, 1:2], small[:, 0:1], SCALE, None, ALU.mult).then_inc(chain, 1)
                    if more:
                        split_x(n + 1, 1 - s)
                    dve.wait_ge(exp_ready, n + 1)
                    v.reciprocal(small[:, 3:4], small[:, 2:3]).then_inc(weigh, 1)
                    dve.wait_ge(weigh, n * 4 + 2)
                    v.tensor_scalar(expert[:], expert[:], small[:, 3:4], None, ALU.mult).then_inc(weigh, 1)
                    dve.wait_ge(weigh, n * 4 + 3)
                    v.tensor_tensor(h[:].rearrange("p (e r) -> p e r", e=EXPERTS),
                                    ps_qh[:, N_Q:N_Q + N_H].rearrange("p (e r) -> p e r", e=EXPERTS),
                                    expert[:].unsqueeze(2).to_broadcast([P, EXPERTS, RANK]), ALU.mult).then_inc(weigh, 1)
                    dve.wait_ge(h_hi, n + 1)
                    v.tensor_tensor(hT[:, LO, :], ps_h, hT[:, HI, :].bitcast(F32), ALU.subtract).then_inc(h_lo, 1)
                    dve.wait_ge(r_ready, n + 1)
                    dve.wait_ge(y_ready, n + 1)
                    v.tensor_tensor(r[:, s, :], ps_y[:, s, :], r[:, s, :], ALU.add).then_inc(sum_ready, 1)
                    ln.vector(dve, n, s, r[:, s, :])
                split_x(0, 0)
                with dve.Fori(0, TILES // 2 - 1) as j:
                    for s in range(2):
                        tile(j * 2 + s, s)
                tile(TILES - 2, 0)
                tile(TILES - 1, 1, more=False)

            @block.tensor
            def _(pe):
                def transposes(s, loads):
                    pe.wait_ge(x_loaded[s], loads * 16)
                    for kt in range(KT):
                        m = nc.tensor.transpose(ps_x[:, kt * P:(kt + 1) * P], xn[:, s, kt * P:(kt + 1) * P], ident[:])
                    m.then_inc(x_turned, 1)

                def product(into, s, at, width, stop=True):
                    for kt in range(KT):
                        for wa, wb in PASSES:
                            m = nc.tensor.matmul(into, xT[:, s, wa, kt * P:(kt + 1) * P], w[:, wb, kt, at:at + width],
                                                 start=(kt == 0 and (wa, wb) == PASSES[0]),
                                                 stop=(stop and kt == KT - 1 and (wa, wb) == PASSES[-1]))
                    return m

                def tile(n, s, loads, more=True):
                    pe.wait_ge(x_lo, n + 1)
                    product(ps_qh[:, 0:N_Q + N_H], s, Q_AT, N_Q + N_H)
                    product(ps_k[:, 0:N_Q], s, K_AT, N_Q).then_inc(qhk_ready, 1)
                    if more:
                        transposes(1 - s, loads)
                    pe.wait_ge(sum_ready, n + 1)
                    product(ps_y[:, s, 0:BANK], s, 0, BANK, stop=False)
                    pe.wait_ge(weigh, n * 4 + 4)
                    nc.tensor.transpose(ps_h, h[:], ident[:]).then_inc(h_turned, 1)
                    product(ps_y[:, s, BANK:D], s, BANK, BANK, stop=False)
                    pe.wait_ge(h_lo, n + 1)
                    for half in range(2):
                        for wa, wb in PASSES:
                            m = nc.tensor.matmul(ps_y[:, s, half * BANK:(half + 1) * BANK], hT[:, wa, :],
                                                 b[:, wb, half * BANK:(half + 1) * BANK], start=False,
                                                 stop=(wa, wb) == PASSES[-1])
                    m.then_inc(y_ready, 1)
                transposes(0, 1)
                pe.wait_ge(w_lo, KT + 1)
                with pe.Fori(0, TILES // 2 - 1) as j:
                    tile(j * 2, 0, j + 1)
                    tile(j * 2 + 1, 1, j + 2)
                tile(TILES - 2, 0, TILES // 2)
                tile(TILES - 1, 1, None, more=False)


def build(nc, x, x_turned, attn_w, attn_mask, codes, scales, qk_w, v_w, tables, o_w, lora_w, bias, lora_b, out):
    dram = lambda name, *shape: nc.dram_tensor(f"between_{name}", shape, F32, kind="Internal").ap()
    x1, x2, x3 = (dram(f"x{i}", TILES, P, D) for i in (1, 2, 3))
    down_w = dram("down_w", CH, P, D)
    inter = dram("inter", CH, BATCH, P, SEQ)
    qk = dram("qk", 2 * QK_GROUPS, BATCH, 8, 2, 2, HD // 2, SEQ)
    v = dram("v", QK_GROUPS, BATCH, SEQ // P, P, 2 * P)
    heads = dram("heads", QK_GROUPS, TILES, P, 2 * P)
    with ExitStack() as ctx:
        sb = lambda name, dt: ctx.enter_context(nc.sbuf_tensor(name, [P, P], dt))
        ident, above = sb("ident", F32), sb("above", F32)
        ident_b, above_b = sb("ident_b", BF16), sb("above_b", BF16)
        make_constants(nc, ident, above, ident_b, above_b)
        linear_ln(nc, "l0", x_turned, attn_w, x, x1, attn_mask)
        with nc.sbuf_tensor("xT1", [P, 2, KT, T], F32R) as xT:
            transpose_tokens(nc, "t1", x1, xT, ident)
            ffn_up(nc, xT, codes, scales, down_w, inter)
        ffn_down(nc, inter, down_w, x1, x2)
        with nc.sbuf_tensor("xT2", [P, 2, KT, T], F32R) as xT:
            transpose_tokens(nc, "t2", x2, xT, ident)
            project_qk(nc, xT, qk_w, tables, qk)
            project_v(nc, xT, v_w, v)
        attention(nc, ident, ident_b, above_b,
                  qk.rearrange("(m u) b h c a j t -> m (u b) h c (a j) t", m=2),
                  v.rearrange("u b k p i -> (u b) k p i"),
                  heads.rearrange("u t p i -> (u t) p i"))
        linear_ln(nc, "l1", heads.rearrange("u n p i -> n p u i"), o_w, x2, x3)
        ffn_lora(nc, x3, lora_w, bias, lora_b, ident, out)


def kernel(L0_attn_data, L0_attn_weight, L0_attn_mask, L0_ffn_gate_codes, L0_ffn_gate_scales, L0_ffn_up_codes,
           L0_ffn_up_scales, L0_ffn_down_codes, L0_ffn_down_scales, L1_attn_wq, L1_attn_wk, L1_attn_wv, L1_attn_wo,
           L1_ffn_W, L1_ffn_b, L1_ffn_Wq, L1_ffn_Wk, L1_ffn_A, L1_ffn_Bm):
    import concourse.bacc as bacc
    from concourse.bass_utils import run_bass_kernel_spmd

    x = np.asarray(L0_attn_data)
    pad = CH * P - I_FFN
    arrays = {}

    def put(name, array):
        arrays[name] = np.ascontiguousarray(array)

    put("x", x.reshape(TILES, P, D))
    put("x_turned", x.reshape(TILES, P, KT, P).transpose(0, 3, 2, 1))
    put("attn_w", np.asarray(L0_attn_weight).T.reshape(KT, P, D))
    put("attn_mask", np.asarray(L0_attn_mask).T.reshape(KT, P, D))

    def up_codes(a):
        a = np.pad(np.asarray(a), ((0, pad), (0, 0)), constant_values=NF4_ZERO)
        return a.reshape(CH, P, KT, P).transpose(0, 3, 2, 1).reshape(CH, P, KT * P)

    def up_scales(a):
        a = np.pad(np.asarray(a), ((0, pad), (0, 0)))
        return a.reshape(CH, P, KT, P // NF4_BLOCK).transpose(0, 3, 2, 1)

    put("gate_codes", up_codes(L0_ffn_gate_codes))
    put("up_codes", up_codes(L0_ffn_up_codes))
    put("down_codes", np.pad(np.asarray(L0_ffn_down_codes).T, ((0, pad), (0, 0)),
                             constant_values=NF4_ZERO).reshape(CH, P, D))
    put("gate_scales", up_scales(L0_ffn_gate_scales))
    put("up_scales", up_scales(L0_ffn_up_scales))
    put("down_scales", np.pad(np.asarray(L0_ffn_down_scales).T,
                              ((0, pad // NF4_BLOCK), (0, 0))).reshape(CH, P // NF4_BLOCK, D))

    def rotary_weight(a):
        a = np.asarray(a).reshape(KT, P, QK_GROUPS, 8, HD // 2, 2)
        return a.transpose(2, 1, 0, 5, 3, 4).reshape(QK_GROUPS, P, KT * 2 * P)

    put("qk_w", np.concatenate([rotary_weight(L1_attn_wq), rotary_weight(L1_attn_wk)]))
    put("v_w", np.asarray(L1_attn_wv).reshape(KT, P, 2, BANK).transpose(2, 1, 0, 3).reshape(2, P, KT * BANK))
    frequency = 1.0 / 10000.0 ** (np.arange(0, HD, 2)[:HD // 2].astype(np.float32) / HD)
    angle = np.outer(np.arange(SEQ), frequency).astype(np.float32)
    k_tables = np.stack([np.tile(f(angle).T, (8, 1)) for f in (np.cos, np.sin)])
    put("tables", np.stack([k_tables * (np.float32(1.0) / np.sqrt(np.float32(HD))), k_tables]).astype(np.float32))
    put("o_w", np.asarray(L1_attn_wo).reshape(KT, P, D))

    lora_a = np.asarray(L1_ffn_A).reshape(EXPERTS * RANK, D)
    put("lora_w", np.concatenate([np.asarray(a).T for a in (L1_ffn_W, L1_ffn_Wq, lora_a, L1_ffn_Wk)],
                                 axis=1).reshape(KT, P, -1))
    put("bias", np.asarray(L1_ffn_b).reshape(1, D))
    put("lora_b", np.asarray(L1_ffn_Bm).transpose(0, 2, 1).reshape(EXPERTS * RANK, D))

    nc = bacc.Bacc("TRN2", target_bir_lowering=False, num_devices=1, dynamic_dma_scratch_size=1024)
    ap = {name: nc.dram_tensor(f"in_{name}", a.shape, mybir.dt.from_np(a.dtype), kind="ExternalInput").ap()
          for name, a in arrays.items()}
    out = nc.dram_tensor("out", (TILES, P, D), F32, kind="ExternalOutput").ap()
    build(nc, ap["x"], ap["x_turned"], ap["attn_w"], ap["attn_mask"],
          (ap["gate_codes"], ap["up_codes"], ap["down_codes"]),
          (ap["gate_scales"], ap["up_scales"], ap["down_scales"]),
          ap["qk_w"], ap["v_w"], ap["tables"], ap["o_w"], ap["lora_w"], ap["bias"], ap["lora_b"], out)
    result = run_bass_kernel_spmd(nc, [{f"in_{name}": a for name, a in arrays.items()}], core_ids=[0])
    return result.results[0]["out"].reshape(x.shape)
```

```python
import numpy as np
import concourse.bass as bass
from concourse import mybir
from contextlib import ExitStack

F32 = mybir.dt.float32
F32R = mybir.dt.float32r
I32 = mybir.dt.int32
BF16 = mybir.dt.bfloat16
ALU = mybir.AluOpType
ACT = mybir.ActivationFunctionType
AX = mybir.AxisListType

P = 128
T, D = 2048, 1024
BATCH, SEQ = 4, 512
TILES = T // P
KT = D // P
BANK = 512
BLK = 32
I_FFN = 2752
CH = -(-I_FFN // P)
NF4_BLOCK = 64
HEADS, HD = 32, 32
GROUPS = 8
QK_GROUPS = 4
EXPERTS, DK, RANK = 8, 32, 16
EPS = 1e-5
SLOTS = 2
MASKED = -1e30

HI, LO = 0, 1
PASSES = ((LO, HI), (HI, LO), (HI, HI))


def one(ap):
    return ap.rearrange("a p n -> p (a n)")


class LayerNorm:

    STEPS = 15

    def __init__(self, nc, ctx, tag, sum_ready, seen, base=SLOTS, slots=2, in_place=False):
        sb = lambda name, shape, dt=F32: ctx.enter_context(nc.sbuf_tensor(f"{tag}_{name}", shape, dt))
        sem = lambda name: ctx.enter_context(nc.semaphore(f"{tag}_{name}"))
        self.nc = nc
        self.x = None if in_place else sb("x", [P, slots, D])
        self.stats = sb("stats", [P, slots, 2, 6])
        self.mv = sb("mv", [P, slots, 2])
        self.small = sb("small", [P, slots, 8])
        self.sum_ready, self.base = sum_ready, base
        self.steps = sem("steps")
        self.seen = seen
        self.x_ready = sem("x_ready")

    def vector(self, dve, n, s, r):
        v, sm, mv, steps, at = self.nc.vector, self.small[:, s, :], self.mv[:, s, :], self.steps, n * self.STEPS
        dve.wait_ge(self.sum_ready, n + self.base + 1)
        v.bn_stats(self.stats[:, s, 0, :], r[:, 0:BANK])
        v.bn_stats(self.stats[:, s, 1, :], r[:, BANK:D]).then_inc(steps, 1)
        dve.wait_ge(steps, at + 1)
        dve.sem_inc(self.seen, 1)
        v.bn_aggr(mv, self.stats[:, s, :, :].rearrange("p a b -> p (a b)")).then_inc(steps, 1)
        dve.wait_ge(steps, at + 2)
        ve, half, y, t = sm[:, 0:1], sm[:, 1:2], sm[:, 2:3], sm[:, 3:4]
        v.tensor_scalar(ve, mv[:, 1:2], EPS, None, ALU.add).then_inc(steps, 1)
        dve.wait_ge(steps, at + 3)
        v.tensor_scalar(half.bitcast(I32), ve.bitcast(I32), 1, None, ALU.logical_shift_right).then_inc(steps, 1)
        dve.wait_ge(steps, at + 4)
        v.tensor_scalar(y.bitcast(I32), half.bitcast(I32), -1.0, float(0x5F3759DF), ALU.mult, ALU.add).then_inc(steps, 1)
        for k in range(3):
            done = at + 3 * k + 5
            dve.wait_ge(steps, done)
            v.scalar_tensor_tensor(t, ve, -0.5, y, ALU.mult, ALU.mult).then_inc(steps, 1)
            dve.wait_ge(steps, done + 1)
            v.tensor_tensor(t, t, y, ALU.mult).then_inc(steps, 1)
            dve.wait_ge(steps, done + 2)
            v.scalar_tensor_tensor(y, t, 1.5, y, ALU.add, ALU.mult).then_inc(steps, 1)
        dve.wait_ge(steps, at + 14)
        v.scalar_tensor_tensor(sm[:, 4:5], mv[:, 0:1], -1.0, y, ALU.mult, ALU.mult).then_inc(steps, 1)

    def scalar(self, act, n, s, r, x_free=None, free_at=0):
        a, sm = self.nc.scalar, self.small[:, s, :]
        act.wait_ge(self.steps, (n + 1) * self.STEPS)
        if x_free is not None:
            act.wait_ge(x_free, free_at)
        a.activation(r if self.x is None else self.x[:, s, :], r, ACT.Identity, bias=sm[:, 4:5], scale=sm[:, 2:3]).then_inc(self.x_ready, 1)


class WeightSplit:

    def __init__(self, nc, ctx, tag, weight, w):
        sem = lambda name: ctx.enter_context(nc.semaphore(f"{tag}_{name}"))
        self.nc, self.weight, self.w = nc, weight, w
        self.raw = ctx.enter_context(nc.sbuf_tensor(f"{tag}_raw", [P, weight.shape[2]], F32))
        self.loaded, self.hi_ready, self.lo_ready = sem("loaded"), sem("hi_ready"), sem("lo_ready")

    def part(self, comp, k):
        return self.w[:, comp, bass.ds(k, 1), :].rearrange("p a n -> p (a n)")

    def sync(self, sp, k, first=False):
        if not first:
            sp.wait_ge(self.lo_ready, k)
        sp.dma_start(self.raw[:], one(self.weight[bass.ds(k, 1)])).then_inc(self.loaded, 16)

    def scalar(self, act, k):
        act.wait_ge(self.loaded, k * 16 + 16)
        self.nc.scalar.copy(self.part(HI, k), self.raw[:]).then_inc(self.hi_ready, 1)

    def vector(self, dve, k):
        dve.wait_ge(self.hi_ready, k + 1)
        self.nc.vector.tensor_tensor(self.part(LO, k), self.raw[:], self.part(HI, k).bitcast(F32),
                                     ALU.subtract).then_inc(self.lo_ready, 1)


def linear_ln(nc, tag, acts, resid, out, seen, weight=None, mask=None, w=None, side=None):
    with ExitStack() as ctx:
        sb = lambda name, shape, dt=F32: ctx.enter_context(nc.sbuf_tensor(f"{tag}_{name}", shape, dt))
        sem = lambda name: ctx.enter_context(nc.semaphore(f"{tag}_{name}"))
        a_raw = sb("a_raw", [P, 2, KT * P])
        a = sb("a", [P, 2, 2, KT * P], F32R)
        r = sb("r", [P, 2, D])
        ps = ctx.enter_context(nc.psum_tensor(f"{tag}_ps", [P, 2, D], F32))
        RAW = 4
        if mask is not None:
            w = sb("w", [P, 2, KT, D], F32R)
            w_raw = sb("w_raw", [P, RAW, D])
            m_raw = sb("m_raw", [P, RAW, D], I32)
            m_sum = sb("m_sum", [P, 2, BLK])
            m_one = sb("m_one", [P, 2, BLK])
            same = sb("same", [P, P])
            pm = ctx.enter_context(nc.psum_tensor(f"{tag}_pm", [P, 2, BANK], F32))
            w_loaded = [sem(f"w_loaded{s}") for s in range(RAW)]
            w_hi, w_lo = sem("w_hi"), sem("w_lo")
            w_masked = sem("w_masked")
            same_ready, sums_ready, blocks_ready, ones_ready = (
                sem(x) for x in ("same_ready", "sums_ready", "blocks_ready", "ones_ready"))
        a_loaded = [sem(f"a_loaded{s}") for s in range(2)]
        r_loaded = [sem(f"r_loaded{s}") for s in range(2)]
        a_hi, a_lo = sem("a_hi"), sem("a_lo")
        y_ready = sem("y_ready")
        sum_ready = sem("sum_ready")
        stored = [sem(f"stored{s}") for s in range(2)]
        ln = LayerNorm(nc, ctx, f"{tag}_ln", sum_ready, seen, in_place=side is not None)
        X = r if side is not None else ln.x

        acts_tile = lambda n: acts[bass.ds(n, 1)].rearrange("a p u i -> (a p) u i")
        a_view = lambda s: a_raw[:, s, :].rearrange("p (u i) -> p u i", u=acts.shape[2])

        with nc.Block() as block:
            @block.sync
            def _(sp):
                sp.sem_inc(stored[0], 16)
                sp.sem_inc(stored[1], 16)

                def load_w(k):
                    sp.dma_start(m_raw[:, k % RAW, :], mask[k]).then_inc(w_loaded[k % RAW], 16)
                    sp.dma_start(w_raw[:, k % RAW, :], weight[k]).then_inc(w_loaded[k % RAW], 16)

                for s in range(2):
                    if mask is not None:
                        load_w(s)
                    sp.dma_start(a_view(s), acts_tile(s)).then_inc(a_loaded[s], 16)
                if mask is not None:
                    for k in range(2, KT):
                        if k >= RAW:
                            sp.wait_ge(w_lo, k - RAW + 1)
                        load_w(k)
                if side is not None:
                    side.sync(sp, 0, first=True)
                for s in range(2):
                    sp.dma_start(r[:, s, :], resid[s]).then_inc(r_loaded[s], 16)

                def load_acts(n, s):
                    sp.wait_ge(a_lo, n - 1)
                    sp.dma_start(a_view(s), acts_tile(n)).then_inc(a_loaded[s], 16)

                def next_tile(n, s, stores):
                    sp.wait_ge(ln.x_ready, n - 1)
                    sp.dma_start(one(out[bass.ds(n - 2, 1)]), X[:, s, :]).then_inc(stored[s], 16)
                    if side is not None:
                        sp.wait_ge(stored[s], stores * 16 + 16)
                    sp.dma_start(r[:, s, :], one(resid[bass.ds(n, 1)])).then_inc(r_loaded[s], 16)

                load_acts(2, 0)
                with sp.Fori(1, TILES // 2 - 1) as j:
                    if side is not None:
                        side.sync(sp, j)
                    load_acts(j * 2 + 1, 1)
                    next_tile(j * 2, 0, j)
                    load_acts(j * 2 + 2, 0)
                    next_tile(j * 2 + 1, 1, j)
                if side is not None:
                    side.sync(sp, KT - 1)
                load_acts(TILES - 1, 1)
                next_tile(TILES - 2, 0, TILES // 2 - 1)
                next_tile(TILES - 1, 1, TILES // 2 - 1)
                for s in range(2):
                    sp.wait_ge(ln.x_ready, TILES - 1 + s)
                    sp.dma_start(out[TILES - 2 + s], X[:, s, :]).then_inc(stored[s], 16)
                for s in range(2):
                    sp.wait_ge(stored[s], 16 * (TILES // 2 + 1))

            @block.scalar
            def _(act):
                def split_hi(n, s, loads):
                    act.wait_ge(a_loaded[s], loads * 16)
                    act.wait_ge(y_ready, n + 1)
                    nc.scalar.copy(a[:, s, HI, :], a_raw[:, s, :]).then_inc(a_hi, 1)

                split_hi(0, 0, 1)
                split_hi(1, 1, 1)
                if mask is not None:
                    for k in range(KT):
                        act.wait_ge(w_masked, k + 1)
                        nc.scalar.copy(w[:, HI, k, :], w_raw[:, k % RAW, :]).then_inc(w_hi, 1)
                with act.Fori(0, TILES // 2 - 1) as j:
                    if side is not None:
                        side.scalar(act, j)
                    for s in range(2):
                        split_hi(j * 2 + 2 + s, s, j + 2)
                        ln.scalar(act, j * 2 + s, s, r[:, s, :], stored[s], j * 16 + 16)
                if side is not None:
                    side.scalar(act, KT - 1)
                for s in range(2):
                    ln.scalar(act, TILES - 2 + s, s, r[:, s, :], stored[s], TILES // 2 * 16)

            @block.vector
            def _(dve):
                v = nc.vector
                dve.sem_inc(sum_ready, SLOTS)
                if mask is not None:
                    v.memset(same[:], 0.0).then_inc(same_ready, 1)
                    dve.wait_ge(same_ready, 1)
                    for b in range(P // BLK):
                        v.memset(same[b * BLK:(b + 1) * BLK, b * BLK:(b + 1) * BLK], 1.0).then_inc(same_ready, 1)

                def mask_sums(k):
                    dve.wait_ge(w_loaded[k % RAW], (k // RAW + 1) * 32)
                    v.reduce_sum(m_sum[:, k % 2, :], m_raw[:, k % RAW, :].rearrange("p (b c) -> p b c", c=BLK),
                                 AX.X).then_inc(sums_ready, 1)

                def mask_weight(k):
                    dve.wait_ge(blocks_ready, k + 1)
                    v.tensor_scalar(m_one[:, k % 2, :], pm[:, k % 2, 0:BLK], 0.0, None, ALU.is_gt).then_inc(ones_ready, 1)
                    dve.wait_ge(ones_ready, k + 1)
                    w3 = w_raw[:, k % RAW, :].rearrange("p (b c) -> p b c", c=BLK)
                    v.tensor_tensor(w3, w3, m_one[:, k % 2, :].unsqueeze(2).to_broadcast([P, BLK, BLK]),
                                    ALU.mult).then_inc(w_masked, 1)

                def weight_lo(k):
                    dve.wait_ge(w_hi, k + 1)
                    v.tensor_tensor(w[:, LO, k, :], w_raw[:, k % RAW, :], w[:, HI, k, :].bitcast(F32),
                                    ALU.subtract).then_inc(w_lo, 1)

                def split_lo(n, s):
                    dve.wait_ge(a_hi, n + 1)
                    v.tensor_tensor(a[:, s, LO, :], a_raw[:, s, :], a[:, s, HI, :].bitcast(F32),
                                    ALU.subtract).then_inc(a_lo, 1)

                def finish(n, s, loads):
                    dve.wait_ge(r_loaded[s], loads * 16)
                    dve.wait_ge(y_ready, n + SLOTS + 1)
                    v.tensor_tensor(r[:, s, :], ps[:, s, :], r[:, s, :], ALU.add).then_inc(sum_ready, 1)
                    ln.vector(dve, n, s, r[:, s, :])

                if mask is not None:
                    mask_sums(0)
                split_lo(0, 0)
                split_lo(1, 1)
                if mask is not None:
                    for k in range(KT):
                        if k + 1 < KT:
                            mask_sums(k + 1)
                        mask_weight(k)
                        if k:
                            weight_lo(k - 1)
                    weight_lo(KT - 1)
                with dve.Fori(0, TILES // 2 - 1) as j:
                    if side is not None:
                        side.vector(dve, j)
                    for s in range(2):
                        split_lo(j * 2 + 2 + s, s)
                        finish(j * 2 + s, s, j + 1)
                if side is not None:
                    side.vector(dve, KT - 1)
                for s in range(2):
                    finish(TILES - 2 + s, s, TILES // 2)

            @block.tensor
            def _(pe):
                pe.sem_inc(y_ready, SLOTS)

                def block_sums(k):
                    pe.wait_ge(sums_ready, k + 1)
                    nc.tensor.matmul(pm[:, k % 2, 0:BLK], same[:], m_sum[:, k % 2, :], start=True, stop=True).then_inc(blocks_ready, 1)

                def products(s, h, kt):
                    for wa, wb in PASSES:
                        mm = nc.tensor.matmul(ps[:, s, h * BANK:(h + 1) * BANK], a[:, s, wa, kt * P:(kt + 1) * P],
                                              w[:, wb, kt, h * BANK:(h + 1) * BANK],
                                              start=(kt == 0 and (wa, wb) == PASSES[0]),
                                              stop=(kt == KT - 1 and (wa, wb) == PASSES[-1]))
                    return mm

                def tile(n, s):
                    pe.wait_ge(a_lo, n + 1)
                    pe.wait_ge(sum_ready, n + 1)
                    for h in range(2):
                        for kt in range(KT):
                            mm = products(s, h, kt)
                    mm.then_inc(y_ready, 1)

                if mask is not None:
                    pe.wait_ge(same_ready, 1 + P // BLK)
                    block_sums(0)
                    block_sums(1)
                    pe.wait_ge(a_lo, 2)
                    for kt in range(KT):
                        if kt + 2 < KT:
                            block_sums(kt + 2)
                        pe.wait_ge(w_lo, kt + 1)
                        for s in range(2):
                            for h in range(2):
                                mm = products(s, h, kt)
                            if kt == KT - 1:
                                mm.then_inc(y_ready, 1)
                else:
                    for s in range(2):
                        tile(s, s)
                with pe.Fori(1, TILES // 2) as j:
                    for s in range(2):
                        tile(j * 2 + s, s)


NF4 = np.array([-1.0, -0.6961928009986877, -0.5250730514526367, -0.39491748809814453, -0.28444138169288635,
                -0.18477343022833334, -0.09105003625154495, 0.0, 0.07958029955625534, 0.16093020141124725,
                0.24611230194568634, 0.33791524171829224, 0.44070982933044434, 0.5626170039176941,
                0.7229568362236023, 1.0], np.float32)
NF4_ZERO = 7


def nf4_lines():
    def line(code, sign, values):
        x0 = code - NF4_ZERO
        slope = np.float64(values[1]) - np.float64(values[0])
        best = None
        for i in range(-64, 65):
            scale = np.float32(slope + i * np.float64(np.spacing(np.float32(slope))))
            for k in range(-8, 9):
                shift = np.float32(np.float64(values[0]) - np.float64(scale) * x0)
                shift = np.float32(shift + k * np.float64(np.spacing(shift)))
                got = [np.float32(np.float64(scale) * (x0 + n) + np.float64(shift)) for n in range(2)]
                miss = sum(abs(np.float64(g) - np.float64(v)) for g, v in zip(got, values))
                if best is None or miss < best[0]:
                    best = (miss, float(scale), float(shift))
        return best[1:]
    above = [line(c, 1, NF4[c:c + 2]) for c in (14, 12, 10, 8)]
    below = [line(c, -1, -NF4[c:c + 2]) for c in (0, 2, 4)]
    below.append(line(6, -1, [-NF4[6], np.float32(-1e-3)]))
    x = np.arange(16) - NF4_ZERO
    value = lambda lines: np.max([[np.float32(np.float64(np.float32(a)) * v + np.float64(np.float32(b))) for v in x]
                                  for a, b in lines] + [np.zeros(16)], axis=0)
    assert np.array_equal(np.float32(value(above)) - np.float32(value(below)), NF4)
    return above, below


class TokenTranspose:
    PAIRS = TILES // 2

    def __init__(self, nc, ctx, tag, x, xT, ident, xn, ps):
        sem = lambda name: ctx.enter_context(nc.semaphore(f"{tag}_{name}"))
        self.nc, self.x, self.xT, self.ident, self.xn, self.ps = nc, x, xT, ident, xn, ps
        self.loaded = [sem(f"x_loaded{s}") for s in range(2)]
        self.turned, self.hi_ready, self.lo_ready = sem("turned"), sem("hi_ready"), sem("lo_ready")

    def psum(self, s):
        return self.ps[s].rearrange("p m (k t) -> p m k t", t=P)

    def part(self, comp, n):
        return self.xT[:, comp, :, bass.ds(n * P, P)].rearrange("p (m k) t -> p m k t", m=2)

    def sync(self, sp, start, end):
        def load(j, slot):
            for s in range(2):
                sp.dma_start(self.xn[2 * slot + s], one(self.x[bass.ds(j * 2 + s, 1)])).then_inc(self.loaded[slot], 16)
        if start == 0:
            load(0, 0)
            load(1, 1)
        with sp.Fori(max(start // 2, 1), end // 2) as i:
            for slot in range(2):
                sp.wait_ge(self.turned, i * 4 + 2 * slot - 2)
                load(i * 2 + slot, slot)

    def tensor(self, pe, start, end):
        with pe.Fori(start // 2, end // 2) as i:
            for slot in range(2):
                pe.wait_ge(self.loaded[slot], i * 32 + 32)
                for s in range(2):
                    pe.wait_ge(self.lo_ready, i * 4 + 2 * slot + s + 1)
                    for kt in range(KT):
                        mm = self.nc.tensor.transpose(self.ps[s][:, kt // 4, kt % 4 * P:(kt % 4 + 1) * P],
                                                      self.xn[2 * slot + s][:, kt * P:(kt + 1) * P], self.ident[:])
                    mm.then_inc(self.turned, 1)

    def scalar(self, act, start, end):
        with act.Fori(start, end) as j:
            for s in range(2):
                act.wait_ge(self.turned, j * 2 + s + 1)
                self.nc.scalar.copy(self.part(HI, j * 2 + s), self.psum(s)).then_inc(self.hi_ready, 1)

    def vector(self, dve, start, end):
        if start == 0:
            dve.sem_inc(self.lo_ready, SLOTS)
        with dve.Fori(start, end) as j:
            for s in range(2):
                dve.wait_ge(self.hi_ready, j * 2 + s + 1)
                self.nc.vector.tensor_tensor(self.part(LO, j * 2 + s), self.psum(s),
                                             self.part(HI, j * 2 + s).bitcast(F32), ALU.subtract).then_inc(self.lo_ready, 1)


GATE, UP, DOWN = range(3)


def ffn_up(nc, x, ident, codes, scales, down_w, inter):
    with ExitStack() as ctx:
        sb = lambda name, shape, dt=F32: ctx.enter_context(nc.sbuf_tensor(f"up_{name}", shape, dt))
        sem = lambda name: ctx.enter_context(nc.semaphore(f"up_{name}"))
        xT = sb("xT", [P, 2, KT, T], F32R)
        code = sb("code", [P, 2, D], I32)
        scale = sb("scale", [P, 2, D])
        line = sb("line", [P, 3, D])
        above, below = sb("above", [P, D]), sb("below", [P, D])
        w = sb("w", [P, 2, 2, 2, D], F32R)
        act_g = sb("act_g", [P, 2, BANK])
        prod = sb("prod", [P, 2, BANK])
        ps = ctx.enter_context(nc.psum_tensor("up_ps", [P, 2, BATCH, BANK], F32))
        code_loaded = [sem(f"code_loaded{s}") for s in range(2)]
        scale_loaded = [sem(f"scale_loaded{s}") for s in range(2)]
        centered = sem("centered")
        line_ready = sem("line_ready")
        folded = sem("folded")
        w_hi, w_lo = sem("w_hi"), sem("w_lo")
        down_stored = sem("down_stored")
        gate_ready, up_ready = sem("gate_ready"), sem("up_ready")
        silu_ready, prod_ready = sem("silu_ready"), sem("prod_ready")
        prod_stored = [sem(f"prod_stored{s}") for s in range(2)]
        turn = TokenTranspose(nc, ctx, "t1", x, xT, ident,
                              [w[:, 1, m, comp, :].bitcast(F32) for m in range(2) for comp in range(2)],
                              [ps[:, m, 2:4, :] for m in range(2)])
        W_FREE = 2 * BATCH
        PS_FREE = BATCH
        hi_lines, lo_lines = nf4_lines()
        LINES = hi_lines + lo_lines
        shifts = sb("shifts", [P, len(LINES)])
        shifts_set = sem("shifts_set")
        places = [above[:], line[:, 0, :], line[:, 1, :], line[:, 2, :],
                  below[:], line[:, 0, :], line[:, 1, :], line[:, 2, :]]

        def load_code(sp, c, m, slot):
            sp.dma_start(code[:, slot, :], one(codes[m][bass.ds(c, 1)])).then_inc(code_loaded[slot], 16)

        def load_scale(sp, c, m, slot):
            for h in range(2):
                dst = scale[64 * h:64 * h + 64, slot, :]
                if m == DOWN:
                    src = scales[m][bass.ds(c, 1), h, :].to_broadcast([64, D])
                    sp.dma_start(dst, src).then_inc(scale_loaded[slot], 16)
                else:
                    src = scales[m][bass.ds(c, 1), h].to_broadcast([64, KT, P])
                    sp.dma_start(dst.rearrange("p (k i) -> p k i", k=KT), src).then_inc(scale_loaded[slot], 16)

        def uses(k, slot):
            return (k - slot) // 2 + 1 if isinstance(k, int) else None

        with nc.Block() as block:
            @block.sync
            def _(sp):
                def after_unit(c, m, slot, k, c2, m2, load=True):
                    if load:
                        sp.wait_ge(line_ready, k * 8 + 8)
                        load_code(sp, c2, m2, slot)
                    if m == DOWN:
                        sp.wait_ge(folded, k * 8 + 8)
                        sp.dma_start(one(down_w[bass.ds(c, 1)]), scale[:, slot, :]).then_inc(down_stored, 16)
                        sp.wait_ge(down_stored, c * 16 + 16)
                    else:
                        sp.wait_ge(w_lo, c * 2 + m + 1)
                    if load:
                        load_scale(sp, c2, m2, slot)

                def store(c, tb):
                    sp.wait_ge(prod_ready, c * BATCH + tb + 1 + PS_FREE)
                    sp.dma_start(inter[bass.ds(c, 1), tb].rearrange("a p n -> p (a n)"),
                                 prod[:, tb % 2, :]).then_inc(prod_stored[tb % 2], 16)

                def nxt(c, m):
                    return (c + (m + 2) // 3, (m + 2) % 3)

                for m in (GATE, UP):
                    load_code(sp, 0, m, m % 2)
                    load_scale(sp, 0, m, m % 2)
                turn.sync(sp, 0, 4)
                for m in range(3):
                    after_unit(0, m, m % 2, m, *nxt(0, m))
                    if m == 0:
                        turn.sync(sp, 4, turn.PAIRS)

                def chunk(c, odd, units, loads=3):
                    for tb in range(BATCH):
                        if tb < 3 and units:
                            k = (c + 1) * 3 + tb
                            after_unit(c + 1, tb, (odd + 1 + tb) % 2, k, *nxt(c + 1, tb), load=tb < loads)
                        store(c, tb)
                with sp.Fori(0, CH // 2 - 1) as j:
                    chunk(j * 2, 0, True)
                    chunk(j * 2 + 1, 1, True)
                chunk(CH - 2, 0, True, loads=1)
                chunk(CH - 1, 1, False)
                for s in range(2):
                    sp.wait_ge(prod_stored[s], 16 * (CH * 2 + 1))

            @block.scalar
            def _(act):
                def unit(k, slot):
                    act.wait_ge(centered, k + 1)
                    for i, (a, b) in enumerate(LINES):
                        if i == 0 and not (isinstance(k, int) and k == 0):
                            act.wait_ge(folded, k * 8)
                        if i >= 5:
                            act.wait_ge(folded, k * 8 + i - 4)
                        x = code[:, slot, :].bitcast(F32)
                        func = ACT.Relu if i in (0, 4) else ACT.Identity
                        nc.scalar.activation(places[i], x, func, bias=shifts[:, i:i + 1], scale=a).then_inc(line_ready, 1)

                def silu(c, tb):
                    act.wait_ge(gate_ready, c * BATCH + tb + 1)
                    act.wait_ge(prod_ready, c * BATCH + tb - 1 + PS_FREE)
                    nc.scalar.activation(act_g[:, tb % 2, :], ps[:, GATE, tb, :], ACT.Silu).then_inc(silu_ready, 1)

                def chunk(c, odd, units):
                    for tb in range(BATCH):
                        if tb < 3 and units:
                            unit((c + 1) * 3 + tb, (odd + 1 + tb) % 2)
                        silu(c, tb)
                act.wait_ge(shifts_set, len(LINES))
                for k in range(3):
                    unit(k, k % 2)
                    if k < 2:
                        turn.scalar(act, k * 4, k * 4 + 4)
                with act.Fori(0, CH // 2 - 1) as j:
                    chunk(j * 2, 0, True)
                    chunk(j * 2 + 1, 1, True)
                chunk(CH - 2, 0, True)
                chunk(CH - 1, 1, False)

            @block.vector
            def _(dve):
                v = nc.vector
                for i, (a, b) in enumerate(LINES):
                    v.memset(shifts[:, i:i + 1], b).then_inc(shifts_set, 1)
                dve.sem_inc(prod_ready, PS_FREE)
                for s in range(2):
                    dve.sem_inc(prod_stored[s], 16)

                def center(k, slot, loads):
                    dve.wait_ge(code_loaded[slot], loads * 16)
                    v.tensor_scalar(code[:, slot, :].bitcast(F32), code[:, slot, :], float(NF4_ZERO), None,
                                    ALU.subtract).then_inc(centered, 1)

                def fold(k, slot, loads):
                    for m in range(1, 7):
                        i = m if m < 4 else m + 1
                        into = above if m < 4 else below
                        dve.wait_ge(line_ready, k * 8 + i + 1)
                        if m > 1:
                            dve.wait_ge(folded, k * 8 + m - 1)
                        v.tensor_tensor(into[:], into[:], places[i], ALU.max).then_inc(folded, 1)
                    dve.wait_ge(folded, k * 8 + 6)
                    v.tensor_tensor(above[:], above[:], below[:], ALU.subtract).then_inc(folded, 1)
                    dve.wait_ge(folded, k * 8 + 7)
                    dve.wait_ge(scale_loaded[slot], loads * 32)
                    v.tensor_tensor(scale[:, slot, :], above[:], scale[:, slot, :], ALU.mult).then_inc(folded, 1)

                def split(c, m, slot, odd, k):
                    dve.wait_ge(folded, k * 8 + 8)
                    dve.wait_ge(up_ready, c * BATCH + W_FREE - BATCH)
                    v.tensor_copy(w[:, odd, m, HI, :], scale[:, slot, :]).then_inc(w_hi, 1)
                    dve.wait_ge(w_hi, c * 2 + m + 1)
                    v.tensor_tensor(w[:, odd, m, LO, :], scale[:, slot, :], w[:, odd, m, HI, :].bitcast(F32),
                                    ALU.subtract).then_inc(w_lo, 1)

                def unit(c, m, odd, slot, k, loads, next_loads, more=True):
                    fold(k, slot, loads)
                    if more:
                        center(k + 1, 1 - slot, next_loads)
                    if m != DOWN:
                        split(c, m, slot, odd, k)

                def product(c, tb, stores):
                    s = tb % 2
                    dve.wait_ge(silu_ready, c * BATCH + tb + 1)
                    dve.wait_ge(up_ready, c * BATCH + tb + 1 + W_FREE)
                    dve.wait_ge(prod_stored[s], stores * 16)
                    v.tensor_tensor(prod[:, s, :], act_g[:, s, :], ps[:, UP, tb, :], ALU.mult).then_inc(prod_ready, 1)

                center(0, 0, 1)
                for k in range(3):
                    unit(0, k, 0, k % 2, k, k // 2 + 1, (k + 1) // 2 + 1)
                    if k < 2:
                        turn.vector(dve, k * 4, k * 4 + 4)

                def chunk(c, odd, units, half):
                    for tb in range(BATCH):
                        if tb < 3 and units:
                            rest = 3 * odd + 3 + tb
                            unit(c + 1, tb, 1 - odd, rest % 2, half * 6 + rest, half * 3 + rest // 2 + 1,
                                 half * 3 + (rest + 1) // 2 + 1,
                                 more=not (isinstance(c, int) and c == CH - 2 and tb == 2))
                        product(c, tb, half * 4 + 2 * odd + tb // 2 + 1)
                with dve.Fori(0, CH // 2 - 1) as j:
                    chunk(j * 2, 0, True, j)
                    chunk(j * 2 + 1, 1, True, j)
                chunk(CH - 2, 0, True, CH // 2 - 1)
                chunk(CH - 1, 1, False, CH // 2 - 1)

            @block.tensor
            def _(pe):
                pe.sem_inc(up_ready, W_FREE)

                def chunk(c, odd):
                    pe.wait_ge(w_lo, c * 2 + 2)
                    for tb in range(BATCH):
                        pe.wait_ge(prod_ready, c * BATCH + tb + 1)
                        for m, ready in ((GATE, gate_ready), (UP, up_ready)):
                            for kt in range(KT):
                                for wa, wb in PASSES:
                                    mm = nc.tensor.matmul(ps[:, m, tb, :], w[:, odd, m, wa, kt * P:(kt + 1) * P],
                                                          xT[:, wb, kt, tb * BANK:(tb + 1) * BANK],
                                                          start=(kt == 0 and (wa, wb) == PASSES[0]),
                                                          stop=(kt == KT - 1 and (wa, wb) == PASSES[-1]))
                            mm.then_inc(ready, 1)
                turn.tensor(pe, 0, turn.PAIRS)
                pe.wait_ge(turn.lo_ready, TILES + SLOTS)
                with pe.Fori(0, CH // 2) as j:
                    chunk(j * 2, 0)
                    chunk(j * 2 + 1, 1)


def ffn_down(nc, inter, weight, resid, out, seen):
    with ExitStack() as ctx:
        sb = lambda name, shape, dt=F32: ctx.enter_context(nc.sbuf_tensor(f"down_{name}", shape, dt))
        sem = lambda name: ctx.enter_context(nc.semaphore(f"down_{name}"))
        w = sb("w", [P, 2, CH, D], F32R)
        w_raw = sb("w_raw", [P, 2, D])
        a_raw = sb("a_raw", [P, 2, BANK])
        a = sb("a", [P, 2, 2, BANK], F32R)
        r = sb("r", [P, 4, D])
        ps = ctx.enter_context(nc.psum_tensor("down_ps", [P, 4, D], F32))
        w_loaded = [sem(f"w_loaded{s}") for s in range(2)]
        w_hi, w_lo = sem("w_hi"), sem("w_lo")
        a_loaded = [sem(f"a_loaded{s}") for s in range(2)]
        a_hi, a_lo = sem("a_hi"), sem("a_lo")
        r_loaded = [sem(f"r_loaded{t}") for t in range(4)]
        used = sem("used")
        y_ready = sem("y_ready")
        sum_ready = sem("sum_ready")
        stored = [sem(f"stored{t}") for t in range(4)]
        ln = LayerNorm(nc, ctx, "down_ln", sum_ready, seen, base=4, slots=4, in_place=True)
        HEAD = 12
        NORM_AT, STORE_AT, RESID_AT = 2, 3, 8

        def over_k(eng, step, first):
            for k in range(HEAD):
                step(k, k % 2, k // 2, first)
            with eng.Fori(HEAD // 2, CH // 2) as j:
                for s in range(2):
                    step(j * 2 + s, s, j, first)

        with nc.Block() as block:
            @block.sync
            def _(sp):
                def block_of(tb, first):
                    def step(k, s, pair, first):
                        if first:
                            if not (isinstance(k, int) and k < 2):
                                sp.wait_ge(w_lo, k - 1)
                            sp.dma_start(w_raw[:, s, :], one(weight[bass.ds(k, 1)])).then_inc(w_loaded[s], 16)
                        if not (first and isinstance(k, int) and k < 2):
                            sp.wait_ge(a_lo, tb * CH + k - 1)
                        sp.dma_start(a_raw[:, s, :], inter[bass.ds(k, 1), bass.ds(tb, 1)].rearrange("a b p n -> p (a b n)")
                                     ).then_inc(a_loaded[s], 16)
                        if isinstance(k, int) and not first and STORE_AT <= k < STORE_AT + 4:
                            store(tb - 1, k - STORE_AT)
                        if isinstance(k, int) and RESID_AT <= k < RESID_AT + 4:
                            t = k - RESID_AT
                            if not first:
                                sp.wait_ge(stored[t], tb * 16)
                            sp.dma_start(r[:, t, :], one(resid[bass.ds(tb * 4 + t, 1)])).then_inc(r_loaded[t], 16)
                    over_k(sp, step, first)

                def store(tb, t):
                    sp.wait_ge(ln.x_ready, tb * 4 + t + 1)
                    sp.dma_start(one(out[bass.ds(tb * 4 + t, 1)]), r[:, t, :]).then_inc(stored[t], 16)

                block_of(0, True)
                with sp.Fori(1, BATCH) as tb:
                    block_of(tb, False)
                for t in range(4):
                    store(BATCH - 1, t)
                for t in range(4):
                    sp.wait_ge(stored[t], BATCH * 16)

            @block.scalar
            def _(act):
                def block_of(tb, first):
                    def step(k, s, pair, first):
                        if first:
                            act.wait_ge(w_loaded[s], pair * 16 + 16)
                            nc.scalar.copy(w[:, HI, bass.ds(k, 1), :].rearrange("p a n -> p (a n)"), w_raw[:, s, :]).then_inc(w_hi, 1)
                        act.wait_ge(a_loaded[s], (tb * (CH // 2) + pair) * 16 + 16)
                        act.wait_ge(used, tb * CH + k + 1)
                        nc.scalar.copy(a[:, s, HI, :], a_raw[:, s, :]).then_inc(a_hi, 1)
                        if isinstance(k, int) and not first and NORM_AT <= k < NORM_AT + 4:
                            ln.scalar(act, tb * 4 - 4 + k - NORM_AT, k - NORM_AT, r[:, k - NORM_AT, :])
                    over_k(act, step, first)
                block_of(0, True)
                with act.Fori(1, BATCH) as tb:
                    block_of(tb, False)
                for t in range(4):
                    ln.scalar(act, (BATCH - 1) * 4 + t, t, r[:, t, :])

            @block.vector
            def _(dve):
                def add(n, t, loads):
                    dve.wait_ge(r_loaded[t], loads * 16)
                    dve.wait_ge(y_ready, n + 1)
                    nc.vector.tensor_tensor(r[:, t, :], ps[:, t, :], r[:, t, :], ALU.add).then_inc(sum_ready, 1)

                def block_of(tb, first):
                    def step(k, s, pair, first):
                        if first:
                            dve.wait_ge(w_hi, k + 1)
                            lo = w[:, LO, bass.ds(k, 1), :].rearrange("p a n -> p (a n)")
                            hi = w[:, HI, bass.ds(k, 1), :].rearrange("p a n -> p (a n)").bitcast(F32)
                            nc.vector.tensor_tensor(lo, w_raw[:, s, :], hi, ALU.subtract).then_inc(w_lo, 1)
                        dve.wait_ge(a_hi, tb * CH + k + 1)
                        nc.vector.tensor_tensor(a[:, s, LO, :], a_raw[:, s, :], a[:, s, HI, :].bitcast(F32),
                                                ALU.subtract).then_inc(a_lo, 1)
                        if isinstance(k, int) and not first:
                            if k == 0:
                                for t in range(4):
                                    add(tb * 4 - 4 + t, t, tb)
                            if NORM_AT <= k + 1 < NORM_AT + 4:
                                ln.vector(dve, tb * 4 - 4 + k + 1 - NORM_AT, k + 1 - NORM_AT, r[:, k + 1 - NORM_AT, :])
                    over_k(dve, step, first)
                dve.sem_inc(sum_ready, 4)
                block_of(0, True)
                with dve.Fori(1, BATCH) as tb:
                    block_of(tb, False)
                for t in range(4):
                    add((BATCH - 1) * 4 + t, t, BATCH)
                for t in range(4):
                    ln.vector(dve, (BATCH - 1) * 4 + t, t, r[:, t, :])

            @block.tensor
            def _(pe):
                pe.sem_inc(used, SLOTS)

                def products(tb, k, s, start, last, first):
                    pe.wait_ge(a_lo, tb * CH + k + 1)
                    if first:
                        pe.wait_ge(w_lo, k + 1)
                    for t in range(4):
                        if start:
                            pe.wait_ge(sum_ready, tb * 4 + t + 1)
                        for h in range(2):
                            for wa, wb in PASSES:
                                rhs = w[:, wb, bass.ds(k, 1), h * BANK:(h + 1) * BANK].rearrange("p a n -> p (a n)")
                                mm = nc.tensor.matmul(ps[:, t, h * BANK:(h + 1) * BANK], a[:, s, wa, t * P:(t + 1) * P], rhs,
                                                      start=(start and (wa, wb) == PASSES[0]),
                                                      stop=(last and (wa, wb) == PASSES[-1]))
                        if last and t < 3:
                            mm.then_inc(y_ready, 1)
                    if last:
                        mm.then_inc(y_ready, 1)
                        pe.wait_ge(y_ready, tb * 4 + 4)
                        pe.sem_inc(used, 1)
                    else:
                        mm.then_inc(used, 1)

                def block_of(tb, first):
                    products(tb, 0, 0, True, False, first)
                    products(tb, 1, 1, False, False, first)
                    with pe.Fori(1, CH // 2 - 1) as j:
                        products(tb, j * 2, 0, False, False, first)
                        products(tb, j * 2 + 1, 1, False, False, first)
                    products(tb, CH - 2, 0, False, False, first)
                    products(tb, CH - 1, 1, False, True, first)
                block_of(0, True)
                with pe.Fori(1, BATCH) as tb:
                    block_of(tb, False)


def project_qkv(nc, x, ident, weight, tables, out, v_out):
    UNITS = 2 * QK_GROUPS
    V_UNITS = QK_GROUPS
    with ExitStack() as ctx:
        sb = lambda name, shape, dt=F32: ctx.enter_context(nc.sbuf_tensor(f"qk_{name}", shape, dt))
        sem = lambda name: ctx.enter_context(nc.semaphore(f"qk_{name}"))
        xT = sb("xT", [P, 2, KT, T], F32R)
        w_raw = sb("w_raw", [P, KT * 2 * P])
        w = sb("w", [P, 2, 2, KT, 2, P], F32R)
        table = sb("table", [P, 2, 2, SEQ])
        t = sb("t", [P, 4, SEQ])
        o = sb("o", [P, 2, 2, 2, SEQ], F32R)
        ps = ctx.enter_context(nc.psum_tensor("qk_ps", [P, 2, 2, BANK], F32))
        turn = TokenTranspose(nc, ctx, "t2", x, xT, ident,
                              [w[:, 1, comp].bitcast(F32).rearrange("p k a i -> p (k a i)")[:, h * D:(h + 1) * D]
                               for comp in range(2) for h in range(2)],
                              [ps[:, s] for s in range(2)])
        table_loaded = sem("table_loaded")
        w_loaded, w_hi, w_lo = sem("w_loaded"), sem("w_hi"), sem("w_lo")
        y_ready = sem("y_ready")
        turned = sem("turned")
        out_hi, out_lo = sem("out_hi"), sem("out_lo")
        v_taken = [sem(f"v_taken{h}") for h in range(2)]
        stored = [sem(f"stored{s}") for s in range(2)]
        W_FREE = 2 * BATCH
        PS_FREE = 2 * 6
        T_FREE = 2
        V_FREE = 2
        QK_BATCHES, V_BATCHES = UNITS * BATCH, V_UNITS * BATCH
        QK_STORED = (QK_BATCHES // 2 + 1) * 64

        def v_part(s, bank):
            return o[:, s, HI, bank, :].bitcast(F32)

        with nc.Block() as block:
            @block.sync
            def _(sp):
                sp.dma_start(w_raw[:], weight[0]).then_inc(w_loaded, 16)
                turn.sync(sp, 0, turn.PAIRS)
                sp.dma_start(table[:], tables.rearrange("m i p n -> p m i n")).then_inc(table_loaded, 16)

                def load_next(u):
                    sp.wait_ge(w_lo, u + 1)
                    sp.dma_start(w_raw[:], one(weight[bass.ds(u + 1, 1)])).then_inc(w_loaded, 16)

                def unit(u):
                    load_next(u)
                    for b in range(BATCH):
                        n, s = u * BATCH + b, b % 2
                        sp.wait_ge(out_lo, n * 2 + 2 + T_FREE)
                        for comp in range(2):
                            for ab in range(2):
                                sp.dma_start(out[bass.ds(u, 1), b, :, comp, ab].rearrange("a h j n -> (a h) j n"),
                                             o[:, s, comp, ab, :].bitcast(F32)).then_inc(stored[s], 16)

                def v_unit(u, last=False):
                    if not last:
                        load_next(u + UNITS)
                    for b in range(BATCH):
                        for bank in range(2):
                            sp.wait_ge(v_taken[bank], u * BATCH + b + 1 + V_FREE)
                        sp.dma_start(v_out[bass.ds(u, 1), b].rearrange("a t p c -> p (a t) c"),
                                     o[:, b % 2, HI].bitcast(F32).rearrange("p a (t c) -> p (a t) c", t=2)
                                     ).then_inc(stored[b % 2], 16)
                with sp.Fori(0, UNITS) as u:
                    unit(u)
                with sp.Fori(0, V_UNITS - 1) as u:
                    v_unit(u)
                v_unit(V_UNITS - 1, last=True)
                for s in range(2):
                    sp.wait_ge(stored[s], QK_STORED + V_BATCHES // 2 * 16)

            @block.scalar
            def _(act):
                def split_hi(u, s):
                    act.wait_ge(w_loaded, u * 16 + 16)
                    act.wait_ge(y_ready, u * BATCH + BATCH)
                    nc.scalar.copy(w[:, s, HI].rearrange("p k a i -> p (k a i)"), w_raw[:]).then_inc(w_hi, 1)

                def outputs(u, b, stores):
                    n, s = u * BATCH + b, b % 2
                    for ab in range(2):
                        act.wait_ge(turned, n * 6 + 3 + 3 * ab + PS_FREE)
                        if ab == 0:
                            act.wait_ge(stored[s], stores * 64)
                        nc.scalar.copy(o[:, s, HI, ab, :], t[:, 2 * ab, :]).then_inc(out_hi, 1)

                def unit(u, s):
                    for b in range(BATCH):
                        outputs(u, b, u * 2 + b // 2 + 1)
                        if b == 0:
                            split_hi(u + 1, 1 - s)

                def v_unit(u, s, more=True):
                    for b in range(BATCH):
                        act.wait_ge(y_ready, (UNITS + u) * BATCH + b + 1 + W_FREE)
                        act.wait_ge(stored[b % 2], (u * 2 + b // 2) * 16 + QK_STORED)
                        nc.scalar.copy(v_part(b % 2, 0), ps[:, b % 2, 0, :]).then_inc(v_taken[0], 1)
                        if b == 0 and more:
                            split_hi(UNITS + u + 1, 1 - s)

                split_hi(0, 0)
                turn.scalar(act, 0, turn.PAIRS)
                with act.Fori(0, UNITS // 2) as j:
                    unit(j * 2, 0)
                    unit(j * 2 + 1, 1)
                with act.Fori(0, V_UNITS // 2 - 1) as j:
                    v_unit(j * 2, 0)
                    v_unit(j * 2 + 1, 1)
                v_unit(V_UNITS - 2, 0)
                v_unit(V_UNITS - 1, 1, more=False)

            @block.vector
            def _(dve):
                v = nc.vector

                def split_lo(u, s):
                    dve.wait_ge(w_hi, u + 1)
                    v.tensor_tensor(w[:, s, LO].rearrange("p k a i -> p (k a i)"), w_raw[:],
                                    w[:, s, HI].rearrange("p k a i -> p (k a i)").bitcast(F32),
                                    ALU.subtract).then_inc(w_lo, 1)

                def rotate(u, b, m):
                    n, s = u * BATCH + b, b % 2
                    dve.wait_ge(y_ready, n + 1 + W_FREE)
                    for ab in range(2):
                        dve.wait_ge(out_lo, n * 2 + ab - 1 + T_FREE)
                        v.tensor_tensor(t[:, 2 * ab, :], ps[:, s, 0, :], table[:, m, ab, :], ALU.mult).then_inc(turned, 1)
                        v.tensor_tensor(t[:, 2 * ab + 1, :], ps[:, s, 1, :], table[:, m, 1 - ab, :], ALU.mult).then_inc(turned, 1)
                        dve.wait_ge(turned, n * 6 + 3 * ab + 2 + PS_FREE)
                        v.tensor_tensor(t[:, 2 * ab, :], t[:, 2 * ab, :], t[:, 2 * ab + 1, :],
                                        ALU.add if ab else ALU.subtract).then_inc(turned, 1)
                    for ab in range(2):
                        dve.wait_ge(out_hi, n * 2 + ab + 1)
                        v.tensor_tensor(o[:, s, LO, ab, :], t[:, 2 * ab, :], o[:, s, HI, ab, :].bitcast(F32),
                                        ALU.subtract).then_inc(out_lo, 1)

                for s in range(2):
                    dve.sem_inc(stored[s], 64)
                dve.sem_inc(turned, PS_FREE)
                dve.sem_inc(out_lo, T_FREE)
                for bank in range(2):
                    dve.sem_inc(v_taken[bank], V_FREE)

                def unit(u, s, m):
                    for b in range(BATCH):
                        rotate(u, b, m)
                        if b == 0:
                            split_lo(u + 1, 1 - s)

                def v_unit(u, s, more=True):
                    for b in range(BATCH):
                        dve.wait_ge(y_ready, (UNITS + u) * BATCH + b + 1 + W_FREE)
                        dve.wait_ge(stored[b % 2], (u * 2 + b // 2) * 16 + QK_STORED)
                        v.tensor_copy(v_part(b % 2, 1), ps[:, b % 2, 1, :]).then_inc(v_taken[1], 1)
                        if b == 0 and more:
                            split_lo(UNITS + u + 1, 1 - s)

                split_lo(0, 0)
                turn.vector(dve, 0, turn.PAIRS)
                dve.wait_ge(table_loaded, 16)
                with dve.Fori(0, QK_GROUPS // 2) as j:
                    unit(j * 2, 0, 0)
                    unit(j * 2 + 1, 1, 0)
                with dve.Fori(QK_GROUPS // 2, UNITS // 2) as j:
                    unit(j * 2, 0, 1)
                    unit(j * 2 + 1, 1, 1)
                with dve.Fori(0, V_UNITS // 2 - 1) as j:
                    v_unit(j * 2, 0)
                    v_unit(j * 2 + 1, 1)
                v_unit(V_UNITS - 2, 0)
                v_unit(V_UNITS - 1, 1, more=False)

            @block.tensor
            def _(pe):
                pe.sem_inc(y_ready, W_FREE)
                turn.tensor(pe, 0, turn.PAIRS)
                pe.wait_ge(turn.lo_ready, TILES + SLOTS)
                with pe.Fori(0, UNITS // 2) as j:
                    for slot in range(2):
                        u = j * 2 + slot
                        pe.wait_ge(w_lo, u + 1)
                        for b in range(BATCH):
                            n, s = u * BATCH + b, b % 2
                            pe.wait_ge(turned, n * 6 + 6)
                            for ab in range(2):
                                for kt in range(KT):
                                    for wa, wb in PASSES:
                                        mm = nc.tensor.matmul(ps[:, s, ab, :], w[:, slot, wa, kt, ab, :],
                                                              xT[:, wb, kt, b * BANK:(b + 1) * BANK],
                                                              start=(kt == 0 and (wa, wb) == PASSES[0]),
                                                              stop=(kt == KT - 1 and (wa, wb) == PASSES[-1]))
                            mm.then_inc(y_ready, 1)
                pe.wait_ge(turned, QK_BATCHES * 6 + PS_FREE)
                with pe.Fori(0, V_UNITS // 2) as j:
                    for slot in range(2):
                        u = j * 2 + slot
                        pe.wait_ge(w_lo, UNITS + u + 1)
                        for b in range(BATCH):
                            for bank in range(2):
                                pe.wait_ge(v_taken[bank], u * BATCH + b + 1)
                                for half in range(2):
                                    at = b * BANK + (2 * bank + half) * P
                                    for kt in range(KT):
                                        for wa, wb in PASSES:
                                            mm = nc.tensor.matmul(ps[:, b % 2, bank, half * 2 * P:(half + 1) * 2 * P],
                                                                  xT[:, wa, kt, at:at + P],
                                                                  w[:, slot, wb, kt].rearrange("p a i -> p (a i)"),
                                                                  start=(kt == 0 and (wa, wb) == PASSES[0]),
                                                                  stop=(kt == KT - 1 and (wa, wb) == PASSES[-1]))
                            mm.then_inc(y_ready, 1)


def attention(nc, ident, ident_b, above_b, qk, v, out, side, seen):
    NS, HU = 16, 8
    N_HEADS = NS * HU
    QT = SEQ // P
    CAUSAL = P * (QT * (QT + 1) // 2)
    WIDE = 2 * P
    S_AT = (2 * BANK + WIDE, 2 * BANK, BANK, 0)
    S_BANKS = ((3,), (2,), (1, 0))
    N_AT = (0, 128, 384, 768)
    T_AT = (0, BANK, 2 * BANK, BANK + 3 * P)
    T_PARTS = ((0,), (1, 3, 2))
    with ExitStack() as ctx:
        sb = lambda name, shape, dt=F32: ctx.enter_context(nc.sbuf_tensor(f"at_{name}", shape, dt))
        sem = lambda name: ctx.enter_context(nc.semaphore(f"at_{name}"))
        qk_sb = sb("qk", [P, 2, 2, 2, SEQ], F32R)
        vc = sb("vc", [P, QT, 2 * P])
        vp = sb("vp", [P, 2, QT * 4 * P])
        prob = sb("prob", [P, 4, CAUSAL])
        pt = sb("pt", [P, 2, CAUSAL])
        ot = sb("ot", [P, 2, SEQ])
        top = sb("top", [P, 2, 4])
        total = sb("total", [P, 2, 4])
        inv = sb("inv", [P, 2, 4])
        ps_s = ctx.enter_context(nc.psum_tensor("at_s", [P, 3 * BANK], F32))
        ps_t = ctx.enter_context(nc.psum_tensor("at_t", [P, 3 * BANK], F32))
        ps_o = ctx.enter_context(nc.psum_tensor("at_o", [P, 2, BANK], F32))
        qk_loaded = [sem(f"qk_loaded{s}") for s in range(2)]
        v_loaded = sem("v_loaded")
        s_ready = sem("s_ready")
        top_ready = sem("top_ready")
        exp_ready = sem("exp_ready")
        inv_ready = sem("inv_ready")
        prob_act, prob_dve = sem("prob_act"), sem("prob_dve")
        turned = sem("turned")
        pt_act, pt_dve = sem("pt_act"), sem("pt_dve")
        zeros_set = sem("zeros_set")
        vp_ready = sem("vp_ready")
        head_done = sem("head_done")
        o_out = sem("o_out")
        stored = [sem(f"stored{s}") for s in range(2)]
        S_BASE, EXP_BASE, PT_BASE, DONE_BASE, O_BASE = 12, 3, 3, 8, 2

        def spread(slot):
            t = vp[:, slot, :]
            return bass.AP(t.tensor, t.offset, [list(t.ap[0]), [4 * P, QT], [P + HD, 4], [1, HD]])

        with nc.Block() as block:
            @block.sync
            def _(sp):
                def load_pair(n, p, s):
                    sp.wait_ge(s_ready, (n * 8 + 2 * p - 2) * 3 + S_BASE)
                    for m in range(2):
                        src = qk[m, bass.ds(n, 1), 2 * p:2 * p + 2].rearrange("a h c r t -> (a c) r h t")
                        for rows in range(4):
                            comp = rows % 2 if m == 0 else rows // 2
                            sp.dma_start(qk_sb[rows * HD:(rows + 1) * HD, s, m].bitcast(F32), src[comp]).then_inc(qk_loaded[s], 16)

                def load_v(n):
                    sp.dma_start(vc[:], v[bass.ds(n, 1)].rearrange("a k p c -> (a p) k c")).then_inc(v_loaded, 16)

                def store(n, gg):
                    sp.wait_ge(o_out, n * 2 + gg + 1 + O_BASE)
                    dst = out[bass.ds(n * QT, QT), :, gg * P:(gg + 1) * P].rearrange("t p i -> p t i")
                    sp.dma_start(dst, ot[:, gg, :].rearrange("p (t i) -> p t i", t=QT)).then_inc(stored[gg], 16)

                def eight(n, first=False, last=False):
                    def side_tiles(*tiles):
                        if first:
                            for k in tiles:
                                side.sync(sp, k)
                    load_pair(n, 2, 0)
                    side_tiles(1, 2)
                    load_pair(n, 3, 1)
                    side_tiles(3, 4)
                    if not first:
                        store(n - 1, 1)
                    if not last:
                        sp.wait_ge(vp_ready, n * 2 + 2)
                        load_v(n + 1)
                        load_pair(n + 1, 0, 0)
                        side_tiles(5, 6, 7)
                        load_pair(n + 1, 1, 1)
                    store(n, 0)

                load_pair(0, 0, 0)
                load_pair(0, 1, 1)
                load_v(0)
                side.sync(sp, 0, first=True)
                eight(0, first=True)
                with sp.Fori(1, NS - 1) as n:
                    eight(n)
                eight(NS - 1, last=True)
                store(NS - 1, 1)
                for s in range(2):
                    sp.wait_ge(stored[s], (NS + 1) * 16)

            @block.gpsimd
            def _(pool):
                g = nc.gpsimd
                g.memset(vp[:], 0.0).then_inc(zeros_set, 1)
                pool.wait_ge(zeros_set, 1)

                def spread_v(n, gg):
                    if gg == 0:
                        pool.wait_ge(v_loaded, n * 16 + 16)
                    pool.wait_ge(head_done, n * 8 + gg * 4 - 4 + DONE_BASE)
                    pool.sem_inc(seen, 1)
                    g.tensor_copy(spread(gg), vc[:, :, gg * P:(gg + 1) * P].rearrange(
                        "p k (j d) -> p k j d", j=4)).then_inc(vp_ready, 1)

                with pool.Fori(0, NS) as n:
                    for gg in range(2):
                        spread_v(n, gg)

            @block.scalar
            def _(act):
                a = nc.scalar

                def exponentials(n, hh):
                    s, i = hh % 2, n * 8 + hh
                    for bank, tiles in enumerate(S_BANKS):
                        act.wait_ge(top_ready, i * 3 + bank + 1)
                        for q in tiles:
                            e = a.activation(prob[:, hh % 4, N_AT[q]:N_AT[q] + (q + 1) * P], ps_s[:, S_AT[q]:S_AT[q] + (q + 1) * P],
                                             ACT.Exp, bias=top[:, s, q:q + 1], accum_out=total[:, s, q:q + 1])
                        e.then_inc(exp_ready, 1)

                def normalize(i, hh):
                    act.wait_ge(inv_ready, i + 1)
                    x = prob[:, hh % 4, N_AT[3]:CAUSAL]
                    a.activation(x, x, ACT.Copy, scale=inv[:, hh % 2, 3:4]).then_inc(prob_act, 1)

                def take_part(i, hh):
                    act.wait_ge(head_done, i - 1 + DONE_BASE)
                    act.wait_ge(turned, i * 2 + 1)
                    a.copy(pt[:, hh % 2, 0:BANK], ps_t[:, 0:BANK]).then_inc(pt_act, 1)

                def step(n, hh, first=False):
                    i = n * 8 + hh
                    if not first or hh >= 2:
                        take_part(i - 2, (hh - 2) % HU)
                    exponentials(n, hh)
                    if not first or hh >= 1:
                        normalize(i - 1, (hh - 1) % HU)
                for hh in range(HU):
                    step(0, hh, first=True)
                    side.scalar(act, hh)
                with act.Fori(1, NS) as n:
                    for hh in range(HU):
                        step(n, hh)
                take_part(N_HEADS - 2, 6)
                normalize(N_HEADS - 1, 7)
                take_part(N_HEADS - 1, 7)

            @block.vector
            def _(dve):
                v_ = nc.vector
                for s, start in ((s_ready, S_BASE), (exp_ready, EXP_BASE), (pt_act, PT_BASE), (pt_dve, PT_BASE),
                                 (head_done, DONE_BASE), (o_out, O_BASE), (stored[0], 16), (stored[1], 16)):
                    dve.sem_inc(s, start)

                def maxima(n, hh):
                    s, i = hh % 2, n * 8 + hh
                    for bank, tiles in enumerate(S_BANKS):
                        dve.wait_ge(s_ready, i * 3 + bank + 1 + S_BASE)
                        for q in tiles:
                            m = v_.reduce_max(top[:, s, q:q + 1], ps_s[:, S_AT[q]:S_AT[q] + (q + 1) * P], AX.X, negate=True)
                        m.then_inc(top_ready, 1)

                def normalize(i, hh):
                    dve.wait_ge(exp_ready, i * 3 + 3 + EXP_BASE)
                    v_.reciprocal(inv[:, hh % 2, :], total[:, hh % 2, :]).then_inc(inv_ready, 1)
                    dve.wait_ge(inv_ready, i + 1)
                    for q in range(3):
                        x = prob[:, hh % 4, N_AT[q]:N_AT[q] + (q + 1) * P]
                        m = v_.tensor_scalar(x, x, inv[:, hh % 2, q:q + 1], None, ALU.mult)
                    m.then_inc(prob_dve, 1)

                def take_part(i, hh):
                    dve.wait_ge(head_done, i - 1 + DONE_BASE)
                    dve.wait_ge(turned, i * 2 + 2)
                    v_.tensor_copy(pt[:, hh % 2, BANK:CAUSAL], ps_t[:, BANK:CAUSAL]).then_inc(pt_dve, 1)

                def take_out(n, gg):
                    dve.wait_ge(head_done, n * 8 + gg * 4 + 4 + DONE_BASE)
                    dve.wait_ge(stored[gg], n * 16 + 16)
                    v_.tensor_copy(ot[:, gg, :], ps_o[:, gg, :]).then_inc(o_out, 1)

                def step(n, hh, first=False):
                    i = n * 8 + hh
                    maxima(n, hh)
                    if not first or hh >= 1:
                        normalize(i - 1, (hh - 1) % HU)
                    if not first or hh >= 2:
                        take_part(i - 2, (hh - 2) % HU)
                    if hh == 3 and not first:
                        take_out(n - 1, 1)
                    if hh == 7:
                        take_out(n, 0)
                for hh in range(HU):
                    step(0, hh, first=True)
                    side.vector(dve, hh)
                with dve.Fori(1, NS) as n:
                    for hh in range(HU):
                        step(n, hh)
                normalize(N_HEADS - 1, 7)
                take_part(N_HEADS - 2, 6)
                take_part(N_HEADS - 1, 7)
                take_out(NS - 1, 1)

            @block.tensor
            def _(pe):
                def scores(n, hh):
                    i, slot = n * 8 + hh, (hh // 2) % 2
                    if hh % 2 == 0:
                        pe.wait_ge(qk_loaded[slot], (n * 2 + hh // 4 + 1) * 128)
                    for bank, tiles in enumerate(S_BANKS):
                        pe.wait_ge(exp_ready, (i - 1) * 3 + bank + 1 + EXP_BASE)
                        for q in tiles:
                            keys = (q + 1) * P
                            nc.tensor.matmul(ps_s[:, S_AT[q]:S_AT[q] + max(keys, WIDE)], qk_sb[:, slot, 0, hh % 2, q * P:keys],
                                             qk_sb[:, slot, 1, hh % 2, 0:max(keys, WIDE)], start=True, stop=True)
                            m = nc.tensor.matmul(ps_s[:, S_AT[q] + q * P:S_AT[q] + keys], ident_b[:], above_b[:], start=False,
                                                 stop=True, skip_group_check=True)
                        m.then_inc(s_ready, 1)

                def transposes(i, hh):
                    pe.wait_ge(prob_act, i + 1)
                    pe.wait_ge(prob_dve, i + 1)
                    for part, (tiles, taken) in enumerate(zip(T_PARTS, (pt_act, pt_dve))):
                        pe.wait_ge(taken, i + PT_BASE)
                        for k in tiles:
                            for q in range(k, QT):
                                at = T_AT[k] + (q - k) * P
                                m = nc.tensor.transpose(ps_t[:, at:at + P],
                                                        prob[:, hh % 4, N_AT[q] + k * P:N_AT[q] + (k + 1) * P], ident[:])
                        m.then_inc(turned, 1)

                def outputs(n, hh):
                    i, j, gg = n * 8 + hh, hh % 4, hh // 4
                    if j == 0:
                        pe.wait_ge(zeros_set, 1)
                        pe.wait_ge(vp_ready, n * 2 + gg + 1)
                        pe.wait_ge(o_out, n * 2 + gg - 1 + O_BASE)
                    pe.wait_ge(pt_act, i + 1 + PT_BASE)
                    pe.wait_ge(pt_dve, i + 1 + PT_BASE)
                    for k in range(QT):
                        m = nc.tensor.matmul(ps_o[:, gg, k * P:SEQ], vp[:, gg, (k * 4 + j) * P:(k * 4 + j + 1) * P],
                                             pt[:, hh % 2, T_AT[k]:T_AT[k] + (QT - k) * P],
                                             start=(j == 0 and k == 0), stop=(j == 3 and k == 3), skip_group_check=True)
                    m.then_inc(head_done, 1)

                def step(n, hh, first=False):
                    i = n * 8 + hh
                    scores(n, hh)
                    if not first or hh >= 2:
                        transposes(i - 2, (hh - 2) % HU)
                    if not first or hh >= 3:
                        outputs(n if hh >= 3 else n - 1, (hh - 3) % HU)
                for hh in range(HU):
                    step(0, hh, first=True)
                with pe.Fori(1, NS) as n:
                    for hh in range(HU):
                        step(n, hh)
                transposes(N_HEADS - 2, 6)
                outputs(NS - 1, 5)
                transposes(N_HEADS - 1, 7)
                outputs(NS - 1, 6)
                outputs(NS - 1, 7)


def make_constants(nc, ident, above, ident_b, above_b):
    with nc.semaphore("const_filled") as filled, nc.semaphore("const_shaped") as shaped, \
            nc.semaphore("const_ready") as ready, nc.Block() as block:
        @block.gpsimd
        def _(pool):
            nc.gpsimd.memset(ident[:], 0.0).then_inc(filled, 1)
            nc.gpsimd.memset(above[:], 0.0).then_inc(filled, 1)
            pool.wait_ge(filled, 2)
            nc.gpsimd.affine_select(out=ident[:], in_=ident[:], compare_op=ALU.not_equal, fill=1.0, base=0,
                                    pattern=[[-1, P]], channel_multiplier=1).then_inc(shaped, 1)
            nc.gpsimd.affine_select(out=above[:], in_=above[:], compare_op=ALU.is_ge, fill=MASKED, base=0,
                                    pattern=[[-1, P]], channel_multiplier=1).then_inc(shaped, 1)

        @block.vector
        def _(dve):
            dve.wait_ge(shaped, 2)
            nc.vector.tensor_copy(ident_b[:], ident[:]).then_inc(ready, 1)
            nc.vector.tensor_copy(above_b[:], above[:]).then_inc(ready, 1)

        @block.tensor
        def _(pe):
            pe.wait_ge(ready, 2)


def ffn_lora(nc, x, w, bias, lora_b, ident, out, seen):
    N_W, N_Q, N_H = D, EXPERTS * DK, EXPERTS * RANK
    Q_AT, H_AT, K_AT = N_W, N_W + N_Q, N_W + N_Q + N_H
    SCALE = float(1.0 / np.sqrt(np.float64(DK)))
    with ExitStack() as ctx:
        sb = lambda name, shape, dt=F32: ctx.enter_context(nc.sbuf_tensor(f"lora_{name}", shape, dt))
        sem = lambda name: ctx.enter_context(nc.semaphore(f"lora_{name}"))
        b = sb("b", [P, 2, D], F32R)
        b_raw = sb("b_raw", [P, D])
        bias_sb = sb("bias", [P, D])
        xn = sb("xn", [P, 2, D])
        xT = sb("xT", [P, 2, 2, KT * P], F32R)
        r = sb("r", [P, 2, D])
        prod = sb("prod", [P, N_Q])
        score = sb("score", [P, EXPERTS])
        small = sb("small", [P, 4])
        expert = sb("expert", [P, EXPERTS])
        h = sb("h", [P, N_H])
        hT = sb("hT", [P, 2, P], F32R)
        ps_y = ctx.enter_context(nc.psum_tensor("lora_ps_y", [P, 2, D], F32))
        ps_qh = ctx.enter_context(nc.psum_tensor("lora_ps_qh", [P, BANK], F32))
        ps_k = ctx.enter_context(nc.psum_tensor("lora_ps_k", [P, BANK], F32))
        ps_x = ctx.enter_context(nc.psum_tensor("lora_ps_x", [P, D], F32))
        ps_h = ps_k[:, N_Q:N_Q + P]
        b_loaded, b_hi, b_lo = sem("b_loaded"), sem("b_hi"), sem("b_lo")
        bias_loaded = sem("bias_loaded")
        x_loaded = [sem(f"x_loaded{s}") for s in range(2)]
        x_turned, x_hi, x_lo = sem("x_turned"), sem("x_hi"), sem("x_lo")
        r_ready = sem("r_ready")
        qhk_ready = sem("qhk_ready")
        chain = sem("chain")
        exp_ready = sem("exp_ready")
        weigh = sem("weigh")
        h_turned, h_hi, h_lo = sem("h_turned"), sem("h_hi"), sem("h_lo")
        y_ready, sum_ready = sem("y_ready"), sem("sum_ready")
        stored = [sem(f"stored{s}") for s in range(2)]
        ln = LayerNorm(nc, ctx, "lora_ln", sum_ready, seen, in_place=True)
        X_BASE = 2

        with nc.Block() as block:
            @block.sync
            def _(sp):
                def load_x(n, s):
                    sp.dma_start(xn[:, s, :], one(x[bass.ds(n, 1)])).then_inc(x_loaded[s], 16)
                for s in range(2):
                    load_x(s, s)
                sp.dma_start(b_raw[:], lora_b).then_inc(b_loaded, 16)
                sp.dma_start(bias_sb[:], bias.to_broadcast([P, D])).then_inc(bias_loaded, 16)

                def tile(n, s):
                    sp.wait_ge(x_turned, n - 1)
                    sp.wait_ge(r_ready, n - 1)
                    load_x(n, s)
                    sp.wait_ge(ln.x_ready, n - 1 + X_BASE)
                    sp.dma_start(one(out[bass.ds(n - 2, 1)]), r[:, s, :]).then_inc(stored[s], 16)
                with sp.Fori(1, TILES // 2) as j:
                    for s in range(2):
                        tile(j * 2 + s, s)
                for s in range(2):
                    sp.wait_ge(ln.x_ready, TILES - 1 + s + X_BASE)
                    sp.dma_start(out[TILES - 2 + s], r[:, s, :]).then_inc(stored[s], 16)
                for s in range(2):
                    sp.wait_ge(stored[s], 16 * (TILES // 2 + 1))

            @block.gpsimd
            def _(pool):
                for s in range(2):
                    pool.sem_inc(stored[s], 16)
                pool.wait_ge(bias_loaded, 16)
                with pool.Fori(0, TILES // 2) as j:
                    for s in range(2):
                        pool.wait_ge(x_loaded[s], j * 16 + 16)
                        pool.wait_ge(stored[s], j * 16 + 16)
                        pool.sem_inc(seen, 1)
                        nc.gpsimd.tensor_tensor(r[:, s, :], xn[:, s, :], bias_sb[:], ALU.add).then_inc(r_ready, 1)

            @block.scalar
            def _(act):
                a = nc.scalar
                act.sem_inc(ln.x_ready, X_BASE)

                def split_x(n, s):
                    act.wait_ge(x_turned, n + 1)
                    a.copy(xT[:, s, HI, :], ps_x[:]).then_inc(x_hi, 1)

                def tile(n, s, more=True):
                    if more:
                        split_x(n + 1, 1 - s)
                    act.wait_ge(chain, n * 4 + 4)
                    a.activation(expert[:], score[:], ACT.Exp, bias=small[:, 1:2], scale=SCALE,
                                 accum_out=small[:, 2:3]).then_inc(exp_ready, 1)
                    act.wait_ge(h_turned, n + 1)
                    a.copy(hT[:, HI, :], ps_h).then_inc(h_hi, 1)
                    ln.scalar(act, n, s, r[:, s, :])
                split_x(0, 0)
                act.wait_ge(b_loaded, 16)
                a.copy(b[:, HI, :], b_raw[:]).then_inc(b_hi, 1)
                with act.Fori(0, TILES // 2 - 1) as j:
                    for s in range(2):
                        tile(j * 2 + s, s)
                tile(TILES - 2, 0)
                tile(TILES - 1, 1, more=False)

            @block.vector
            def _(dve):
                v = nc.vector
                dve.sem_inc(sum_ready, SLOTS)

                def split_x(n, s):
                    dve.wait_ge(x_hi, n + 1)
                    v.tensor_tensor(xT[:, s, LO, :], ps_x[:], xT[:, s, HI, :].bitcast(F32), ALU.subtract).then_inc(x_lo, 1)

                def tile(n, s, more=True):
                    dve.wait_ge(qhk_ready, n + 1)
                    v.tensor_copy(prod[:], ps_k[:, 0:N_Q]).then_inc(chain, 1)
                    dve.wait_ge(chain, n * 4 + 1)
                    v.tensor_tensor(prod[:], ps_qh[:, 0:N_Q], prod[:], ALU.mult).then_inc(chain, 1)
                    dve.wait_ge(chain, n * 4 + 2)
                    v.reduce_sum(score[:], prod[:].rearrange("p (e d) -> p e d", e=EXPERTS), AX.X).then_inc(chain, 1)
                    dve.wait_ge(chain, n * 4 + 3)
                    v.reduce_max(small[:, 0:1], score[:], AX.X, negate=True).then_inc(weigh, 1)
                    dve.wait_ge(weigh, n * 4 + 1)
                    v.tensor_scalar(small[:, 1:2], small[:, 0:1], SCALE, None, ALU.mult).then_inc(chain, 1)
                    if more:
                        split_x(n + 1, 1 - s)
                    dve.wait_ge(exp_ready, n + 1)
                    v.reciprocal(small[:, 3:4], small[:, 2:3]).then_inc(weigh, 1)
                    dve.wait_ge(weigh, n * 4 + 2)
                    v.tensor_scalar(expert[:], expert[:], small[:, 3:4], None, ALU.mult).then_inc(weigh, 1)
                    dve.wait_ge(weigh, n * 4 + 3)
                    v.tensor_tensor(h[:].rearrange("p (e r) -> p e r", e=EXPERTS),
                                    ps_qh[:, N_Q:N_Q + N_H].rearrange("p (e r) -> p e r", e=EXPERTS),
                                    expert[:].unsqueeze(2).to_broadcast([P, EXPERTS, RANK]), ALU.mult).then_inc(weigh, 1)
                    dve.wait_ge(h_hi, n + 1)
                    v.tensor_tensor(hT[:, LO, :], ps_h, hT[:, HI, :].bitcast(F32), ALU.subtract).then_inc(h_lo, 1)
                    dve.wait_ge(r_ready, n + 1)
                    dve.wait_ge(y_ready, n + 1)
                    v.tensor_tensor(r[:, s, :], ps_y[:, s, :], r[:, s, :], ALU.add).then_inc(sum_ready, 1)
                    ln.vector(dve, n, s, r[:, s, :])
                split_x(0, 0)
                dve.wait_ge(b_hi, 1)
                v.tensor_tensor(b[:, LO, :], b_raw[:], b[:, HI, :].bitcast(F32), ALU.subtract).then_inc(b_lo, 1)
                with dve.Fori(0, TILES // 2 - 1) as j:
                    for s in range(2):
                        tile(j * 2 + s, s)
                tile(TILES - 2, 0)
                tile(TILES - 1, 1, more=False)

            @block.tensor
            def _(pe):
                def transposes(s, loads):
                    pe.wait_ge(x_loaded[s], loads * 16)
                    for kt in range(KT):
                        m = nc.tensor.transpose(ps_x[:, kt * P:(kt + 1) * P], xn[:, s, kt * P:(kt + 1) * P], ident[:])
                    m.then_inc(x_turned, 1)

                def product(into, s, at, width, stop=True):
                    for kt in range(KT):
                        for wa, wb in PASSES:
                            m = nc.tensor.matmul(into, xT[:, s, wa, kt * P:(kt + 1) * P], w[:, wb, kt, at:at + width],
                                                 start=(kt == 0 and (wa, wb) == PASSES[0]),
                                                 stop=(stop and kt == KT - 1 and (wa, wb) == PASSES[-1]))
                    return m

                def tile(n, s, loads, more=True):
                    pe.wait_ge(x_lo, n + 1)
                    product(ps_qh[:, 0:N_Q + N_H], s, Q_AT, N_Q + N_H)
                    product(ps_k[:, 0:N_Q], s, K_AT, N_Q).then_inc(qhk_ready, 1)
                    if more:
                        transposes(1 - s, loads)
                    pe.wait_ge(sum_ready, n + 1)
                    product(ps_y[:, s, 0:BANK], s, 0, BANK, stop=False)
                    pe.wait_ge(weigh, n * 4 + 4)
                    nc.tensor.transpose(ps_h, h[:], ident[:]).then_inc(h_turned, 1)
                    product(ps_y[:, s, BANK:D], s, BANK, BANK, stop=False)
                    pe.wait_ge(b_lo, 1)
                    pe.wait_ge(h_lo, n + 1)
                    for half in range(2):
                        for wa, wb in PASSES:
                            m = nc.tensor.matmul(ps_y[:, s, half * BANK:(half + 1) * BANK], hT[:, wa, :],
                                                 b[:, wb, half * BANK:(half + 1) * BANK], start=False,
                                                 stop=(wa, wb) == PASSES[-1])
                    m.then_inc(y_ready, 1)
                transposes(0, 1)
                with pe.Fori(0, TILES // 2 - 1) as j:
                    tile(j * 2, 0, j + 1)
                    tile(j * 2 + 1, 1, j + 2)
                tile(TILES - 2, 0, TILES // 2)
                tile(TILES - 1, 1, None, more=False)


def build(nc, x, x_turned, attn_w, attn_mask, codes, scales, qkv_w, tables, o_w, lora_w, bias, lora_b, out):
    dram = lambda name, *shape: nc.dram_tensor(f"between_{name}", shape, F32, kind="Internal").ap()
    x1, x2, x3 = (dram(f"x{i}", TILES, P, D) for i in (1, 2, 3))
    down_w = dram("down_w", CH, P, D)
    inter = dram("inter", CH, BATCH, P, SEQ)
    qk = dram("qk", 2 * QK_GROUPS, BATCH, 8, 2, 2, HD // 2, SEQ)
    v = dram("v", QK_GROUPS, BATCH, SEQ // P, P, 2 * P)
    heads = dram("heads", QK_GROUPS, TILES, P, 2 * P)
    with ExitStack() as ctx:
        sb = lambda name, dt: ctx.enter_context(nc.sbuf_tensor(name, [P, P], dt))
        ident, above = sb("ident", F32), sb("above", F32)
        ident_b, above_b = sb("ident_b", BF16), sb("above_b", BF16)
        seen = ctx.enter_context(nc.semaphore("seen"))
        make_constants(nc, ident, above, ident_b, above_b)
        linear_ln(nc, "l0", x_turned, x, x1, seen, weight=attn_w, mask=attn_mask)
        ffn_up(nc, x1, ident, codes, scales, down_w, inter)
        ffn_down(nc, inter, down_w, x1, x2, seen)
        project_qkv(nc, x2, ident, qkv_w, tables, qk, v)
        with ExitStack() as late:
            o_wt = late.enter_context(nc.sbuf_tensor("o_wt", [P, 2, KT, D], F32R))
            with ExitStack() as beside:
                attention(nc, ident, ident_b, above_b,
                          qk.rearrange("(m u) b h c a j t -> m (u b) h c (a j) t", m=2),
                          v.rearrange("u b k p i -> (u b) k p i"),
                          heads.rearrange("u t p i -> (u t) p i"),
                          WeightSplit(nc, beside, "o_wt", o_w, o_wt), seen)
            lora_wt = late.enter_context(nc.sbuf_tensor("lora_wt", [P, 2, KT, lora_w.shape[2]], F32R))
            with ExitStack() as beside:
                linear_ln(nc, "l1", heads.rearrange("u n p i -> n p u i"), x2, x3, seen, w=o_wt,
                          side=WeightSplit(nc, beside, "lora_wt", lora_w, lora_wt))
            ffn_lora(nc, x3, lora_wt, bias, lora_b, ident, out, seen)


def kernel(L0_attn_data, L0_attn_weight, L0_attn_mask, L0_ffn_gate_codes, L0_ffn_gate_scales, L0_ffn_up_codes,
           L0_ffn_up_scales, L0_ffn_down_codes, L0_ffn_down_scales, L1_attn_wq, L1_attn_wk, L1_attn_wv, L1_attn_wo,
           L1_ffn_W, L1_ffn_b, L1_ffn_Wq, L1_ffn_Wk, L1_ffn_A, L1_ffn_Bm):
    import concourse.bacc as bacc
    from concourse.bass_utils import run_bass_kernel_spmd

    x = np.asarray(L0_attn_data)
    pad = CH * P - I_FFN
    arrays = {}

    def put(name, array):
        arrays[name] = np.ascontiguousarray(array)

    put("x", x.reshape(TILES, P, D))
    put("x_turned", x.reshape(TILES, P, KT, P).transpose(0, 3, 2, 1))
    put("attn_w", np.asarray(L0_attn_weight).T.reshape(KT, P, D))
    put("attn_mask", np.asarray(L0_attn_mask).T.reshape(KT, P, D))

    def up_codes(a):
        a = np.pad(np.asarray(a), ((0, pad), (0, 0)), constant_values=NF4_ZERO)
        return a.reshape(CH, P, KT, P).transpose(0, 3, 2, 1).reshape(CH, P, KT * P)

    def up_scales(a):
        a = np.pad(np.asarray(a), ((0, pad), (0, 0)))
        return a.reshape(CH, P, KT, P // NF4_BLOCK).transpose(0, 3, 2, 1)

    put("gate_codes", up_codes(L0_ffn_gate_codes))
    put("up_codes", up_codes(L0_ffn_up_codes))
    put("down_codes", np.pad(np.asarray(L0_ffn_down_codes).T, ((0, pad), (0, 0)),
                             constant_values=NF4_ZERO).reshape(CH, P, D))
    put("gate_scales", up_scales(L0_ffn_gate_scales))
    put("up_scales", up_scales(L0_ffn_up_scales))
    put("down_scales", np.pad(np.asarray(L0_ffn_down_scales).T,
                              ((0, pad // NF4_BLOCK), (0, 0))).reshape(CH, P // NF4_BLOCK, D))

    def rotary_weight(a):
        a = np.asarray(a).reshape(KT, P, QK_GROUPS, 8, HD // 2, 2)
        return a.transpose(2, 1, 0, 5, 3, 4).reshape(QK_GROUPS, P, KT * 2 * P)

    v_w = np.asarray(L1_attn_wv).reshape(KT, P, QK_GROUPS, 2 * P).transpose(2, 1, 0, 3).reshape(QK_GROUPS, P, -1)
    put("qkv_w", np.concatenate([rotary_weight(L1_attn_wq), rotary_weight(L1_attn_wk), v_w]))
    frequency = 1.0 / 10000.0 ** (np.arange(0, HD, 2)[:HD // 2].astype(np.float32) / HD)
    angle = np.outer(np.arange(SEQ), frequency).astype(np.float32)
    k_tables = np.stack([np.tile(f(angle).T, (8, 1)) for f in (np.cos, np.sin)])
    put("tables", np.stack([k_tables * (np.float32(1.0) / np.sqrt(np.float32(HD))), k_tables]).astype(np.float32))
    put("o_w", np.asarray(L1_attn_wo).reshape(KT, P, D))

    lora_a = np.asarray(L1_ffn_A).reshape(EXPERTS * RANK, D)
    put("lora_w", np.concatenate([np.asarray(a).T for a in (L1_ffn_W, L1_ffn_Wq, lora_a, L1_ffn_Wk)],
                                 axis=1).reshape(KT, P, -1))
    put("bias", np.asarray(L1_ffn_b).reshape(1, D))
    put("lora_b", np.asarray(L1_ffn_Bm).transpose(0, 2, 1).reshape(EXPERTS * RANK, D))

    nc = bacc.Bacc("TRN2", target_bir_lowering=False, num_devices=1, dynamic_dma_scratch_size=1024)
    ap = {name: nc.dram_tensor(f"in_{name}", a.shape, mybir.dt.from_np(a.dtype), kind="ExternalInput").ap()
          for name, a in arrays.items()}
    out = nc.dram_tensor("out", (TILES, P, D), F32, kind="ExternalOutput").ap()
    build(nc, ap["x"], ap["x_turned"], ap["attn_w"], ap["attn_mask"],
          (ap["gate_codes"], ap["up_codes"], ap["down_codes"]),
          (ap["gate_scales"], ap["up_scales"], ap["down_scales"]),
          ap["qkv_w"], ap["tables"], ap["o_w"], ap["lora_w"], ap["bias"], ap["lora_b"], out)
    result = run_bass_kernel_spmd(nc, [{f"in_{name}": a for name, a in arrays.items()}], core_ids=[0])
    return result.results[0]["out"].reshape(x.shape)
```

```python
import numpy as np
import concourse.bass as bass
from concourse import mybir
from contextlib import ExitStack

F32 = mybir.dt.float32
F32R = mybir.dt.float32r
I32 = mybir.dt.int32
BF16 = mybir.dt.bfloat16
ALU = mybir.AluOpType
ACT = mybir.ActivationFunctionType
AX = mybir.AxisListType

P = 128
T, D = 2048, 1024
BATCH, SEQ = 4, 512
TILES = T // P
KT = D // P
BANK = 512
BLK = 32
I_FFN = 2752
CH = -(-I_FFN // P)
NF4_BLOCK = 64
HEADS, HD = 32, 32
GROUPS = 8
QK_GROUPS = 4
EXPERTS, DK, RANK = 8, 32, 16
EPS = 1e-5
SLOTS = 2
MASKED = -1e30

HI, LO = 0, 1
PASSES = ((LO, HI), (HI, LO), (HI, HI))


def one(ap):
    return ap.rearrange("a p n -> p (a n)")


class LayerNorm:

    STEPS = 15

    def __init__(self, nc, ctx, tag, sum_ready, seen, base=SLOTS, slots=2, in_place=False):
        sb = lambda name, shape, dt=F32: ctx.enter_context(nc.sbuf_tensor(f"{tag}_{name}", shape, dt))
        sem = lambda name: ctx.enter_context(nc.semaphore(f"{tag}_{name}"))
        self.nc = nc
        self.x = None if in_place else sb("x", [P, slots, D])
        self.stats = sb("stats", [P, slots, 2, 6])
        self.mv = sb("mv", [P, slots, 2])
        self.small = sb("small", [P, slots, 8])
        self.sum_ready, self.base = sum_ready, base
        self.steps = sem("steps")
        self.seen = seen
        self.x_ready = sem("x_ready")

    def vector(self, dve, n, s, r):
        v, sm, mv, steps, at = self.nc.vector, self.small[:, s, :], self.mv[:, s, :], self.steps, n * self.STEPS
        dve.wait_ge(self.sum_ready, n + self.base + 1)
        v.bn_stats(self.stats[:, s, 0, :], r[:, 0:BANK])
        v.bn_stats(self.stats[:, s, 1, :], r[:, BANK:D]).then_inc(steps, 1)
        dve.wait_ge(steps, at + 1)
        dve.sem_inc(self.seen, 1)
        v.bn_aggr(mv, self.stats[:, s, :, :].rearrange("p a b -> p (a b)")).then_inc(steps, 1)
        dve.wait_ge(steps, at + 2)
        ve, half, y, t = sm[:, 0:1], sm[:, 1:2], sm[:, 2:3], sm[:, 3:4]
        v.tensor_scalar(ve, mv[:, 1:2], EPS, None, ALU.add).then_inc(steps, 1)
        dve.wait_ge(steps, at + 3)
        v.tensor_scalar(half.bitcast(I32), ve.bitcast(I32), 1, None, ALU.logical_shift_right).then_inc(steps, 1)
        dve.wait_ge(steps, at + 4)
        v.tensor_scalar(y.bitcast(I32), half.bitcast(I32), -1.0, float(0x5F3759DF), ALU.mult, ALU.add).then_inc(steps, 1)
        for k in range(3):
            done = at + 3 * k + 5
            dve.wait_ge(steps, done)
            v.scalar_tensor_tensor(t, ve, -0.5, y, ALU.mult, ALU.mult).then_inc(steps, 1)
            dve.wait_ge(steps, done + 1)
            v.tensor_tensor(t, t, y, ALU.mult).then_inc(steps, 1)
            dve.wait_ge(steps, done + 2)
            v.scalar_tensor_tensor(y, t, 1.5, y, ALU.add, ALU.mult).then_inc(steps, 1)
        dve.wait_ge(steps, at + 14)
        v.scalar_tensor_tensor(sm[:, 4:5], mv[:, 0:1], -1.0, y, ALU.mult, ALU.mult).then_inc(steps, 1)

    def scalar(self, act, n, s, r, x_free=None, free_at=0):
        a, sm = self.nc.scalar, self.small[:, s, :]
        act.wait_ge(self.steps, (n + 1) * self.STEPS)
        if x_free is not None:
            act.wait_ge(x_free, free_at)
        a.activation(r if self.x is None else self.x[:, s, :], r, ACT.Identity, bias=sm[:, 4:5], scale=sm[:, 2:3]).then_inc(self.x_ready, 1)


class WeightSplit:

    def __init__(self, nc, ctx, tag, weight, w):
        sem = lambda name: ctx.enter_context(nc.semaphore(f"{tag}_{name}"))
        self.nc, self.weight, self.w = nc, weight, w
        self.raw = ctx.enter_context(nc.sbuf_tensor(f"{tag}_raw", [P, weight.shape[2]], F32))
        self.loaded, self.hi_ready, self.lo_ready = sem("loaded"), sem("hi_ready"), sem("lo_ready")

    def part(self, comp, k):
        return self.w[:, comp, bass.ds(k, 1), :].rearrange("p a n -> p (a n)")

    def sync(self, sp, k, first=False):
        if not first:
            sp.wait_ge(self.lo_ready, k)
        sp.dma_start(self.raw[:], one(self.weight[bass.ds(k, 1)])).then_inc(self.loaded, 16)

    def scalar(self, act, k):
        act.wait_ge(self.loaded, k * 16 + 16)
        self.nc.scalar.copy(self.part(HI, k), self.raw[:]).then_inc(self.hi_ready, 1)

    def vector(self, dve, k):
        dve.wait_ge(self.hi_ready, k + 1)
        self.nc.vector.tensor_tensor(self.part(LO, k), self.raw[:], self.part(HI, k).bitcast(F32),
                                     ALU.subtract).then_inc(self.lo_ready, 1)


def linear_ln(nc, tag, acts, resid, out, seen, weight=None, mask=None, w=None, side=None, late=None):
    N_LATE = 0 if late is None else late.HALVES
    LOOPED = TILES // 2 - 1 - N_LATE
    with ExitStack() as ctx:
        sb = lambda name, shape, dt=F32: ctx.enter_context(nc.sbuf_tensor(f"{tag}_{name}", shape, dt))
        sem = lambda name: ctx.enter_context(nc.semaphore(f"{tag}_{name}"))
        a_raw = sb("a_raw", [P, 2, KT * P])
        a = sb("a", [P, 2, 2, KT * P], F32R)
        r = sb("r", [P, 2, D])
        ps = ctx.enter_context(nc.psum_tensor(f"{tag}_ps", [P, 2, D], F32))
        RAW = 4
        if mask is not None:
            w = sb("w", [P, 2, KT, D], F32R)
            w_raw = sb("w_raw", [P, RAW, D])
            m_raw = sb("m_raw", [P, RAW, D], I32)
            m_sum = sb("m_sum", [P, 2, BLK])
            m_one = sb("m_one", [P, 2, BLK])
            same = sb("same", [P, P])
            pm = ctx.enter_context(nc.psum_tensor(f"{tag}_pm", [P, 2, BANK], F32))
            w_loaded = [sem(f"w_loaded{s}") for s in range(RAW)]
            w_hi, w_lo = sem("w_hi"), sem("w_lo")
            w_masked = sem("w_masked")
            same_ready, sums_ready, blocks_ready, ones_ready = (
                sem(x) for x in ("same_ready", "sums_ready", "blocks_ready", "ones_ready"))
        a_loaded = [sem(f"a_loaded{s}") for s in range(2)]
        r_loaded = [sem(f"r_loaded{s}") for s in range(2)]
        a_hi, a_lo = sem("a_hi"), sem("a_lo")
        y_ready = sem("y_ready")
        sum_ready = sem("sum_ready")
        stored = [sem(f"stored{s}") for s in range(2)]
        ln = LayerNorm(nc, ctx, f"{tag}_ln", sum_ready, seen, in_place=side is not None)
        X = r if side is not None else ln.x

        acts_tile = lambda n: acts[bass.ds(n, 1)].rearrange("a p u i -> (a p) u i")
        a_view = lambda s: a_raw[:, s, :].rearrange("p (u i) -> p u i", u=acts.shape[2])

        with nc.Block() as block:
            @block.sync
            def _(sp):
                sp.sem_inc(stored[0], 16)
                sp.sem_inc(stored[1], 16)

                def load_w(k):
                    sp.dma_start(m_raw[:, k % RAW, :], mask[k]).then_inc(w_loaded[k % RAW], 16)
                    sp.dma_start(w_raw[:, k % RAW, :], weight[k]).then_inc(w_loaded[k % RAW], 16)

                for s in range(2):
                    if mask is not None:
                        load_w(s)
                    sp.dma_start(a_view(s), acts_tile(s)).then_inc(a_loaded[s], 16)
                if mask is not None:
                    for k in range(2, KT):
                        if k >= RAW:
                            sp.wait_ge(w_lo, k - RAW + 1)
                        load_w(k)
                if side is not None:
                    side.sync(sp, 0, first=True)
                for s in range(2):
                    sp.dma_start(r[:, s, :], resid[s]).then_inc(r_loaded[s], 16)

                def load_acts(n, s):
                    sp.wait_ge(a_lo, n - 1)
                    sp.dma_start(a_view(s), acts_tile(n)).then_inc(a_loaded[s], 16)

                def next_tile(n, s, stores):
                    sp.wait_ge(ln.x_ready, n - 1)
                    sp.dma_start(one(out[bass.ds(n - 2, 1)]), X[:, s, :]).then_inc(stored[s], 16)
                    if side is not None:
                        sp.wait_ge(stored[s], stores * 16 + 16)
                    sp.dma_start(r[:, s, :], one(resid[bass.ds(n, 1)])).then_inc(r_loaded[s], 16)

                load_acts(2, 0)

                def pair(j, h=None):
                    load_acts(j * 2 + 1, 1)
                    next_tile(j * 2, 0, j)
                    load_acts(j * 2 + 2, 0)
                    next_tile(j * 2 + 1, 1, j)
                    if h:
                        late.sync(sp, h)
                if LOOPED > 1:
                    with sp.Fori(1, LOOPED) as j:
                        if side is not None:
                            side.sync(sp, j)
                        pair(j)
                if late is not None:
                    late.sync(sp, 0)
                for h in range(N_LATE):
                    pair(LOOPED + h, h)
                if side is not None:
                    side.sync(sp, KT - 1)
                load_acts(TILES - 1, 1)
                next_tile(TILES - 2, 0, TILES // 2 - 1)
                next_tile(TILES - 1, 1, TILES // 2 - 1)
                if late is not None:
                    late.sync(sp, N_LATE)
                for s in range(2):
                    sp.wait_ge(ln.x_ready, TILES - 1 + s)
                    sp.dma_start(out[TILES - 2 + s], X[:, s, :]).then_inc(stored[s], 16)
                for s in range(2):
                    sp.wait_ge(stored[s], 16 * (TILES // 2 + 1))

            @block.scalar
            def _(act):
                def split_hi(n, s, loads):
                    act.wait_ge(a_loaded[s], loads * 16)
                    act.wait_ge(y_ready, n + 1)
                    nc.scalar.copy(a[:, s, HI, :], a_raw[:, s, :]).then_inc(a_hi, 1)

                split_hi(0, 0, 1)
                split_hi(1, 1, 1)
                if mask is not None:
                    for k in range(KT):
                        act.wait_ge(w_masked, k + 1)
                        nc.scalar.copy(w[:, HI, k, :], w_raw[:, k % RAW, :]).then_inc(w_hi, 1)

                def pair(j, h=None):
                    for s in range(2):
                        split_hi(j * 2 + 2 + s, s, j + 2)
                        ln.scalar(act, j * 2 + s, s, r[:, s, :], stored[s], j * 16 + 16)
                        if h is not None and s == 0:
                            late.scalar(act, h)
                with act.Fori(0, LOOPED) as j:
                    if side is not None:
                        side.scalar(act, j)
                    pair(j)
                for h in range(N_LATE):
                    pair(LOOPED + h, h)
                if side is not None:
                    side.scalar(act, KT - 1)
                for s in range(2):
                    ln.scalar(act, TILES - 2 + s, s, r[:, s, :], stored[s], TILES // 2 * 16)

            @block.vector
            def _(dve):
                v = nc.vector
                dve.sem_inc(sum_ready, SLOTS)
                if mask is not None:
                    v.memset(same[:], 0.0).then_inc(same_ready, 1)
                    dve.wait_ge(same_ready, 1)
                    for b in range(P // BLK):
                        v.memset(same[b * BLK:(b + 1) * BLK, b * BLK:(b + 1) * BLK], 1.0).then_inc(same_ready, 1)

                def mask_sums(k):
                    dve.wait_ge(w_loaded[k % RAW], (k // RAW + 1) * 32)
                    v.reduce_sum(m_sum[:, k % 2, :], m_raw[:, k % RAW, :].rearrange("p (b c) -> p b c", c=BLK),
                                 AX.X).then_inc(sums_ready, 1)

                def mask_weight(k):
                    dve.wait_ge(blocks_ready, k + 1)
                    v.tensor_scalar(m_one[:, k % 2, :], pm[:, k % 2, 0:BLK], 0.0, None, ALU.is_gt).then_inc(ones_ready, 1)
                    dve.wait_ge(ones_ready, k + 1)
                    w3 = w_raw[:, k % RAW, :].rearrange("p (b c) -> p b c", c=BLK)
                    v.tensor_tensor(w3, w3, m_one[:, k % 2, :].unsqueeze(2).to_broadcast([P, BLK, BLK]),
                                    ALU.mult).then_inc(w_masked, 1)

                def weight_lo(k):
                    dve.wait_ge(w_hi, k + 1)
                    v.tensor_tensor(w[:, LO, k, :], w_raw[:, k % RAW, :], w[:, HI, k, :].bitcast(F32),
                                    ALU.subtract).then_inc(w_lo, 1)

                def split_lo(n, s):
                    dve.wait_ge(a_hi, n + 1)
                    v.tensor_tensor(a[:, s, LO, :], a_raw[:, s, :], a[:, s, HI, :].bitcast(F32),
                                    ALU.subtract).then_inc(a_lo, 1)

                def finish(n, s, loads):
                    dve.wait_ge(r_loaded[s], loads * 16)
                    dve.wait_ge(y_ready, n + SLOTS + 1)
                    v.tensor_tensor(r[:, s, :], ps[:, s, :], r[:, s, :], ALU.add).then_inc(sum_ready, 1)
                    ln.vector(dve, n, s, r[:, s, :])

                if mask is not None:
                    mask_sums(0)
                split_lo(0, 0)
                split_lo(1, 1)
                if mask is not None:
                    for k in range(KT):
                        if k + 1 < KT:
                            mask_sums(k + 1)
                        mask_weight(k)
                        if k:
                            weight_lo(k - 1)
                    weight_lo(KT - 1)

                def pair(j, h=None):
                    for s in range(2):
                        split_lo(j * 2 + 2 + s, s)
                        finish(j * 2 + s, s, j + 1)
                        if h is not None:
                            late.vector(dve, h, s)
                with dve.Fori(0, LOOPED) as j:
                    if side is not None:
                        side.vector(dve, j)
                    pair(j)
                for h in range(N_LATE):
                    pair(LOOPED + h, h)
                if side is not None:
                    side.vector(dve, KT - 1)
                for s in range(2):
                    finish(TILES - 2 + s, s, TILES // 2)

            @block.tensor
            def _(pe):
                pe.sem_inc(y_ready, SLOTS)

                def block_sums(k):
                    pe.wait_ge(sums_ready, k + 1)
                    nc.tensor.matmul(pm[:, k % 2, 0:BLK], same[:], m_sum[:, k % 2, :], start=True, stop=True).then_inc(blocks_ready, 1)

                def products(s, h, kt):
                    for wa, wb in PASSES:
                        mm = nc.tensor.matmul(ps[:, s, h * BANK:(h + 1) * BANK], a[:, s, wa, kt * P:(kt + 1) * P],
                                              w[:, wb, kt, h * BANK:(h + 1) * BANK],
                                              start=(kt == 0 and (wa, wb) == PASSES[0]),
                                              stop=(kt == KT - 1 and (wa, wb) == PASSES[-1]))
                    return mm

                def tile(n, s):
                    pe.wait_ge(a_lo, n + 1)
                    pe.wait_ge(sum_ready, n + 1)
                    for h in range(2):
                        for kt in range(KT):
                            mm = products(s, h, kt)
                    mm.then_inc(y_ready, 1)

                if mask is not None:
                    pe.wait_ge(same_ready, 1 + P // BLK)
                    block_sums(0)
                    block_sums(1)
                    pe.wait_ge(a_lo, 2)
                    for kt in range(KT):
                        if kt + 2 < KT:
                            block_sums(kt + 2)
                        pe.wait_ge(w_lo, kt + 1)
                        for s in range(2):
                            for h in range(2):
                                mm = products(s, h, kt)
                            if kt == KT - 1:
                                mm.then_inc(y_ready, 1)
                else:
                    for s in range(2):
                        tile(s, s)
                with pe.Fori(1, TILES // 2) as j:
                    for s in range(2):
                        tile(j * 2 + s, s)


NF4 = np.array([-1.0, -0.6961928009986877, -0.5250730514526367, -0.39491748809814453, -0.28444138169288635,
                -0.18477343022833334, -0.09105003625154495, 0.0, 0.07958029955625534, 0.16093020141124725,
                0.24611230194568634, 0.33791524171829224, 0.44070982933044434, 0.5626170039176941,
                0.7229568362236023, 1.0], np.float32)
NF4_ZERO = 7


def nf4_lines():
    def line(code, sign, values):
        x0 = code - NF4_ZERO
        slope = np.float64(values[1]) - np.float64(values[0])
        best = None
        for i in range(-64, 65):
            scale = np.float32(slope + i * np.float64(np.spacing(np.float32(slope))))
            for k in range(-8, 9):
                shift = np.float32(np.float64(values[0]) - np.float64(scale) * x0)
                shift = np.float32(shift + k * np.float64(np.spacing(shift)))
                got = [np.float32(np.float64(scale) * (x0 + n) + np.float64(shift)) for n in range(2)]
                miss = sum(abs(np.float64(g) - np.float64(v)) for g, v in zip(got, values))
                if best is None or miss < best[0]:
                    best = (miss, float(scale), float(shift))
        return best[1:]
    above = [line(c, 1, NF4[c:c + 2]) for c in (14, 12, 10, 8)]
    below = [line(c, -1, -NF4[c:c + 2]) for c in (0, 2, 4)]
    below.append(line(6, -1, [-NF4[6], np.float32(-1e-3)]))
    x = np.arange(16) - NF4_ZERO
    value = lambda lines: np.max([[np.float32(np.float64(np.float32(a)) * v + np.float64(np.float32(b))) for v in x]
                                  for a, b in lines] + [np.zeros(16)], axis=0)
    assert np.array_equal(np.float32(value(above)) - np.float32(value(below)), NF4)
    return above, below


class TokenTranspose:
    PAIRS = TILES // 2

    def __init__(self, nc, ctx, tag, x, xT, ident, xn, ps):
        sem = lambda name: ctx.enter_context(nc.semaphore(f"{tag}_{name}"))
        self.nc, self.x, self.xT, self.ident, self.xn, self.ps = nc, x, xT, ident, xn, ps
        self.loaded = [sem(f"x_loaded{s}") for s in range(2)]
        self.turned, self.hi_ready, self.lo_ready = sem("turned"), sem("hi_ready"), sem("lo_ready")

    def psum(self, s):
        return self.ps[s].rearrange("p m (k t) -> p m k t", t=P)

    def part(self, comp, n):
        return self.xT[:, comp, :, bass.ds(n * P, P)].rearrange("p (m k) t -> p m k t", m=2)

    def load(self, sp, j, slot):
        for s in range(2):
            sp.dma_start(self.xn[2 * slot + s], one(self.x[bass.ds(j * 2 + s, 1)])).then_inc(self.loaded[slot], 16)

    def sync_first(self, sp):
        self.load(sp, 0, 0)

    def sync_rest(self, sp):
        self.load(sp, 1, 1)
        with sp.Fori(1, self.PAIRS // 2) as i:
            for slot in range(2):
                sp.wait_ge(self.turned, i * 4 + 2 * slot - 2)
                self.load(sp, i * 2 + slot, slot)

    def tensor_pair(self, pe, j, slot, loads):
        pe.wait_ge(self.loaded[slot], loads * 32)
        for s in range(2):
            pe.wait_ge(self.lo_ready, j * 2 + s + 1)
            for kt in range(KT):
                mm = self.nc.tensor.transpose(self.ps[s][:, kt // 4, kt % 4 * P:(kt % 4 + 1) * P],
                                              self.xn[2 * slot + s][:, kt * P:(kt + 1) * P], self.ident[:])
            mm.then_inc(self.turned, 1)

    def scalar_pair(self, act, j):
        for s in range(2):
            act.wait_ge(self.turned, j * 2 + s + 1)
            self.nc.scalar.copy(self.part(HI, j * 2 + s), self.psum(s)).then_inc(self.hi_ready, 1)

    def free(self, dve):
        dve.sem_inc(self.lo_ready, SLOTS)

    def vector_pair(self, dve, j):
        for s in range(2):
            dve.wait_ge(self.hi_ready, j * 2 + s + 1)
            self.nc.vector.tensor_tensor(self.part(LO, j * 2 + s), self.psum(s),
                                         self.part(HI, j * 2 + s).bitcast(F32), ALU.subtract).then_inc(self.lo_ready, 1)

    def wait_tiles(self, pe, n):
        pe.wait_ge(self.lo_ready, n + SLOTS)


GATE, UP, DOWN = range(3)


class Nf4Decoder:
    HALVES = 6

    def __init__(self, nc, ctx, codes, scales, down_w):
        sb = lambda name, shape, dt=F32: ctx.enter_context(nc.sbuf_tensor(f"nf4_{name}", shape, dt))
        sem = lambda name: ctx.enter_context(nc.semaphore(f"nf4_{name}"))
        self.nc, self.codes, self.scales, self.down_w = nc, codes, scales, down_w
        self.code = sb("code", [P, 2, D], I32)
        self.scale = sb("scale", [P, 2, D])
        line = sb("line", [P, 3, D])
        self.above, self.below = sb("above", [P, D]), sb("below", [P, D])
        self.w = sb("w", [P, 2, 2, 2, D], F32R)
        self.code_loaded = [sem(f"code_loaded{s}") for s in range(2)]
        self.scale_loaded = [sem(f"scale_loaded{s}") for s in range(2)]
        self.centered = sem("centered")
        self.line_ready = sem("line_ready")
        self.folded = sem("folded")
        self.w_hi, self.w_lo = sem("w_hi"), sem("w_lo")
        self.down_stored = sem("down_stored")
        self.up_ready = sem("up_ready")
        hi_lines, lo_lines = nf4_lines()
        self.lines = hi_lines + lo_lines
        self.shifts = sb("shifts", [P, len(self.lines)])
        self.shifts_set = sem("shifts_set")
        self.places = [self.above[:], line[:, 0, :], line[:, 1, :], line[:, 2, :],
                       self.below[:], line[:, 0, :], line[:, 1, :], line[:, 2, :]]

    def load_code(self, sp, c, m, slot):
        sp.dma_start(self.code[:, slot, :], one(self.codes[m][bass.ds(c, 1)])).then_inc(self.code_loaded[slot], 16)

    def load_scale(self, sp, c, m, slot):
        for h in range(2):
            dst = self.scale[64 * h:64 * h + 64, slot, :]
            if m == DOWN:
                src = self.scales[m][bass.ds(c, 1), h, :].to_broadcast([64, D])
                sp.dma_start(dst, src).then_inc(self.scale_loaded[slot], 16)
            else:
                src = self.scales[m][bass.ds(c, 1), h].to_broadcast([64, KT, P])
                sp.dma_start(dst.rearrange("p (k i) -> p k i", k=KT), src).then_inc(self.scale_loaded[slot], 16)

    def after_unit(self, sp, c, m, slot, k, load=True):
        c2, m2 = c + (m + 2) // 3, (m + 2) % 3
        if load:
            sp.wait_ge(self.line_ready, k * 8 + 8)
            self.load_code(sp, c2, m2, slot)
        if m == DOWN:
            sp.wait_ge(self.folded, k * 8 + 8)
            sp.dma_start(one(self.down_w[bass.ds(c, 1)]), self.scale[:, slot, :]).then_inc(self.down_stored, 16)
            sp.wait_ge(self.down_stored, c * 16 + 16)
        else:
            sp.wait_ge(self.w_lo, c * 2 + m + 1)
        if load:
            self.load_scale(sp, c2, m2, slot)

    def unit_scalar(self, act, k, slot, lines=range(8)):
        act.wait_ge(self.centered, k + 1)
        for i in lines:
            a = self.lines[i][0]
            if i == 0 and not (isinstance(k, int) and k == 0):
                act.wait_ge(self.folded, k * 8)
            if i >= 5:
                act.wait_ge(self.folded, k * 8 + i - 4)
            x = self.code[:, slot, :].bitcast(F32)
            func = ACT.Relu if i in (0, 4) else ACT.Identity
            self.nc.scalar.activation(self.places[i], x, func, bias=self.shifts[:, i:i + 1],
                                      scale=a).then_inc(self.line_ready, 1)

    def center(self, dve, k, slot, loads):
        dve.wait_ge(self.code_loaded[slot], loads * 16)
        self.nc.vector.tensor_scalar(self.code[:, slot, :].bitcast(F32), self.code[:, slot, :], float(NF4_ZERO), None,
                                     ALU.subtract).then_inc(self.centered, 1)

    def maxima(self, dve, k, lines=range(1, 7)):
        v, above, below, folded = self.nc.vector, self.above, self.below, self.folded
        for m in lines:
            i = m if m < 4 else m + 1
            into = above if m < 4 else below
            dve.wait_ge(self.line_ready, k * 8 + i + 1)
            if m > 1:
                dve.wait_ge(folded, k * 8 + m - 1)
            v.tensor_tensor(into[:], into[:], self.places[i], ALU.max).then_inc(folded, 1)

    def scaled(self, dve, k, slot, loads):
        v, above, below, folded = self.nc.vector, self.above, self.below, self.folded
        dve.wait_ge(folded, k * 8 + 6)
        v.tensor_tensor(above[:], above[:], below[:], ALU.subtract).then_inc(folded, 1)
        dve.wait_ge(folded, k * 8 + 7)
        dve.wait_ge(self.scale_loaded[slot], loads * 32)
        v.tensor_tensor(self.scale[:, slot, :], above[:], self.scale[:, slot, :], ALU.mult).then_inc(folded, 1)

    def split(self, dve, c, m, slot, odd, k):
        v, w = self.nc.vector, self.w
        dve.wait_ge(self.folded, k * 8 + 8)
        if not (isinstance(c, int) and c < 2):
            dve.wait_ge(self.up_ready, (c - 1) * BATCH)
        v.tensor_copy(w[:, odd, m, HI, :], self.scale[:, slot, :]).then_inc(self.w_hi, 1)
        dve.wait_ge(self.w_hi, c * 2 + m + 1)
        v.tensor_tensor(w[:, odd, m, LO, :], self.scale[:, slot, :], w[:, odd, m, HI, :].bitcast(F32),
                        ALU.subtract).then_inc(self.w_lo, 1)

    def unit_vector(self, dve, c, m, odd, slot, k, loads, next_loads, more=True, folded=False):
        if not folded:
            self.maxima(dve, k)
        self.scaled(dve, k, slot, loads)
        if more:
            self.center(dve, k + 1, 1 - slot, next_loads)
        if m != DOWN:
            self.split(dve, c, m, slot, odd, k)


    def sync(self, sp, h):
        k = h // 2
        if h == 0:
            for m in (GATE, UP):
                self.load_code(sp, 0, m, m)
                self.load_scale(sp, 0, m, m)
        elif h % 2 == 0:
            self.after_unit(sp, 0, k - 1, (k - 1) % 2, k - 1)

    def scalar(self, act, h):
        if h == 0:
            act.wait_ge(self.shifts_set, len(self.lines))
        self.unit_scalar(act, h // 2, h // 2 % 2, range(4 * (h % 2), 4 * (h % 2) + 4))

    def vector(self, dve, h, s):
        k = h // 2
        if h == 0 and s == 0:
            for i, (a, b) in enumerate(self.lines):
                self.nc.vector.memset(self.shifts[:, i:i + 1], b).then_inc(self.shifts_set, 1)
            self.center(dve, 0, 0, 1)
        if s == 0:
            self.maxima(dve, k, range(3 * (h % 2) + 1, 3 * (h % 2) + 4))
        elif h % 2 == 1:
            self.unit_vector(dve, 0, k, 0, k % 2, k, k // 2 + 1, (k + 1) // 2 + 1, folded=True)


def ffn_up(nc, x, ident, decoder, inter):
    with ExitStack() as ctx:
        sb = lambda name, shape, dt=F32: ctx.enter_context(nc.sbuf_tensor(f"up_{name}", shape, dt))
        sem = lambda name: ctx.enter_context(nc.semaphore(f"up_{name}"))
        xT = sb("xT", [P, 2, KT, T], F32R)
        act_g = sb("act_g", [P, 2, BANK])
        prod = sb("prod", [P, 2, BANK])
        ps = ctx.enter_context(nc.psum_tensor("up_ps", [P, 2, BATCH, BANK], F32))
        w, w_lo, up_ready = decoder.w, decoder.w_lo, decoder.up_ready
        gate_ready = sem("gate_ready")
        silu_ready, prod_ready = sem("silu_ready"), sem("prod_ready")
        prod_stored = [sem(f"prod_stored{s}") for s in range(2)]
        turn = TokenTranspose(nc, ctx, "t1", x, xT, ident,
                              [w[:, 1, m, comp, :].bitcast(F32) for m in range(2) for comp in range(2)],
                              [ps[:, m, 2:4, :] for m in range(2)])
        HALF = P // 2
        PS_FREE = BATCH

        with nc.Block() as block:
            @block.sync
            def _(sp):
                def store(c, tb):
                    sp.wait_ge(prod_ready, c * BATCH + tb + 1 + PS_FREE)
                    sp.dma_start(inter[bass.ds(c, 1), tb].rearrange("a p n -> p (a n)"),
                                 prod[:, tb % 2, :]).then_inc(prod_stored[tb % 2], 16)

                def chunk(c, odd, units, loads=3):
                    for tb in range(BATCH):
                        if tb < 3 and units:
                            decoder.after_unit(sp, c + 1, tb, (odd + 1 + tb) % 2, (c + 1) * 3 + tb, load=tb < loads)
                        store(c, tb)
                turn.sync_first(sp)
                turn.sync_rest(sp)
                with sp.Fori(0, CH // 2 - 1) as j:
                    chunk(j * 2, 0, True)
                    chunk(j * 2 + 1, 1, True)
                chunk(CH - 2, 0, True, loads=1)
                chunk(CH - 1, 1, False)
                for s in range(2):
                    sp.wait_ge(prod_stored[s], 16 * (CH * 2 + 1))

            @block.scalar
            def _(act):
                def silu(c, tb):
                    act.wait_ge(gate_ready, c * BATCH + tb + 1)
                    act.wait_ge(prod_ready, c * BATCH + tb - 1 + PS_FREE)
                    nc.scalar.activation(act_g[:, tb % 2, :], ps[:, GATE, tb, :], ACT.Silu).then_inc(silu_ready, 1)

                def chunk(c, odd, units):
                    for tb in range(BATCH):
                        if tb < 3 and units:
                            decoder.unit_scalar(act, (c + 1) * 3 + tb, (odd + 1 + tb) % 2)
                        silu(c, tb)
                with act.Fori(0, turn.PAIRS) as j:
                    turn.scalar_pair(act, j)
                with act.Fori(0, CH // 2 - 1) as j:
                    chunk(j * 2, 0, True)
                    chunk(j * 2 + 1, 1, True)
                chunk(CH - 2, 0, True)
                for tb in range(BATCH):
                    act.wait_ge(gate_ready, (CH - 1) * BATCH + tb + 1)
                    act.wait_ge(prod_ready, (CH - 1) * BATCH + tb - 1 + PS_FREE)
                    for q in range(0, HALF, 32):
                        g = nc.scalar.activation(act_g[HALF + q:HALF + q + 32, tb % 2, :], ps[q:q + 32, GATE, tb, :], ACT.Silu)
                    g.then_inc(silu_ready, 1)

            @block.vector
            def _(dve):
                v = nc.vector
                dve.sem_inc(prod_ready, PS_FREE)
                for s in range(2):
                    dve.sem_inc(prod_stored[s], 16)

                def product(c, tb, stores):
                    s = tb % 2
                    dve.wait_ge(silu_ready, c * BATCH + tb + 1)
                    dve.wait_ge(up_ready, c * BATCH + tb + 1)
                    dve.wait_ge(prod_stored[s], stores * 16)
                    v.tensor_tensor(prod[:, s, :], act_g[:, s, :], ps[:, UP, tb, :], ALU.mult).then_inc(prod_ready, 1)

                def chunk(c, odd, units, half):
                    for tb in range(BATCH):
                        if tb < 3 and units:
                            rest = 3 * odd + 3 + tb
                            decoder.unit_vector(dve, c + 1, tb, 1 - odd, rest % 2, half * 6 + rest, half * 3 + rest // 2 + 1,
                                                half * 3 + (rest + 1) // 2 + 1,
                                                more=not (isinstance(c, int) and c == CH - 2 and tb == 2))
                        product(c, tb, half * 4 + 2 * odd + tb // 2 + 1)
                turn.free(dve)
                with dve.Fori(0, turn.PAIRS) as j:
                    turn.vector_pair(dve, j)
                chunk(0, 0, True, 0)
                chunk(1, 1, True, 0)
                with dve.Fori(1, CH // 2 - 1) as j:
                    chunk(j * 2, 0, True, j)
                    chunk(j * 2 + 1, 1, True, j)
                chunk(CH - 2, 0, True, CH // 2 - 1)
                for tb in range(BATCH):
                    s, n = tb % 2, (CH - 1) * BATCH + tb
                    dve.wait_ge(silu_ready, n + 1)
                    dve.wait_ge(prod_stored[s], (n // 2 + 1) * 16)
                    if tb < 2:
                        v.memset(prod[0:HALF, s, :], 0.0)
                    v.tensor_tensor(prod[HALF:P, s, :], act_g[HALF:P, s, :], ps[HALF:P, GATE, tb, :],
                                    ALU.mult).then_inc(prod_ready, 1)

            @block.tensor
            def _(pe):
                def chunk(c, odd, last=False):
                    pe.wait_ge(w_lo, c * 2 + (1 if last else 2))
                    for tb in range(BATCH):
                        pe.wait_ge(prod_ready, c * BATCH + tb + 1)
                        for m, ready in ((GATE, gate_ready), (UP, up_ready)):
                            if last and m == UP:
                                continue
                            for kt in range(KT):
                                for wa, wb in PASSES:
                                    mm = nc.tensor.matmul(ps[:, m, tb, :], w[:, odd, m, wa, kt * P:(kt + 1) * P],
                                                          xT[:, wb, kt, tb * BANK:(tb + 1) * BANK],
                                                          start=(kt == 0 and (wa, wb) == PASSES[0]),
                                                          stop=(kt == KT - 1 and (wa, wb) == PASSES[-1]))
                            mm.then_inc(ready, 1)
                with pe.Fori(0, turn.PAIRS // 2) as i:
                    for slot in range(2):
                        turn.tensor_pair(pe, i * 2 + slot, slot, i + 1)
                turn.wait_tiles(pe, TILES)
                with pe.Fori(0, CH // 2 - 1) as j:
                    chunk(j * 2, 0)
                    chunk(j * 2 + 1, 1)
                chunk(CH - 2, 0)
                chunk(CH - 1, 1, last=True)


def ffn_down(nc, inter, weight, resid, out, seen):
    with ExitStack() as ctx:
        sb = lambda name, shape, dt=F32: ctx.enter_context(nc.sbuf_tensor(f"down_{name}", shape, dt))
        sem = lambda name: ctx.enter_context(nc.semaphore(f"down_{name}"))
        w = sb("w", [P, 2, CH, D], F32R)
        w_raw = sb("w_raw", [P, 2, D])
        a_raw = sb("a_raw", [P, 2, BANK])
        a = sb("a", [P, 2, 2, BANK], F32R)
        r = sb("r", [P, 4, D])
        ps = ctx.enter_context(nc.psum_tensor("down_ps", [P, 4, D], F32))
        w_loaded = [sem(f"w_loaded{s}") for s in range(2)]
        w_hi, w_lo = sem("w_hi"), sem("w_lo")
        a_loaded = [sem(f"a_loaded{s}") for s in range(2)]
        a_hi, a_lo = sem("a_hi"), sem("a_lo")
        r_loaded = [sem(f"r_loaded{t}") for t in range(4)]
        used = sem("used")
        y_ready = sem("y_ready")
        sum_ready = sem("sum_ready")
        stored = [sem(f"stored{t}") for t in range(4)]
        ln = LayerNorm(nc, ctx, "down_ln", sum_ready, seen, base=4, slots=4, in_place=True)
        HEAD = 12
        NORM_AT, STORE_AT, RESID_AT = 2, 3, 8

        def over_k(eng, step, first):
            for k in range(HEAD):
                step(k, k % 2, k // 2, first)
            with eng.Fori(HEAD // 2, CH // 2) as j:
                for s in range(2):
                    step(j * 2 + s, s, j, first)

        with nc.Block() as block:
            @block.sync
            def _(sp):
                def block_of(tb, first):
                    def step(k, s, pair, first):
                        if first:
                            if not (isinstance(k, int) and k < 2):
                                sp.wait_ge(w_lo, k - 1)
                            sp.dma_start(w_raw[:, s, :], one(weight[bass.ds(k, 1)])).then_inc(w_loaded[s], 16)
                        if not (first and isinstance(k, int) and k < 2):
                            sp.wait_ge(a_lo, tb * CH + k - 1)
                        sp.dma_start(a_raw[:, s, :], inter[bass.ds(k, 1), bass.ds(tb, 1)].rearrange("a b p n -> p (a b n)")
                                     ).then_inc(a_loaded[s], 16)
                        if isinstance(k, int) and not first and STORE_AT <= k < STORE_AT + 4:
                            store(tb - 1, k - STORE_AT)
                        if isinstance(k, int) and RESID_AT <= k < RESID_AT + 4:
                            t = k - RESID_AT
                            if not first:
                                sp.wait_ge(stored[t], tb * 16)
                            sp.dma_start(r[:, t, :], one(resid[bass.ds(tb * 4 + t, 1)])).then_inc(r_loaded[t], 16)
                    over_k(sp, step, first)

                def store(tb, t):
                    sp.wait_ge(ln.x_ready, tb * 4 + t + 1)
                    sp.dma_start(one(out[bass.ds(tb * 4 + t, 1)]), r[:, t, :]).then_inc(stored[t], 16)

                block_of(0, True)
                with sp.Fori(1, BATCH) as tb:
                    block_of(tb, False)
                for t in range(4):
                    store(BATCH - 1, t)
                for t in range(4):
                    sp.wait_ge(stored[t], BATCH * 16)

            @block.scalar
            def _(act):
                def block_of(tb, first):
                    def step(k, s, pair, first):
                        if first:
                            act.wait_ge(w_loaded[s], pair * 16 + 16)
                            nc.scalar.copy(w[:, HI, bass.ds(k, 1), :].rearrange("p a n -> p (a n)"), w_raw[:, s, :]).then_inc(w_hi, 1)
                        act.wait_ge(a_loaded[s], (tb * (CH // 2) + pair) * 16 + 16)
                        act.wait_ge(used, tb * CH + k + 1)
                        nc.scalar.copy(a[:, s, HI, :], a_raw[:, s, :]).then_inc(a_hi, 1)
                        if isinstance(k, int) and not first and NORM_AT <= k < NORM_AT + 4:
                            ln.scalar(act, tb * 4 - 4 + k - NORM_AT, k - NORM_AT, r[:, k - NORM_AT, :])
                    over_k(act, step, first)
                block_of(0, True)
                with act.Fori(1, BATCH) as tb:
                    block_of(tb, False)
                for t in range(4):
                    ln.scalar(act, (BATCH - 1) * 4 + t, t, r[:, t, :])

            @block.vector
            def _(dve):
                def add(n, t, loads):
                    dve.wait_ge(r_loaded[t], loads * 16)
                    dve.wait_ge(y_ready, n + 1)
                    nc.vector.tensor_tensor(r[:, t, :], ps[:, t, :], r[:, t, :], ALU.add).then_inc(sum_ready, 1)

                def block_of(tb, first):
                    def step(k, s, pair, first):
                        if first:
                            dve.wait_ge(w_hi, k + 1)
                            lo = w[:, LO, bass.ds(k, 1), :].rearrange("p a n -> p (a n)")
                            hi = w[:, HI, bass.ds(k, 1), :].rearrange("p a n -> p (a n)").bitcast(F32)
                            nc.vector.tensor_tensor(lo, w_raw[:, s, :], hi, ALU.subtract).then_inc(w_lo, 1)
                        dve.wait_ge(a_hi, tb * CH + k + 1)
                        nc.vector.tensor_tensor(a[:, s, LO, :], a_raw[:, s, :], a[:, s, HI, :].bitcast(F32),
                                                ALU.subtract).then_inc(a_lo, 1)
                        if isinstance(k, int) and not first:
                            if k == 0:
                                for t in range(4):
                                    add(tb * 4 - 4 + t, t, tb)
                            if NORM_AT <= k + 1 < NORM_AT + 4:
                                ln.vector(dve, tb * 4 - 4 + k + 1 - NORM_AT, k + 1 - NORM_AT, r[:, k + 1 - NORM_AT, :])
                    over_k(dve, step, first)
                dve.sem_inc(sum_ready, 4)
                block_of(0, True)
                with dve.Fori(1, BATCH) as tb:
                    block_of(tb, False)
                for t in range(4):
                    add((BATCH - 1) * 4 + t, t, BATCH)
                for t in range(4):
                    ln.vector(dve, (BATCH - 1) * 4 + t, t, r[:, t, :])

            @block.tensor
            def _(pe):
                pe.sem_inc(used, SLOTS)

                def products(tb, k, s, start, last, first):
                    pe.wait_ge(a_lo, tb * CH + k + 1)
                    if first:
                        pe.wait_ge(w_lo, k + 1)
                    for t in range(4):
                        if start:
                            pe.wait_ge(sum_ready, tb * 4 + t + 1)
                        for h in range(2):
                            for wa, wb in PASSES:
                                rhs = w[:, wb, bass.ds(k, 1), h * BANK:(h + 1) * BANK].rearrange("p a n -> p (a n)")
                                mm = nc.tensor.matmul(ps[:, t, h * BANK:(h + 1) * BANK], a[:, s, wa, t * P:(t + 1) * P], rhs,
                                                      start=(start and (wa, wb) == PASSES[0]),
                                                      stop=(last and (wa, wb) == PASSES[-1]))
                        if last and t < 3:
                            mm.then_inc(y_ready, 1)
                    if last:
                        mm.then_inc(y_ready, 1)
                        pe.wait_ge(y_ready, tb * 4 + 4)
                        pe.sem_inc(used, 1)
                    else:
                        mm.then_inc(used, 1)

                def block_of(tb, first):
                    products(tb, 0, 0, True, False, first)
                    products(tb, 1, 1, False, False, first)
                    with pe.Fori(1, CH // 2 - 1) as j:
                        products(tb, j * 2, 0, False, False, first)
                        products(tb, j * 2 + 1, 1, False, False, first)
                    products(tb, CH - 2, 0, False, False, first)
                    products(tb, CH - 1, 1, False, True, first)
                block_of(0, True)
                with pe.Fori(1, BATCH) as tb:
                    block_of(tb, False)


def project_qkv(nc, x, ident, weight, tables, out, v_out):
    UNITS = 2 * QK_GROUPS
    V_UNITS = QK_GROUPS
    with ExitStack() as ctx:
        sb = lambda name, shape, dt=F32: ctx.enter_context(nc.sbuf_tensor(f"qk_{name}", shape, dt))
        sem = lambda name: ctx.enter_context(nc.semaphore(f"qk_{name}"))
        xT = sb("xT", [P, 2, KT, T], F32R)
        w_raw = sb("w_raw", [P, KT * 2 * P])
        w = sb("w", [P, 2, 2, KT, 2, P], F32R)
        table = sb("table", [P, 2, 2, SEQ])
        t = sb("t", [P, 4, SEQ])
        o = sb("o", [P, 2, 2, 2, SEQ], F32R)
        ps = ctx.enter_context(nc.psum_tensor("qk_ps", [P, 2, 2, BANK], F32))
        ps_t = ctx.enter_context(nc.psum_tensor("qk_ps_t", [P, 2, 2, BANK], F32))
        AHEAD = 2
        turn = TokenTranspose(nc, ctx, "t2", x, xT, ident,
                              [w[:, 1, comp].bitcast(F32).rearrange("p k a i -> p (k a i)")[:, h * D:(h + 1) * D]
                               for comp in range(2) for h in range(2)],
                              [ps_t[:, s] for s in range(2)])
        table_loaded = sem("table_loaded")
        w_loaded, w_hi, w_lo = sem("w_loaded"), sem("w_hi"), sem("w_lo")
        y_ready = sem("y_ready")
        turned = sem("turned")
        out_hi, out_lo = sem("out_hi"), sem("out_lo")
        v_taken = [sem(f"v_taken{h}") for h in range(2)]
        stored = [sem(f"stored{s}") for s in range(2)]
        W_FREE = 2 * BATCH
        PS_FREE = 2 * 6
        T_FREE = 2
        V_FREE = 2
        QK_BATCHES, V_BATCHES = UNITS * BATCH, V_UNITS * BATCH
        QK_STORED = (QK_BATCHES // 2 + 1) * 64

        def v_part(s, bank):
            return o[:, s, HI, bank, :].bitcast(F32)

        with nc.Block() as block:
            @block.sync
            def _(sp):
                turn.sync_first(sp)
                sp.dma_start(w_raw[:], weight[0]).then_inc(w_loaded, 16)
                turn.sync_rest(sp)

                def load_next(u):
                    sp.wait_ge(w_lo, u + 1)
                    sp.dma_start(w_raw[:], one(weight[bass.ds(u + 1, 1)])).then_inc(w_loaded, 16)

                def unit(u):
                    load_next(u)
                    for b in range(BATCH):
                        n, s = u * BATCH + b, b % 2
                        sp.wait_ge(out_lo, n * 2 + 2 + T_FREE)
                        for comp in range(2):
                            for ab in range(2):
                                sp.dma_start(out[bass.ds(u, 1), b, :, comp, ab].rearrange("a h j n -> (a h) j n"),
                                             o[:, s, comp, ab, :].bitcast(F32)).then_inc(stored[s], 16)

                def v_unit(u, last=False):
                    if not last:
                        load_next(u + UNITS)
                    for b in range(BATCH):
                        for bank in range(2):
                            sp.wait_ge(v_taken[bank], u * BATCH + b + 1 + V_FREE)
                        sp.dma_start(v_out[bass.ds(u, 1), b].rearrange("a t p c -> p (a t) c"),
                                     o[:, b % 2, HI].bitcast(F32).rearrange("p a (t c) -> p (a t) c", t=2)
                                     ).then_inc(stored[b % 2], 16)
                with sp.Fori(0, UNITS) as u:
                    unit(u)
                with sp.Fori(0, V_UNITS - 1) as u:
                    v_unit(u)
                v_unit(V_UNITS - 1, last=True)
                for s in range(2):
                    sp.wait_ge(stored[s], QK_STORED + V_BATCHES // 2 * 16)

            @block.scalar
            def _(act):
                def split_hi(u, s):
                    act.wait_ge(w_loaded, u * 16 + 16)
                    act.wait_ge(y_ready, u * BATCH + BATCH)
                    nc.scalar.copy(w[:, s, HI].rearrange("p k a i -> p (k a i)"), w_raw[:]).then_inc(w_hi, 1)

                def outputs(u, b, stores):
                    n, s = u * BATCH + b, b % 2
                    for ab in range(2):
                        act.wait_ge(turned, n * 6 + 3 + 3 * ab + PS_FREE)
                        if ab == 0:
                            act.wait_ge(stored[s], stores * 64)
                        nc.scalar.copy(o[:, s, HI, ab, :], t[:, 2 * ab, :]).then_inc(out_hi, 1)

                def unit(u, s, first=False):
                    for b in range(BATCH):
                        if first and b < 3:
                            for half in range(2):
                                turn.scalar_pair(act, AHEAD + 2 * b + half)
                        outputs(u, b, u * 2 + b // 2 + 1)
                        if b == (2 if first else 0):
                            split_hi(u + 1, 1 - s)

                def v_unit(u, s, more=True):
                    for b in range(BATCH):
                        act.wait_ge(y_ready, (UNITS + u) * BATCH + b + 1 + W_FREE)
                        act.wait_ge(stored[b % 2], (u * 2 + b // 2) * 16 + QK_STORED)
                        nc.scalar.copy(v_part(b % 2, 0), ps[:, b % 2, 0, :]).then_inc(v_taken[0], 1)
                        if b == 0 and more:
                            split_hi(UNITS + u + 1, 1 - s)

                turn.scalar_pair(act, 0)
                act.dma_start(table[:], tables.rearrange("m i p n -> p m i n")).then_inc(table_loaded, 16)
                split_hi(0, 0)
                turn.scalar_pair(act, 1)
                unit(0, 0, first=True)
                unit(1, 1)
                with act.Fori(1, UNITS // 2) as j:
                    unit(j * 2, 0)
                    unit(j * 2 + 1, 1)
                with act.Fori(0, V_UNITS // 2 - 1) as j:
                    v_unit(j * 2, 0)
                    v_unit(j * 2 + 1, 1)
                v_unit(V_UNITS - 2, 0)
                v_unit(V_UNITS - 1, 1, more=False)

            @block.vector
            def _(dve):
                v = nc.vector

                def split_lo(u, s):
                    dve.wait_ge(w_hi, u + 1)
                    v.tensor_tensor(w[:, s, LO].rearrange("p k a i -> p (k a i)"), w_raw[:],
                                    w[:, s, HI].rearrange("p k a i -> p (k a i)").bitcast(F32),
                                    ALU.subtract).then_inc(w_lo, 1)

                def rotate(u, b, m):
                    n, s = u * BATCH + b, b % 2
                    dve.wait_ge(y_ready, n + 1 + W_FREE)
                    for ab in range(2):
                        dve.wait_ge(out_lo, n * 2 + ab - 1 + T_FREE)
                        v.tensor_tensor(t[:, 2 * ab, :], ps[:, s, 0, :], table[:, m, ab, :], ALU.mult).then_inc(turned, 1)
                        v.tensor_tensor(t[:, 2 * ab + 1, :], ps[:, s, 1, :], table[:, m, 1 - ab, :], ALU.mult).then_inc(turned, 1)
                        dve.wait_ge(turned, n * 6 + 3 * ab + 2 + PS_FREE)
                        v.tensor_tensor(t[:, 2 * ab, :], t[:, 2 * ab, :], t[:, 2 * ab + 1, :],
                                        ALU.add if ab else ALU.subtract).then_inc(turned, 1)
                    for ab in range(2):
                        dve.wait_ge(out_hi, n * 2 + ab + 1)
                        v.tensor_tensor(o[:, s, LO, ab, :], t[:, 2 * ab, :], o[:, s, HI, ab, :].bitcast(F32),
                                        ALU.subtract).then_inc(out_lo, 1)

                for s in range(2):
                    dve.sem_inc(stored[s], 64)
                dve.sem_inc(turned, PS_FREE)
                dve.sem_inc(out_lo, T_FREE)
                for bank in range(2):
                    dve.sem_inc(v_taken[bank], V_FREE)

                def unit(u, s, m, first=False):
                    for b in range(BATCH):
                        if first and b < 3:
                            for half in range(2):
                                turn.vector_pair(dve, AHEAD + 2 * b + half)
                        if first and b == 0:
                            dve.wait_ge(table_loaded, 16)
                        rotate(u, b, m)
                        if b == (2 if first else 0):
                            split_lo(u + 1, 1 - s)

                def v_unit(u, s, more=True):
                    for b in range(BATCH):
                        dve.wait_ge(y_ready, (UNITS + u) * BATCH + b + 1 + W_FREE)
                        dve.wait_ge(stored[b % 2], (u * 2 + b // 2) * 16 + QK_STORED)
                        v.tensor_copy(v_part(b % 2, 1), ps[:, b % 2, 1, :]).then_inc(v_taken[1], 1)
                        if b == 0 and more:
                            split_lo(UNITS + u + 1, 1 - s)

                turn.free(dve)
                turn.vector_pair(dve, 0)
                split_lo(0, 0)
                turn.vector_pair(dve, 1)
                unit(0, 0, 0, first=True)
                unit(1, 1, 0)
                with dve.Fori(1, QK_GROUPS // 2) as j:
                    unit(j * 2, 0, 0)
                    unit(j * 2 + 1, 1, 0)
                with dve.Fori(QK_GROUPS // 2, UNITS // 2) as j:
                    unit(j * 2, 0, 1)
                    unit(j * 2 + 1, 1, 1)
                with dve.Fori(0, V_UNITS // 2 - 1) as j:
                    v_unit(j * 2, 0)
                    v_unit(j * 2 + 1, 1)
                v_unit(V_UNITS - 2, 0)
                v_unit(V_UNITS - 1, 1, more=False)

            @block.tensor
            def _(pe):
                pe.sem_inc(y_ready, W_FREE)

                def unit(u, slot, first=False):
                    pe.wait_ge(w_lo, u + 1)
                    for b in range(BATCH):
                        n, s = u * BATCH + b, b % 2
                        if first:
                            turn.wait_tiles(pe, 4 * b + 4)
                        pe.wait_ge(turned, n * 6 + 6)
                        for ab in range(2):
                            for kt in range(KT):
                                for wa, wb in PASSES:
                                    mm = nc.tensor.matmul(ps[:, s, ab, :], w[:, slot, wa, kt, ab, :],
                                                          xT[:, wb, kt, b * BANK:(b + 1) * BANK],
                                                          start=(kt == 0 and (wa, wb) == PASSES[0]),
                                                          stop=(kt == KT - 1 and (wa, wb) == PASSES[-1]))
                            if ab == 1:
                                mm.then_inc(y_ready, 1)
                            if first and b < 3:
                                j = AHEAD + 2 * b + ab
                                turn.tensor_pair(pe, j, j % 2, j // 2 + 1)
                for j in range(AHEAD):
                    turn.tensor_pair(pe, j, j, 1)
                unit(0, 0, first=True)
                unit(1, 1)
                with pe.Fori(1, UNITS // 2) as j:
                    unit(j * 2, 0)
                    unit(j * 2 + 1, 1)
                pe.wait_ge(turned, QK_BATCHES * 6 + PS_FREE)
                with pe.Fori(0, V_UNITS // 2) as j:
                    for slot in range(2):
                        u = j * 2 + slot
                        pe.wait_ge(w_lo, UNITS + u + 1)
                        for b in range(BATCH):
                            for bank in range(2):
                                pe.wait_ge(v_taken[bank], u * BATCH + b + 1)
                                for half in range(2):
                                    at = b * BANK + (2 * bank + half) * P
                                    for kt in range(KT):
                                        for wa, wb in PASSES:
                                            mm = nc.tensor.matmul(ps[:, b % 2, bank, half * 2 * P:(half + 1) * 2 * P],
                                                                  xT[:, wa, kt, at:at + P],
                                                                  w[:, slot, wb, kt].rearrange("p a i -> p (a i)"),
                                                                  start=(kt == 0 and (wa, wb) == PASSES[0]),
                                                                  stop=(kt == KT - 1 and (wa, wb) == PASSES[-1]))
                            mm.then_inc(y_ready, 1)


def attention(nc, ident, ident_b, above_b, qk, v, out, side, seen):
    NS, HU = 16, 8
    N_HEADS = NS * HU
    QT = SEQ // P
    CAUSAL = P * (QT * (QT + 1) // 2)
    WIDE = 2 * P
    S_AT = (2 * BANK + WIDE, 2 * BANK, BANK, 0)
    S_BANKS = ((3,), (2,), (1, 0))
    N_AT = (0, 128, 384, 768)
    T_AT = (0, BANK, 2 * BANK, BANK + 3 * P)
    T_PARTS = ((0,), (1, 3, 2))
    with ExitStack() as ctx:
        sb = lambda name, shape, dt=F32: ctx.enter_context(nc.sbuf_tensor(f"at_{name}", shape, dt))
        sem = lambda name: ctx.enter_context(nc.semaphore(f"at_{name}"))
        qk_sb = sb("qk", [P, 2, 2, 2, SEQ], F32R)
        vc = sb("vc", [P, QT, 2 * P])
        vp = sb("vp", [P, 2, QT * 4 * P])
        prob = sb("prob", [P, 4, CAUSAL])
        pt = sb("pt", [P, 2, CAUSAL])
        ot = sb("ot", [P, 2, SEQ])
        top = sb("top", [P, 2, 4])
        total = sb("total", [P, 2, 4])
        inv = sb("inv", [P, 2, 4])
        ps_s = ctx.enter_context(nc.psum_tensor("at_s", [P, 3 * BANK], F32))
        ps_t = ctx.enter_context(nc.psum_tensor("at_t", [P, 3 * BANK], F32))
        ps_o = ctx.enter_context(nc.psum_tensor("at_o", [P, 2, BANK], F32))
        qk_loaded = [sem(f"qk_loaded{s}") for s in range(2)]
        v_loaded = sem("v_loaded")
        s_ready = sem("s_ready")
        top_ready = sem("top_ready")
        exp_ready = sem("exp_ready")
        inv_ready = sem("inv_ready")
        prob_act, prob_dve = sem("prob_act"), sem("prob_dve")
        turned = sem("turned")
        pt_act, pt_dve = sem("pt_act"), sem("pt_dve")
        zeros_set = sem("zeros_set")
        vp_ready = sem("vp_ready")
        head_done = sem("head_done")
        o_out = sem("o_out")
        stored = [sem(f"stored{s}") for s in range(2)]
        S_BASE, EXP_BASE, PT_BASE, DONE_BASE, O_BASE = 12, 3, 3, 8, 2

        def spread(slot):
            t = vp[:, slot, :]
            return bass.AP(t.tensor, t.offset, [list(t.ap[0]), [4 * P, QT], [P + HD, 4], [1, HD]])

        with nc.Block() as block:
            @block.sync
            def _(sp):
                def load_pair(n, p, s):
                    sp.wait_ge(s_ready, (n * 8 + 2 * p - 2) * 3 + S_BASE)
                    for m in range(2):
                        src = qk[m, bass.ds(n, 1), 2 * p:2 * p + 2].rearrange("a h c r t -> (a c) r h t")
                        for rows in range(4):
                            comp = rows % 2 if m == 0 else rows // 2
                            sp.dma_start(qk_sb[rows * HD:(rows + 1) * HD, s, m].bitcast(F32), src[comp]).then_inc(qk_loaded[s], 16)

                def load_v(n):
                    sp.dma_start(vc[:], v[bass.ds(n, 1)].rearrange("a k p c -> (a p) k c")).then_inc(v_loaded, 16)

                def store(n, gg):
                    sp.wait_ge(o_out, n * 2 + gg + 1 + O_BASE)
                    dst = out[bass.ds(n * QT, QT), :, gg * P:(gg + 1) * P].rearrange("t p i -> p t i")
                    sp.dma_start(dst, ot[:, gg, :].rearrange("p (t i) -> p t i", t=QT)).then_inc(stored[gg], 16)

                def eight(n, first=False, last=False):
                    def side_tiles(*tiles):
                        if first:
                            for k in tiles:
                                side.sync(sp, k)
                    load_pair(n, 2, 0)
                    side_tiles(1, 2)
                    load_pair(n, 3, 1)
                    side_tiles(3, 4)
                    if not first:
                        store(n - 1, 1)
                    if not last:
                        sp.wait_ge(vp_ready, n * 2 + 2)
                        load_v(n + 1)
                        load_pair(n + 1, 0, 0)
                        side_tiles(5, 6, 7)
                        load_pair(n + 1, 1, 1)
                    store(n, 0)

                load_pair(0, 0, 0)
                load_pair(0, 1, 1)
                load_v(0)
                side.sync(sp, 0, first=True)
                eight(0, first=True)
                with sp.Fori(1, NS - 1) as n:
                    eight(n)
                eight(NS - 1, last=True)
                store(NS - 1, 1)
                for s in range(2):
                    sp.wait_ge(stored[s], (NS + 1) * 16)

            @block.gpsimd
            def _(pool):
                g = nc.gpsimd
                g.memset(vp[:], 0.0).then_inc(zeros_set, 1)
                pool.wait_ge(zeros_set, 1)

                def spread_v(n, gg):
                    if gg == 0:
                        pool.wait_ge(v_loaded, n * 16 + 16)
                    pool.wait_ge(head_done, n * 8 + gg * 4 - 4 + DONE_BASE)
                    pool.sem_inc(seen, 1)
                    g.tensor_copy(spread(gg), vc[:, :, gg * P:(gg + 1) * P].rearrange(
                        "p k (j d) -> p k j d", j=4)).then_inc(vp_ready, 1)

                with pool.Fori(0, NS) as n:
                    for gg in range(2):
                        spread_v(n, gg)

            @block.scalar
            def _(act):
                a = nc.scalar

                def exponentials(n, hh):
                    s, i = hh % 2, n * 8 + hh
                    for bank, tiles in enumerate(S_BANKS):
                        act.wait_ge(top_ready, i * 3 + bank + 1)
                        for q in tiles:
                            e = a.activation(prob[:, hh % 4, N_AT[q]:N_AT[q] + (q + 1) * P], ps_s[:, S_AT[q]:S_AT[q] + (q + 1) * P],
                                             ACT.Exp, bias=top[:, s, q:q + 1], accum_out=total[:, s, q:q + 1])
                        e.then_inc(exp_ready, 1)

                def normalize(i, hh):
                    act.wait_ge(inv_ready, i + 1)
                    x = prob[:, hh % 4, N_AT[3]:CAUSAL]
                    a.activation(x, x, ACT.Copy, scale=inv[:, hh % 2, 3:4]).then_inc(prob_act, 1)

                def take_part(i, hh):
                    act.wait_ge(head_done, i - 1 + DONE_BASE)
                    act.wait_ge(turned, i * 2 + 1)
                    a.copy(pt[:, hh % 2, 0:BANK], ps_t[:, 0:BANK]).then_inc(pt_act, 1)

                def step(n, hh, first=False):
                    i = n * 8 + hh
                    if not first or hh >= 2:
                        take_part(i - 2, (hh - 2) % HU)
                    exponentials(n, hh)
                    if not first or hh >= 1:
                        normalize(i - 1, (hh - 1) % HU)
                for hh in range(HU):
                    step(0, hh, first=True)
                    side.scalar(act, hh)
                with act.Fori(1, NS) as n:
                    for hh in range(HU):
                        step(n, hh)
                take_part(N_HEADS - 2, 6)
                normalize(N_HEADS - 1, 7)
                take_part(N_HEADS - 1, 7)

            @block.vector
            def _(dve):
                v_ = nc.vector
                for s, start in ((s_ready, S_BASE), (exp_ready, EXP_BASE), (pt_act, PT_BASE), (pt_dve, PT_BASE),
                                 (head_done, DONE_BASE), (o_out, O_BASE), (stored[0], 16), (stored[1], 16)):
                    dve.sem_inc(s, start)

                def maxima(n, hh):
                    s, i = hh % 2, n * 8 + hh
                    for bank, tiles in enumerate(S_BANKS):
                        dve.wait_ge(s_ready, i * 3 + bank + 1 + S_BASE)
                        for q in tiles:
                            m = v_.reduce_max(top[:, s, q:q + 1], ps_s[:, S_AT[q]:S_AT[q] + (q + 1) * P], AX.X, negate=True)
                        m.then_inc(top_ready, 1)

                def normalize(i, hh):
                    dve.wait_ge(exp_ready, i * 3 + 3 + EXP_BASE)
                    v_.reciprocal(inv[:, hh % 2, :], total[:, hh % 2, :]).then_inc(inv_ready, 1)
                    dve.wait_ge(inv_ready, i + 1)
                    for q in range(3):
                        x = prob[:, hh % 4, N_AT[q]:N_AT[q] + (q + 1) * P]
                        m = v_.tensor_scalar(x, x, inv[:, hh % 2, q:q + 1], None, ALU.mult)
                    m.then_inc(prob_dve, 1)

                def take_part(i, hh):
                    dve.wait_ge(head_done, i - 1 + DONE_BASE)
                    dve.wait_ge(turned, i * 2 + 2)
                    v_.tensor_copy(pt[:, hh % 2, BANK:CAUSAL], ps_t[:, BANK:CAUSAL]).then_inc(pt_dve, 1)

                def take_out(n, gg):
                    dve.wait_ge(head_done, n * 8 + gg * 4 + 4 + DONE_BASE)
                    dve.wait_ge(stored[gg], n * 16 + 16)
                    v_.tensor_copy(ot[:, gg, :], ps_o[:, gg, :]).then_inc(o_out, 1)

                def step(n, hh, first=False):
                    i = n * 8 + hh
                    maxima(n, hh)
                    if not first or hh >= 1:
                        normalize(i - 1, (hh - 1) % HU)
                    if not first or hh >= 2:
                        take_part(i - 2, (hh - 2) % HU)
                    if hh == 3 and not first:
                        take_out(n - 1, 1)
                    if hh == 7:
                        take_out(n, 0)
                for hh in range(HU):
                    step(0, hh, first=True)
                    side.vector(dve, hh)
                with dve.Fori(1, NS) as n:
                    for hh in range(HU):
                        step(n, hh)
                normalize(N_HEADS - 1, 7)
                take_part(N_HEADS - 2, 6)
                take_part(N_HEADS - 1, 7)
                take_out(NS - 1, 1)

            @block.tensor
            def _(pe):
                def scores(n, hh):
                    i, slot = n * 8 + hh, (hh // 2) % 2
                    if hh % 2 == 0:
                        pe.wait_ge(qk_loaded[slot], (n * 2 + hh // 4 + 1) * 128)
                    for bank, tiles in enumerate(S_BANKS):
                        pe.wait_ge(exp_ready, (i - 1) * 3 + bank + 1 + EXP_BASE)
                        for q in tiles:
                            keys = (q + 1) * P
                            nc.tensor.matmul(ps_s[:, S_AT[q]:S_AT[q] + max(keys, WIDE)], qk_sb[:, slot, 0, hh % 2, q * P:keys],
                                             qk_sb[:, slot, 1, hh % 2, 0:max(keys, WIDE)], start=True, stop=True)
                            m = nc.tensor.matmul(ps_s[:, S_AT[q] + q * P:S_AT[q] + keys], ident_b[:], above_b[:], start=False,
                                                 stop=True, skip_group_check=True)
                        m.then_inc(s_ready, 1)

                def transposes(i, hh):
                    pe.wait_ge(prob_act, i + 1)
                    pe.wait_ge(prob_dve, i + 1)
                    for part, (tiles, taken) in enumerate(zip(T_PARTS, (pt_act, pt_dve))):
                        pe.wait_ge(taken, i + PT_BASE)
                        for k in tiles:
                            for q in range(k, QT):
                                at = T_AT[k] + (q - k) * P
                                m = nc.tensor.transpose(ps_t[:, at:at + P],
                                                        prob[:, hh % 4, N_AT[q] + k * P:N_AT[q] + (k + 1) * P], ident[:])
                        m.then_inc(turned, 1)

                def outputs(n, hh):
                    i, j, gg = n * 8 + hh, hh % 4, hh // 4
                    if j == 0:
                        pe.wait_ge(zeros_set, 1)
                        pe.wait_ge(vp_ready, n * 2 + gg + 1)
                        pe.wait_ge(o_out, n * 2 + gg - 1 + O_BASE)
                    pe.wait_ge(pt_act, i + 1 + PT_BASE)
                    pe.wait_ge(pt_dve, i + 1 + PT_BASE)
                    for k in range(QT):
                        m = nc.tensor.matmul(ps_o[:, gg, k * P:SEQ], vp[:, gg, (k * 4 + j) * P:(k * 4 + j + 1) * P],
                                             pt[:, hh % 2, T_AT[k]:T_AT[k] + (QT - k) * P],
                                             start=(j == 0 and k == 0), stop=(j == 3 and k == 3), skip_group_check=True)
                    m.then_inc(head_done, 1)

                def step(n, hh, first=False):
                    i = n * 8 + hh
                    scores(n, hh)
                    if not first or hh >= 2:
                        transposes(i - 2, (hh - 2) % HU)
                    if not first or hh >= 3:
                        outputs(n if hh >= 3 else n - 1, (hh - 3) % HU)
                for hh in range(HU):
                    step(0, hh, first=True)
                with pe.Fori(1, NS) as n:
                    for hh in range(HU):
                        step(n, hh)
                transposes(N_HEADS - 2, 6)
                outputs(NS - 1, 5)
                transposes(N_HEADS - 1, 7)
                outputs(NS - 1, 6)
                outputs(NS - 1, 7)


def make_constants(nc, ident, above, ident_b, above_b):
    with nc.semaphore("const_filled") as filled, nc.semaphore("const_shaped") as shaped, \
            nc.semaphore("const_ready") as ready, nc.Block() as block:
        @block.gpsimd
        def _(pool):
            nc.gpsimd.memset(ident[:], 0.0).then_inc(filled, 1)
            nc.gpsimd.memset(above[:], 0.0).then_inc(filled, 1)
            pool.wait_ge(filled, 2)
            nc.gpsimd.affine_select(out=ident[:], in_=ident[:], compare_op=ALU.not_equal, fill=1.0, base=0,
                                    pattern=[[-1, P]], channel_multiplier=1).then_inc(shaped, 1)
            nc.gpsimd.affine_select(out=above[:], in_=above[:], compare_op=ALU.is_ge, fill=MASKED, base=0,
                                    pattern=[[-1, P]], channel_multiplier=1).then_inc(shaped, 1)

        @block.vector
        def _(dve):
            dve.wait_ge(shaped, 2)
            nc.vector.tensor_copy(ident_b[:], ident[:]).then_inc(ready, 1)
            nc.vector.tensor_copy(above_b[:], above[:]).then_inc(ready, 1)

        @block.tensor
        def _(pe):
            pe.wait_ge(ready, 2)


def ffn_lora(nc, x, w, bias, lora_b, ident, out, seen):
    N_W, N_Q, N_H = D, EXPERTS * DK, EXPERTS * RANK
    Q_AT, H_AT, K_AT = N_W, N_W + N_Q, N_W + N_Q + N_H
    SCALE = float(1.0 / np.sqrt(np.float64(DK)))
    with ExitStack() as ctx:
        sb = lambda name, shape, dt=F32: ctx.enter_context(nc.sbuf_tensor(f"lora_{name}", shape, dt))
        sem = lambda name: ctx.enter_context(nc.semaphore(f"lora_{name}"))
        b = sb("b", [P, 2, D], F32R)
        b_raw = sb("b_raw", [P, D])
        bias_sb = sb("bias", [P, D])
        xn = sb("xn", [P, 2, D])
        xT = sb("xT", [P, 2, 2, KT * P], F32R)
        r = sb("r", [P, 2, D])
        prod = sb("prod", [P, N_Q])
        score = sb("score", [P, EXPERTS])
        small = sb("small", [P, 4])
        expert = sb("expert", [P, EXPERTS])
        h = sb("h", [P, N_H])
        hT = sb("hT", [P, 2, P], F32R)
        ps_y = ctx.enter_context(nc.psum_tensor("lora_ps_y", [P, 2, D], F32))
        ps_qh = ctx.enter_context(nc.psum_tensor("lora_ps_qh", [P, BANK], F32))
        ps_k = ctx.enter_context(nc.psum_tensor("lora_ps_k", [P, BANK], F32))
        ps_x = ctx.enter_context(nc.psum_tensor("lora_ps_x", [P, D], F32))
        ps_h = ps_k[:, N_Q:N_Q + P]
        b_loaded, b_hi, b_lo = sem("b_loaded"), sem("b_hi"), sem("b_lo")
        bias_loaded = sem("bias_loaded")
        x_loaded = [sem(f"x_loaded{s}") for s in range(2)]
        x_turned, x_hi, x_lo = sem("x_turned"), sem("x_hi"), sem("x_lo")
        r_ready = sem("r_ready")
        qhk_ready = sem("qhk_ready")
        chain = sem("chain")
        exp_ready = sem("exp_ready")
        weigh = sem("weigh")
        h_turned, h_hi, h_lo = sem("h_turned"), sem("h_hi"), sem("h_lo")
        y_ready, sum_ready = sem("y_ready"), sem("sum_ready")
        stored = [sem(f"stored{s}") for s in range(2)]
        ln = LayerNorm(nc, ctx, "lora_ln", sum_ready, seen, in_place=True)
        X_BASE = 2

        with nc.Block() as block:
            @block.sync
            def _(sp):
                def load_x(n, s):
                    sp.dma_start(xn[:, s, :], one(x[bass.ds(n, 1)])).then_inc(x_loaded[s], 16)
                for s in range(2):
                    load_x(s, s)
                sp.dma_start(b_raw[:], lora_b).then_inc(b_loaded, 16)
                sp.dma_start(bias_sb[:], bias.to_broadcast([P, D])).then_inc(bias_loaded, 16)

                def tile(n, s):
                    sp.wait_ge(x_turned, n - 1)
                    sp.wait_ge(r_ready, n - 1)
                    load_x(n, s)
                    sp.wait_ge(ln.x_ready, n - 1 + X_BASE)
                    sp.dma_start(one(out[bass.ds(n - 2, 1)]), r[:, s, :]).then_inc(stored[s], 16)
                with sp.Fori(1, TILES // 2) as j:
                    for s in range(2):
                        tile(j * 2 + s, s)
                for s in range(2):
                    sp.wait_ge(ln.x_ready, TILES - 1 + s + X_BASE)
                    sp.dma_start(out[TILES - 2 + s], r[:, s, :]).then_inc(stored[s], 16)
                for s in range(2):
                    sp.wait_ge(stored[s], 16 * (TILES // 2 + 1))

            @block.gpsimd
            def _(pool):
                for s in range(2):
                    pool.sem_inc(stored[s], 16)
                pool.wait_ge(bias_loaded, 16)
                with pool.Fori(0, TILES // 2) as j:
                    for s in range(2):
                        pool.wait_ge(x_loaded[s], j * 16 + 16)
                        pool.wait_ge(stored[s], j * 16 + 16)
                        pool.sem_inc(seen, 1)
                        nc.gpsimd.tensor_tensor(r[:, s, :], xn[:, s, :], bias_sb[:], ALU.add).then_inc(r_ready, 1)

            @block.scalar
            def _(act):
                a = nc.scalar
                act.sem_inc(ln.x_ready, X_BASE)

                def split_x(n, s):
                    act.wait_ge(x_turned, n + 1)
                    a.copy(xT[:, s, HI, :], ps_x[:]).then_inc(x_hi, 1)

                def tile(n, s, more=True):
                    if more:
                        split_x(n + 1, 1 - s)
                    act.wait_ge(chain, n * 4 + 4)
                    a.activation(expert[:], score[:], ACT.Exp, bias=small[:, 1:2], scale=SCALE,
                                 accum_out=small[:, 2:3]).then_inc(exp_ready, 1)
                    act.wait_ge(h_turned, n + 1)
                    a.copy(hT[:, HI, :], ps_h).then_inc(h_hi, 1)
                    ln.scalar(act, n, s, r[:, s, :])
                split_x(0, 0)
                act.wait_ge(b_loaded, 16)
                a.copy(b[:, HI, :], b_raw[:]).then_inc(b_hi, 1)
                with act.Fori(0, TILES // 2 - 1) as j:
                    for s in range(2):
                        tile(j * 2 + s, s)
                tile(TILES - 2, 0)
                tile(TILES - 1, 1, more=False)

            @block.vector
            def _(dve):
                v = nc.vector
                dve.sem_inc(sum_ready, SLOTS)

                def split_x(n, s):
                    dve.wait_ge(x_hi, n + 1)
                    v.tensor_tensor(xT[:, s, LO, :], ps_x[:], xT[:, s, HI, :].bitcast(F32), ALU.subtract).then_inc(x_lo, 1)

                def tile(n, s, more=True):
                    dve.wait_ge(qhk_ready, n + 1)
                    v.tensor_copy(prod[:], ps_k[:, 0:N_Q]).then_inc(chain, 1)
                    dve.wait_ge(chain, n * 4 + 1)
                    v.tensor_tensor(prod[:], ps_qh[:, 0:N_Q], prod[:], ALU.mult).then_inc(chain, 1)
                    dve.wait_ge(chain, n * 4 + 2)
                    v.reduce_sum(score[:], prod[:].rearrange("p (e d) -> p e d", e=EXPERTS), AX.X).then_inc(chain, 1)
                    dve.wait_ge(chain, n * 4 + 3)
                    v.reduce_max(small[:, 0:1], score[:], AX.X, negate=True).then_inc(weigh, 1)
                    dve.wait_ge(weigh, n * 4 + 1)
                    v.tensor_scalar(small[:, 1:2], small[:, 0:1], SCALE, None, ALU.mult).then_inc(chain, 1)
                    if more:
                        split_x(n + 1, 1 - s)
                    dve.wait_ge(exp_ready, n + 1)
                    v.reciprocal(small[:, 3:4], small[:, 2:3]).then_inc(weigh, 1)
                    dve.wait_ge(weigh, n * 4 + 2)
                    v.tensor_scalar(expert[:], expert[:], small[:, 3:4], None, ALU.mult).then_inc(weigh, 1)
                    dve.wait_ge(weigh, n * 4 + 3)
                    v.tensor_tensor(h[:].rearrange("p (e r) -> p e r", e=EXPERTS),
                                    ps_qh[:, N_Q:N_Q + N_H].rearrange("p (e r) -> p e r", e=EXPERTS),
                                    expert[:].unsqueeze(2).to_broadcast([P, EXPERTS, RANK]), ALU.mult).then_inc(weigh, 1)
                    dve.wait_ge(h_hi, n + 1)
                    v.tensor_tensor(hT[:, LO, :], ps_h, hT[:, HI, :].bitcast(F32), ALU.subtract).then_inc(h_lo, 1)
                    dve.wait_ge(r_ready, n + 1)
                    dve.wait_ge(y_ready, n + 1)
                    v.tensor_tensor(r[:, s, :], ps_y[:, s, :], r[:, s, :], ALU.add).then_inc(sum_ready, 1)
                    ln.vector(dve, n, s, r[:, s, :])
                split_x(0, 0)
                dve.wait_ge(b_hi, 1)
                v.tensor_tensor(b[:, LO, :], b_raw[:], b[:, HI, :].bitcast(F32), ALU.subtract).then_inc(b_lo, 1)
                with dve.Fori(0, TILES // 2 - 1) as j:
                    for s in range(2):
                        tile(j * 2 + s, s)
                tile(TILES - 2, 0)
                tile(TILES - 1, 1, more=False)

            @block.tensor
            def _(pe):
                def transposes(s, loads):
                    pe.wait_ge(x_loaded[s], loads * 16)
                    for kt in range(KT):
                        m = nc.tensor.transpose(ps_x[:, kt * P:(kt + 1) * P], xn[:, s, kt * P:(kt + 1) * P], ident[:])
                    m.then_inc(x_turned, 1)

                def product(into, s, at, width, stop=True):
                    for kt in range(KT):
                        for wa, wb in PASSES:
                            m = nc.tensor.matmul(into, xT[:, s, wa, kt * P:(kt + 1) * P], w[:, wb, kt, at:at + width],
                                                 start=(kt == 0 and (wa, wb) == PASSES[0]),
                                                 stop=(stop and kt == KT - 1 and (wa, wb) == PASSES[-1]))
                    return m

                def tile(n, s, loads, more=True):
                    pe.wait_ge(x_lo, n + 1)
                    product(ps_qh[:, 0:N_Q + N_H], s, Q_AT, N_Q + N_H)
                    product(ps_k[:, 0:N_Q], s, K_AT, N_Q).then_inc(qhk_ready, 1)
                    if more:
                        transposes(1 - s, loads)
                    pe.wait_ge(sum_ready, n + 1)
                    product(ps_y[:, s, 0:BANK], s, 0, BANK, stop=False)
                    pe.wait_ge(weigh, n * 4 + 4)
                    nc.tensor.transpose(ps_h, h[:], ident[:]).then_inc(h_turned, 1)
                    product(ps_y[:, s, BANK:D], s, BANK, BANK, stop=False)
                    pe.wait_ge(b_lo, 1)
                    pe.wait_ge(h_lo, n + 1)
                    for half in range(2):
                        for wa, wb in PASSES:
                            m = nc.tensor.matmul(ps_y[:, s, half * BANK:(half + 1) * BANK], hT[:, wa, :],
                                                 b[:, wb, half * BANK:(half + 1) * BANK], start=False,
                                                 stop=(wa, wb) == PASSES[-1])
                    m.then_inc(y_ready, 1)
                transposes(0, 1)
                with pe.Fori(0, TILES // 2 - 1) as j:
                    tile(j * 2, 0, j + 1)
                    tile(j * 2 + 1, 1, j + 2)
                tile(TILES - 2, 0, TILES // 2)
                tile(TILES - 1, 1, None, more=False)


def build(nc, x, x_turned, attn_w, attn_mask, codes, scales, qkv_w, tables, o_w, lora_w, bias, lora_b, out):
    dram = lambda name, *shape: nc.dram_tensor(f"between_{name}", shape, F32, kind="Internal").ap()
    x1, x2, x3 = (dram(f"x{i}", TILES, P, D) for i in (1, 2, 3))
    down_w = dram("down_w", CH, P, D)
    inter = dram("inter", CH, BATCH, P, SEQ)
    qk = dram("qk", 2 * QK_GROUPS, BATCH, 8, 2, 2, HD // 2, SEQ)
    v = dram("v", QK_GROUPS, BATCH, SEQ // P, P, 2 * P)
    heads = dram("heads", QK_GROUPS, TILES, P, 2 * P)
    with ExitStack() as ctx:
        sb = lambda name, dt: ctx.enter_context(nc.sbuf_tensor(name, [P, P], dt))
        ident, above = sb("ident", F32), sb("above", F32)
        ident_b, above_b = sb("ident_b", BF16), sb("above_b", BF16)
        seen = ctx.enter_context(nc.semaphore("seen"))
        make_constants(nc, ident, above, ident_b, above_b)
        with ExitStack() as ffn:
            decoder = Nf4Decoder(nc, ffn, codes, scales, down_w)
            linear_ln(nc, "l0", x_turned, x, x1, seen, weight=attn_w, mask=attn_mask, late=decoder)
            ffn_up(nc, x1, ident, decoder, inter)
        ffn_down(nc, inter, down_w, x1, x2, seen)
        project_qkv(nc, x2, ident, qkv_w, tables, qk, v)
        with ExitStack() as late:
            o_wt = late.enter_context(nc.sbuf_tensor("o_wt", [P, 2, KT, D], F32R))
            with ExitStack() as beside:
                attention(nc, ident, ident_b, above_b,
                          qk.rearrange("(m u) b h c a j t -> m (u b) h c (a j) t", m=2),
                          v.rearrange("u b k p i -> (u b) k p i"),
                          heads.rearrange("u t p i -> (u t) p i"),
                          WeightSplit(nc, beside, "o_wt", o_w, o_wt), seen)
            lora_wt = late.enter_context(nc.sbuf_tensor("lora_wt", [P, 2, KT, lora_w.shape[2]], F32R))
            with ExitStack() as beside:
                linear_ln(nc, "l1", heads.rearrange("u n p i -> n p u i"), x2, x3, seen, w=o_wt,
                          side=WeightSplit(nc, beside, "lora_wt", lora_w, lora_wt))
            ffn_lora(nc, x3, lora_wt, bias, lora_b, ident, out, seen)


def kernel(L0_attn_data, L0_attn_weight, L0_attn_mask, L0_ffn_gate_codes, L0_ffn_gate_scales, L0_ffn_up_codes,
           L0_ffn_up_scales, L0_ffn_down_codes, L0_ffn_down_scales, L1_attn_wq, L1_attn_wk, L1_attn_wv, L1_attn_wo,
           L1_ffn_W, L1_ffn_b, L1_ffn_Wq, L1_ffn_Wk, L1_ffn_A, L1_ffn_Bm):
    import concourse.bacc as bacc
    from concourse.bass_utils import run_bass_kernel_spmd

    x = np.asarray(L0_attn_data)
    pad = CH * P - I_FFN
    arrays = {}

    def put(name, array):
        arrays[name] = np.ascontiguousarray(array)

    put("x", x.reshape(TILES, P, D))
    put("x_turned", x.reshape(TILES, P, KT, P).transpose(0, 3, 2, 1))
    put("attn_w", np.asarray(L0_attn_weight).T.reshape(KT, P, D))
    put("attn_mask", np.asarray(L0_attn_mask).T.reshape(KT, P, D))

    full = I_FFN - (P - pad)

    def up_codes(a):
        return a.reshape(CH, P, KT, P).transpose(0, 3, 2, 1).reshape(CH, P, KT * P)

    def up_scales(a):
        return a.reshape(CH, P, KT, P // NF4_BLOCK).transpose(0, 3, 2, 1)

    gate_codes, up_codes_in = np.asarray(L0_ffn_gate_codes), np.asarray(L0_ffn_up_codes)
    gate_scales, up_scales_in = np.asarray(L0_ffn_gate_scales), np.asarray(L0_ffn_up_scales)
    put("gate_codes", up_codes(np.concatenate([gate_codes, up_codes_in[full:]])))
    put("up_codes", up_codes(np.concatenate([up_codes_in[:full], np.full((P, D), NF4_ZERO, up_codes_in.dtype)])))
    put("gate_scales", up_scales(np.concatenate([gate_scales, up_scales_in[full:]])))
    put("up_scales", up_scales(np.concatenate([up_scales_in[:full],
                                               np.zeros((P, D // NF4_BLOCK), up_scales_in.dtype)])))
    down_codes, down_scales = np.asarray(L0_ffn_down_codes).T, np.asarray(L0_ffn_down_scales).T
    put("down_codes", np.concatenate([down_codes[:full], np.full((pad, D), NF4_ZERO, down_codes.dtype),
                                      down_codes[full:]]).reshape(CH, P, D))
    put("down_scales", np.concatenate([down_scales[:full // NF4_BLOCK],
                                       np.zeros((pad // NF4_BLOCK, D), down_scales.dtype),
                                       down_scales[full // NF4_BLOCK:]]).reshape(CH, P // NF4_BLOCK, D))

    def rotary_weight(a):
        a = np.asarray(a).reshape(KT, P, QK_GROUPS, 8, HD // 2, 2)
        return a.transpose(2, 1, 0, 5, 3, 4).reshape(QK_GROUPS, P, KT * 2 * P)

    v_w = np.asarray(L1_attn_wv).reshape(KT, P, QK_GROUPS, 2 * P).transpose(2, 1, 0, 3).reshape(QK_GROUPS, P, -1)
    put("qkv_w", np.concatenate([rotary_weight(L1_attn_wq), rotary_weight(L1_attn_wk), v_w]))
    frequency = 1.0 / 10000.0 ** (np.arange(0, HD, 2)[:HD // 2].astype(np.float32) / HD)
    angle = np.outer(np.arange(SEQ), frequency).astype(np.float32)
    k_tables = np.stack([np.tile(f(angle).T, (8, 1)) for f in (np.cos, np.sin)])
    put("tables", np.stack([k_tables * (np.float32(1.0) / np.sqrt(np.float32(HD))), k_tables]).astype(np.float32))
    put("o_w", np.asarray(L1_attn_wo).reshape(KT, P, D))

    lora_a = np.asarray(L1_ffn_A).reshape(EXPERTS * RANK, D)
    put("lora_w", np.concatenate([np.asarray(a).T for a in (L1_ffn_W, L1_ffn_Wq, lora_a, L1_ffn_Wk)],
                                 axis=1).reshape(KT, P, -1))
    put("bias", np.asarray(L1_ffn_b).reshape(1, D))
    put("lora_b", np.asarray(L1_ffn_Bm).transpose(0, 2, 1).reshape(EXPERTS * RANK, D))

    nc = bacc.Bacc("TRN2", target_bir_lowering=False, num_devices=1, dynamic_dma_scratch_size=1024)
    ap = {name: nc.dram_tensor(f"in_{name}", a.shape, mybir.dt.from_np(a.dtype), kind="ExternalInput").ap()
          for name, a in arrays.items()}
    out = nc.dram_tensor("out", (TILES, P, D), F32, kind="ExternalOutput").ap()
    build(nc, ap["x"], ap["x_turned"], ap["attn_w"], ap["attn_mask"],
          (ap["gate_codes"], ap["up_codes"], ap["down_codes"]),
          (ap["gate_scales"], ap["up_scales"], ap["down_scales"]),
          ap["qkv_w"], ap["tables"], ap["o_w"], ap["lora_w"], ap["bias"], ap["lora_b"], out)
    result = run_bass_kernel_spmd(nc, [{f"in_{name}": a for name, a in arrays.items()}], core_ids=[0])
    return result.results[0]["out"].reshape(x.shape)
```
